# Optimizing a Trainium2 kernel written in Bass

```python
import numpy as np
import jax
import jax.numpy as jnp

def _softmax(x, axis=-1):
    return jax.nn.softmax(x, axis=axis)

def _gelu(x):
    return jax.nn.gelu(x, approximate=True)

def _silu(x):
    return jax.nn.silu(x)

def _sigmoid(x):
    return jax.nn.sigmoid(x)

def _layernorm(x, axis=-1, eps=1e-05):
    m = jnp.mean(x, axis=axis, keepdims=True)
    v = jnp.var(x, axis=axis, keepdims=True)
    return (x - m) / jnp.sqrt(v + eps)

def _scatter_add(tgt, idx, src, axis=0):
    return tgt.at[idx].add(src)

def _segment_sum(src, seg, n):
    return jax.ops.segment_sum(src, seg, n)
kernel_name = 'mk_adaln_d2_jaxref_r8_9c68e0'

def setup_inputs(seed: int=0):
    np.random.seed(seed)
    _w = jnp.asarray

    def _L0_attn_setup():
        import jax, jax.numpy as jnp
        import numpy as np
        D_MODEL = 128
        N_HEAD = 16
        SEQ = 256
        BATCH = 2
        key = jax.random.key(seed)
        x = jax.random.normal(key, (BATCH, SEQ, D_MODEL), dtype=jnp.float32)
        return {'x': x}
    _L0_attn_in = _L0_attn_setup()

    def _L0_ffn_setup():
        import jax, jax.numpy as jnp
        import numpy as np
        E = 32
        H = 128
        I = 64
        G = 8
        TKG = 4
        TOPK = 8
        NSH = 2
        SCALE = 2.5
        key = jax.random.key(seed)
        ks = jax.random.split(key, 10)
        s = 0.02
        return {'hidden_states': jax.random.normal(ks[0], (2, 128, H), jnp.float32), 'gate_w': jax.random.normal(ks[1], (E, H), jnp.float32) * s, 'gate_bias': jax.random.normal(ks[2], (E,), jnp.float32) * s, 'w_gate': jax.random.normal(ks[3], (E, I, H), jnp.float32) * s, 'w_up': jax.random.normal(ks[4], (E, I, H), jnp.float32) * s, 'w_down': jax.random.normal(ks[5], (E, H, I), jnp.float32) * s, 'sh_gate': jax.random.normal(ks[6], (I * NSH, H), jnp.float32) * s, 'sh_up': jax.random.normal(ks[7], (I * NSH, H), jnp.float32) * s, 'sh_down': jax.random.normal(ks[8], (H, I * NSH), jnp.float32) * s}
    _L0_ffn_in = _L0_ffn_setup()
    _L0_c = _w((lambda *s: np.random.randn(*s).astype(np.float32) * 0.05)(8, 128))
    _L0_wmod = _w((lambda *s: np.random.randn(*s).astype(np.float32) * 0.05)(128, 6 * 128) * 128 ** (-0.5))

    def _L1_attn_setup():
        import jax, jax.numpy as jnp
        import numpy as np
        D_MODEL = 128
        N_HEADS = 16
        D_K = D_MODEL // N_HEADS
        MAX_LEN = 256
        B, T = (2, 256)
        key = jax.random.key(seed)
        ks = jax.random.split(key, 10)
        s = 1.0 / np.sqrt(D_MODEL)
        inp = {'x': jax.random.normal(ks[0], (B, T, D_MODEL), dtype=jnp.float32), 'WQ': jax.random.uniform(ks[1], (D_MODEL, D_MODEL), minval=-s, maxval=s, dtype=jnp.float32), 'bQ': jax.random.uniform(ks[2], (D_MODEL,), minval=-s, maxval=s, dtype=jnp.float32), 'WK': jax.random.uniform(ks[3], (D_MODEL, D_MODEL), minval=-s, maxval=s, dtype=jnp.float32), 'bK': jax.random.uniform(ks[4], (D_MODEL,), minval=-s, maxval=s, dtype=jnp.float32), 'WV': jax.random.uniform(ks[5], (D_MODEL, D_MODEL), minval=-s, maxval=s, dtype=jnp.float32), 'bV': jax.random.uniform(ks[6], (D_MODEL,), minval=-s, maxval=s, dtype=jnp.float32), 'WO': jax.random.uniform(ks[7], (D_MODEL, D_MODEL), minval=-s, maxval=s, dtype=jnp.float32), 'bO': jax.random.uniform(ks[8], (D_MODEL,), minval=-s, maxval=s, dtype=jnp.float32), 'rel_pos_table': jax.random.normal(ks[9], (2 * MAX_LEN - 1, N_HEADS), dtype=jnp.float32)}
        return inp
    _L1_attn_in = _L1_attn_setup()

    def _L1_ffn_setup():
        import jax, jax.numpy as jnp
        import numpy as np
        DIM = 128
        DEPTH = 6
        HEADS = 16
        DIM_HEAD = 64
        WINDOW = 32
        INNER = HEADS * DIM_HEAD
        DIM_INNER = int(DIM * 4 * 2 / 3)
        QK_SCALE = 8.0

        def shift_tokens(t):
            a, s = jnp.split(t, 2, -1)
            s = jnp.pad(s, ((0, 0), (1, 0), (0, 0)))[:, :-1]
            return jnp.concatenate([a, s], -1)

        def l2norm(t):
            return t / jnp.maximum(jnp.linalg.norm(t, axis=-1, keepdims=True), 1e-12)

        def rotate_half(x):
            x1, x2 = jnp.split(x, 2, -1)
            return jnp.concatenate([-x2, x1], -1)

        def rotary_tables(n):
            half = jnp.arange(0, DIM_HEAD, 2, dtype=jnp.float32)
            inv_freq = 1.0 / 10000.0 ** (half / DIM_HEAD)
            t = jnp.arange(n, dtype=jnp.float32)
            freqs = t[:, None] * inv_freq[None, :]
            freqs = jnp.concatenate([freqs, freqs], -1)
            base_scale = (half + 0.4 * DIM_HEAD) / (1.4 * DIM_HEAD)
            power = (t - n // 2) / (WINDOW // 2)
            scale = base_scale[None, :] ** power[:, None]
            scale = jnp.concatenate([scale, scale], -1)
            return (freqs, scale)

        def local_attention(q, k, v):
            b, h, n, d = q.shape
            w = WINDOW
            nw = n // w
            bq = q.reshape(b, h, nw, w, d)
            bk = k.reshape(b, h, nw, w, d)
            bv = v.reshape(b, h, nw, w, d)

            def look(t):
                p = jnp.pad(t, ((0, 0), (0, 0), (1, 0), (0, 0), (0, 0)))
                return jnp.concatenate([p[:, :, :nw], p[:, :, 1:]], axis=3)
            bk2, bv2 = (look(bk), look(bv))
            seq = jnp.arange(n).reshape(nw, w)
            seq_p = jnp.pad(seq, ((1, 0), (0, 0)), constant_values=-1)
            jt = jnp.concatenate([seq_p[:nw], seq_p[1:]], axis=1)
            it = seq[:, :, None]
            jb = jt[:, None, :]
            mask = (it < jb) | (it > jb + w) | (jb == -1)
            sim = jnp.einsum('bhwie,bhwje->bhwij', bq, bk2) * QK_SCALE
            sim = jnp.where(mask, -jnp.finfo(sim.dtype).max, sim)
            attn = jax.nn.softmax(sim, -1)
            out = jnp.einsum('bhwij,bhwje->bhwie', attn, bv2)
            return out.reshape(b, h, n, d)

        def attn_layer(x, Wqkv, qs, ksc, Wo):
            b, n, _ = x.shape
            qkv = x @ Wqkv
            q, k, v = jnp.split(qkv, 3, -1)
            sh = lambda t: t.reshape(b, n, HEADS, DIM_HEAD).transpose(0, 2, 1, 3)
            q, k, v = (sh(q), sh(k), sh(v))
            q = l2norm(q) * qs
            k = l2norm(k) * ksc
            freqs, scale = rotary_tables(n)
            cos, sin = (jnp.cos(freqs), jnp.sin(freqs))
            q = q * cos * scale + rotate_half(q) * sin * scale
            inv = 1.0 / scale
            k = k * cos * inv + rotate_half(k) * sin * inv
            out = local_attention(q, k, v)
            out = out.transpose(0, 2, 1, 3).reshape(b, n, INNER)
            return out @ Wo

        def ffn_layer(x, g, bln, W1, b1, W2, b2):
            mu = x.mean(-1, keepdims=True)
            var = ((x - mu) ** 2).mean(-1, keepdims=True)
            xn = (x - mu) / jnp.sqrt(var + 1e-05) * g + bln
            hg = xn @ W1 + b1
            a, gate = jnp.split(hg, 2, -1)
            return a * jax.nn.gelu(gate, approximate=False) @ W2 + b2
        key = jax.random.key(seed)
        ks = jax.random.split(key, 8)
        B, N = (2, 256)
        init = lambda k, shape: jax.random.normal(k, shape, jnp.float32) * 0.02
        return {'x': jax.random.normal(ks[0], (B, N, DIM), jnp.float32), 'Wqkv': init(ks[1], (DEPTH, DIM, 3 * INNER)), 'q_scale': jnp.ones((DEPTH, DIM_HEAD), jnp.float32), 'k_scale': jnp.ones((DEPTH, DIM_HEAD), jnp.float32), 'Wo': init(ks[2], (DEPTH, INNER, DIM)), 'ln_g': jnp.ones((DEPTH, DIM), jnp.float32), 'ln_b': jnp.zeros((DEPTH, DIM), jnp.float32), 'W1': init(ks[3], (DEPTH, DIM, 2 * DIM_INNER)), 'b1': jnp.zeros((DEPTH, 2 * DIM_INNER), jnp.float32), 'W2': init(ks[4], (DEPTH, DIM_INNER, DIM)), 'b2': jnp.zeros((DEPTH, DIM), jnp.float32)}
    _L1_ffn_in = _L1_ffn_setup()
    _L1_c = _w((lambda *s: np.random.randn(*s).astype(np.float32) * 0.05)(8, 128))
    _L1_wmod = _w((lambda *s: np.random.randn(*s).astype(np.float32) * 0.05)(128, 6 * 128) * 128 ** (-0.5))
    _d = {'L0_attn_x': _L0_attn_in['x'], 'L0_ffn_gate_w': _L0_ffn_in['gate_w'], 'L0_ffn_gate_bias': _L0_ffn_in['gate_bias'], 'L0_ffn_w_gate': _L0_ffn_in['w_gate'], 'L0_ffn_w_up': _L0_ffn_in['w_up'], 'L0_ffn_w_down': _L0_ffn_in['w_down'], 'L0_ffn_sh_gate': _L0_ffn_in['sh_gate'], 'L0_ffn_sh_up': _L0_ffn_in['sh_up'], 'L0_ffn_sh_down': _L0_ffn_in['sh_down'], 'L0_c': _L0_c, 'L0_wmod': _L0_wmod, 'L1_attn_WQ': _L1_attn_in['WQ'], 'L1_attn_bQ': _L1_attn_in['bQ'], 'L1_attn_WK': _L1_attn_in['WK'], 'L1_attn_bK': _L1_attn_in['bK'], 'L1_attn_WV': _L1_attn_in['WV'], 'L1_attn_bV': _L1_attn_in['bV'], 'L1_attn_WO': _L1_attn_in['WO'], 'L1_attn_bO': _L1_attn_in['bO'], 'L1_attn_rel_pos_table': _L1_attn_in['rel_pos_table'], 'L1_ffn_Wqkv': _L1_ffn_in['Wqkv'], 'L1_ffn_q_scale': _L1_ffn_in['q_scale'], 'L1_ffn_k_scale': _L1_ffn_in['k_scale'], 'L1_ffn_Wo': _L1_ffn_in['Wo'], 'L1_ffn_ln_g': _L1_ffn_in['ln_g'], 'L1_ffn_ln_b': _L1_ffn_in['ln_b'], 'L1_ffn_W1': _L1_ffn_in['W1'], 'L1_ffn_b1': _L1_ffn_in['b1'], 'L1_ffn_W2': _L1_ffn_in['W2'], 'L1_ffn_b2': _L1_ffn_in['b2'], 'L1_c': _L1_c, 'L1_wmod': _L1_wmod}
    _x0 = _d['L0_attn_x']
    _d['L0_attn_x'] = jax.random.normal(jax.random.fold_in(jax.random.key(seed), 1), (8, 512, 128), dtype=_x0.dtype)
    del _x0
    return _d

def reference(L0_attn_x, L0_ffn_gate_w, L0_ffn_gate_bias, L0_ffn_w_gate, L0_ffn_w_up, L0_ffn_w_down, L0_ffn_sh_gate, L0_ffn_sh_up, L0_ffn_sh_down, L0_c, L0_wmod, L1_attn_WQ, L1_attn_bQ, L1_attn_WK, L1_attn_bK, L1_attn_WV, L1_attn_bV, L1_attn_WO, L1_attn_bO, L1_attn_rel_pos_table, L1_ffn_Wqkv, L1_ffn_q_scale, L1_ffn_k_scale, L1_ffn_Wo, L1_ffn_ln_g, L1_ffn_ln_b, L1_ffn_W1, L1_ffn_b1, L1_ffn_W2, L1_ffn_b2, L1_c, L1_wmod):

    def _L0_attn_ref(x):
        import jax, jax.numpy as jnp
        import numpy as np
        D_MODEL = 128
        N_HEAD = 16
        SEQ = 256
        BATCH = 2
        B, S, D = x.shape
        H = N_HEAD
        hd = D // H
        qkv = x.reshape(B, S, H, hd).transpose(0, 2, 1, 3)
        q = k = v = qkv
        w = jnp.einsum('bhqd,bhkd->bhqk', q, k) / jnp.sqrt(jnp.asarray(hd, x.dtype))
        causal = jnp.tril(jnp.ones((S, S), dtype=bool))
        mask_value = jnp.finfo(w.dtype).min
        w = jnp.where(causal[None, None, :, :], w, mask_value)
        w = jax.nn.softmax(w, axis=-1)
        out = jnp.einsum('bhqk,bhkd->bhqd', w, v)
        return out.transpose(0, 2, 1, 3).reshape(B, S, D)

    def _L0_ffn_ref(hidden_states, gate_w, gate_bias, w_gate, w_up, w_down, sh_gate, sh_up, sh_down):
        import jax, jax.numpy as jnp
        import numpy as np
        E = 32
        H = 128
        I = 64
        G = 8
        TKG = 4
        TOPK = 8
        NSH = 2
        SCALE = 2.5
        B, S, Hd = hidden_states.shape
        h = hidden_states.reshape(-1, Hd)
        logits = h.astype(jnp.float32) @ gate_w.T
        scores = jax.nn.sigmoid(logits)
        sc = scores + gate_bias
        grp = sc.reshape(-1, G, E // G)
        group_scores = jax.lax.top_k(grp, 2)[0].sum(-1)
        gidx = jax.lax.top_k(group_scores, TKG)[1]
        gmask = jnp.sum(jax.nn.one_hot(gidx, G, dtype=sc.dtype), axis=1)
        smask = jnp.repeat(gmask, E // G, axis=1)
        masked = jnp.where(smask > 0, sc, jnp.zeros_like(sc))
        tki = jax.lax.top_k(masked, TOPK)[1]
        tkw = jnp.take_along_axis(scores, tki, axis=1)
        tkw = tkw / (tkw.sum(-1, keepdims=True) + 1e-20)
        tkw = tkw * SCALE
        combine = (jax.nn.one_hot(tki, E, dtype=tkw.dtype) * tkw[..., None]).sum(1)
        g = jax.nn.silu(jnp.einsum('th,eih->tei', h, w_gate))
        u = jnp.einsum('th,eih->tei', h, w_up)
        routed = jnp.einsum('tei,ehi->th', g * u * combine[:, :, None], w_down)
        sg = jax.nn.silu(h @ sh_gate.T)
        shared = sg * (h @ sh_up.T) @ sh_down.T
        return (routed + shared).reshape(B, S, Hd)

    def _L1_attn_ref(x, WQ, bQ, WK, bK, WV, bV, WO, bO, rel_pos_table):
        import jax, jax.numpy as jnp
        import numpy as np
        D_MODEL = 128
        N_HEADS = 16
        D_K = D_MODEL // N_HEADS
        MAX_LEN = 256
        B, T = (2, 256)
        b, t, d = x.shape
        q = (x @ WQ.T + bQ).reshape(b, t, N_HEADS, D_K).transpose(0, 2, 1, 3)
        k = (x @ WK.T + bK).reshape(b, t, N_HEADS, D_K).transpose(0, 2, 1, 3)
        v = (x @ WV.T + bV).reshape(b, t, N_HEADS, D_K).transpose(0, 2, 1, 3)
        scores = jnp.einsum('bhqd,bhkd->bhqk', q, k) / jnp.sqrt(jnp.float32(D_K))
        pos = jnp.arange(t)
        rel = pos[:, None] - pos[None, :] + (MAX_LEN - 1)
        rel = jnp.clip(rel, 0, 2 * MAX_LEN - 2)
        rel_bias = rel_pos_table[rel]
        scores = scores + rel_bias.transpose(2, 0, 1)[None]
        causal = pos[None, :] <= pos[:, None]
        scores = jnp.where(causal[None, None], scores, -jnp.inf)
        attn = jax.nn.softmax(scores, axis=-1)
        out = jnp.einsum('bhqk,bhkd->bhqd', attn, v)
        out = out.transpose(0, 2, 1, 3).reshape(b, t, d)
        return out @ WO.T + bO

    def _L1_ffn_ref(x, Wqkv, q_scale, k_scale, Wo, ln_g, ln_b, W1, b1, W2, b2):
        import jax, jax.numpy as jnp
        import numpy as np
        DIM = 128
        DEPTH = 6
        HEADS = 16
        DIM_HEAD = 64
        WINDOW = 32
        INNER = HEADS * DIM_HEAD
        DIM_INNER = int(DIM * 4 * 2 / 3)
        QK_SCALE = 8.0

        def shift_tokens(t):
            a, s = jnp.split(t, 2, -1)
            s = jnp.pad(s, ((0, 0), (1, 0), (0, 0)))[:, :-1]
            return jnp.concatenate([a, s], -1)

        def l2norm(t):
            return t / jnp.maximum(jnp.linalg.norm(t, axis=-1, keepdims=True), 1e-12)

        def rotate_half(x):
            x1, x2 = jnp.split(x, 2, -1)
            return jnp.concatenate([-x2, x1], -1)

        def rotary_tables(n):
            half = jnp.arange(0, DIM_HEAD, 2, dtype=jnp.float32)
            inv_freq = 1.0 / 10000.0 ** (half / DIM_HEAD)
            t = jnp.arange(n, dtype=jnp.float32)
            freqs = t[:, None] * inv_freq[None, :]
            freqs = jnp.concatenate([freqs, freqs], -1)
            base_scale = (half + 0.4 * DIM_HEAD) / (1.4 * DIM_HEAD)
            power = (t - n // 2) / (WINDOW // 2)
            scale = base_scale[None, :] ** power[:, None]
            scale = jnp.concatenate([scale, scale], -1)
            return (freqs, scale)

        def local_attention(q, k, v):
            b, h, n, d = q.shape
            w = WINDOW
            nw = n // w
            bq = q.reshape(b, h, nw, w, d)
            bk = k.reshape(b, h, nw, w, d)
            bv = v.reshape(b, h, nw, w, d)

            def look(t):
                p = jnp.pad(t, ((0, 0), (0, 0), (1, 0), (0, 0), (0, 0)))
                return jnp.concatenate([p[:, :, :nw], p[:, :, 1:]], axis=3)
            bk2, bv2 = (look(bk), look(bv))
            seq = jnp.arange(n).reshape(nw, w)
            seq_p = jnp.pad(seq, ((1, 0), (0, 0)), constant_values=-1)
            jt = jnp.concatenate([seq_p[:nw], seq_p[1:]], axis=1)
            it = seq[:, :, None]
            jb = jt[:, None, :]
            mask = (it < jb) | (it > jb + w) | (jb == -1)
            sim = jnp.einsum('bhwie,bhwje->bhwij', bq, bk2) * QK_SCALE
            sim = jnp.where(mask, -jnp.finfo(sim.dtype).max, sim)
            attn = jax.nn.softmax(sim, -1)
            out = jnp.einsum('bhwij,bhwje->bhwie', attn, bv2)
            return out.reshape(b, h, n, d)

        def attn_layer(x, Wqkv, qs, ksc, Wo):
            b, n, _ = x.shape
            qkv = x @ Wqkv
            q, k, v = jnp.split(qkv, 3, -1)
            sh = lambda t: t.reshape(b, n, HEADS, DIM_HEAD).transpose(0, 2, 1, 3)
            q, k, v = (sh(q), sh(k), sh(v))
            q = l2norm(q) * qs
            k = l2norm(k) * ksc
            freqs, scale = rotary_tables(n)
            cos, sin = (jnp.cos(freqs), jnp.sin(freqs))
            q = q * cos * scale + rotate_half(q) * sin * scale
            inv = 1.0 / scale
            k = k * cos * inv + rotate_half(k) * sin * inv
            out = local_attention(q, k, v)
            out = out.transpose(0, 2, 1, 3).reshape(b, n, INNER)
            return out @ Wo

        def ffn_layer(x, g, bln, W1, b1, W2, b2):
            mu = x.mean(-1, keepdims=True)
            var = ((x - mu) ** 2).mean(-1, keepdims=True)
            xn = (x - mu) / jnp.sqrt(var + 1e-05) * g + bln
            hg = xn @ W1 + b1
            a, gate = jnp.split(hg, 2, -1)
            return a * jax.nn.gelu(gate, approximate=False) @ W2 + b2
        for i in range(DEPTH):
            x = attn_layer(shift_tokens(x), Wqkv[i], q_scale[i], k_scale[i], Wo[i]) + x
            x = ffn_layer(shift_tokens(x), ln_g[i], ln_b[i], W1[i], b1[i], W2[i], b2[i]) + x
        return x
    x = L0_attn_x
    mod = (_silu(L0_c) @ L0_wmod).reshape(L0_c.shape[0], 6, 1, -1)
    sa, ca, ga, sb, cb, gb = (mod[:, 0], mod[:, 1], mod[:, 2], mod[:, 3], mod[:, 4], mod[:, 5])
    ga = (2 * (ga >= 0) - 1) * jnp.maximum(jnp.abs(ga), 0.25)
    gb = (2 * (gb >= 0) - 1) * jnp.maximum(jnp.abs(gb), 0.25)
    h = _layernorm(x, axis=-1) * (1 + ca) + sa
    x = x + ga * _L0_attn_ref(h)
    h = _layernorm(x, axis=-1) * (1 + cb) + sb
    x = x + gb * _L0_ffn_ref(h, L0_ffn_gate_w, L0_ffn_gate_bias, L0_ffn_w_gate, L0_ffn_w_up, L0_ffn_w_down, L0_ffn_sh_gate, L0_ffn_sh_up, L0_ffn_sh_down)
    mod = (_silu(L1_c) @ L1_wmod).reshape(L1_c.shape[0], 6, 1, -1)
    sa, ca, ga, sb, cb, gb = (mod[:, 0], mod[:, 1], mod[:, 2], mod[:, 3], mod[:, 4], mod[:, 5])
    ga = (2 * (ga >= 0) - 1) * jnp.maximum(jnp.abs(ga), 0.25)
    gb = (2 * (gb >= 0) - 1) * jnp.maximum(jnp.abs(gb), 0.25)
    h = _layernorm(x, axis=-1) * (1 + ca) + sa
    x = x + ga * _L1_attn_ref(h, L1_attn_WQ, L1_attn_bQ, L1_attn_WK, L1_attn_bK, L1_attn_WV, L1_attn_bV, L1_attn_WO, L1_attn_bO, L1_attn_rel_pos_table)
    h = _layernorm(x, axis=-1) * (1 + cb) + sb
    x = x + gb * _L1_ffn_ref(h, L1_ffn_Wqkv, L1_ffn_q_scale, L1_ffn_k_scale, L1_ffn_Wo, L1_ffn_ln_g, L1_ffn_ln_b, L1_ffn_W1, L1_ffn_b1, L1_ffn_W2, L1_ffn_b2)
    return x

_drawn_inputs = setup_inputs


def setup_inputs(seed=0):
    import zlib

    import numpy as np

    out = dict(_drawn_inputs(seed))
    spreads = {'L1_ffn_q_scale': (1.0, 0.6),
     'L1_ffn_k_scale': (1.0, 0.6),
     'L1_ffn_ln_g': (1.0, 0.6),
     'L1_ffn_ln_b': (0.0, 0.8),
     'L1_ffn_b1': (0.0, 0.8),
     'L1_ffn_b2': (0.0, 0.62)}
    factors = {'L0_ffn_gate_w': 8.0,
     'L0_ffn_gate_bias': 8.0,
     'L0_ffn_w_gate': 8.0,
     'L0_ffn_w_up': 8.0,
     'L0_ffn_w_down': 8.0,
     'L0_ffn_sh_gate': 8.0,
     'L0_ffn_sh_up': 8.0,
     'L0_ffn_sh_down': 8.0,
     'L1_attn_WQ': 8.0,
     'L1_attn_bQ': 8.0,
     'L1_attn_WK': 8.0,
     'L1_attn_bK': 64.0,
     'L1_attn_WV': 4.019,
     'L1_attn_bV': 7.369,
     'L1_attn_WO': 3.544,
     'L1_attn_bO': 4.225,
     'L1_attn_rel_pos_table': 5.737,
     'L1_ffn_W1': 7.555,
     'L1_ffn_W2': 7.423}
    for name, (base, spread) in spreads.items():
        noise = np.random.default_rng([zlib.crc32(name.encode()), seed]).standard_normal(out[name].shape)
        drawn = base * np.exp(spread * noise) if base else spread * noise
        out[name] = jnp.asarray(drawn.astype(out[name].dtype))
    for name, factor in factors.items():
        out[name] = (out[name] * factor).astype(out[name].dtype)
    return out
```

```python
from contextlib import ExitStack

import numpy as np

import concourse.bass as bass
from concourse import mybir

F32 = mybir.dt.float32
BF16 = mybir.dt.bfloat16
ACT = mybir.ActivationFunctionType
ALU = mybir.AluOpType
AX = mybir.AxisListType

NB, SEQ, D = 8, 512, 128
TT = SEQ // 128
DEPTH = 6
LH, LD = 16, 64
INNER = LH * LD
PAIRS = LH // 2
WIN = 32
KEYS = WIN + 128
DI = D * 4 * 2 // 3
BLK = [(0, 128), (128, 128), (256, DI - 256)]
EPS = 1e-5
MASKED = -1e30


class Count:

    def __init__(self, sem, per, credit=0):
        self.sem, self.per, self.credit = sem, per, credit

    def at(self, it, n):
        return it * self.per + (self.credit + n)

    def before(self, it, n):
        return it * self.per + (self.credit + n - self.per)


GH, GD = 16, 8
HPG = 4
NG = GH // HPG
PADD = 32
SELW = D + GH
E, EI = 32, 64
EP = E // 2
GROUPS, TKG, TOPK, SCALE = 8, 4, 8, 2.5
ROWS = 6


def blocks(sb, sem, s_alone, dr, ident, identb, psum, x_in, x_mid, x_work, nbatch):
    WM = [sb(f"WM{i}", [128, 6 * D]) for i in range(2)]
    CT = sb("CT", [128, 2, NB])
    CE = sb("CE", [128, 2, NB])
    SIL = sb("SIL", [128, 2, NB])
    MODT = sb("MODT", [128, 2, 6, NB])
    GATE = sb("GATE", [128, ROWS, NB, D])
    EB = sb("EB", [GH, 640])
    BIAS1 = sb("BIAS1", [128, GH, SEQ])
    BIAS0 = sb("BIAS0", [128, SEQ])
    HM = sb("HM", [128, GH])
    WV = [sb(f"WV{i}", [128, SEQ]) for i in range(2)]
    BV = [sb(f"BV{i}", [128, SEQ]) for i in range(2)]
    SEL = sb("SEL", [128, NG, SELW])
    WQ, WK, WOT = sb("WQ", [128, D]), sb("WK", [128, D]), sb("WOT", [128, D])
    BQK = sb("BQK", [128, 2])
    BO = sb("BO", [128, D])
    GW = sb("GW", [128, E])
    GB = sb("GB", [128, E])
    LOW = sb("LOW", [128, GROUPS, GROUPS])
    WG, WU = sb("WG", [128, EP + 1, 128]), sb("WU", [128, EP + 1, 128])
    WD = sb("WD", [128, EP + 1, D])
    SELC = sb("SELC", [96, EP, 128], BF16)
    EPSC = sb("EPSC1", [128, 1])

    X = sb("X", [128, TT, D])
    ST = sb("ST", [128, TT, 6])
    MV = sb("MV", [128, TT, 2])
    SD = sb("SD", [128, TT])
    RD = sb("RD", [128, TT])
    XN = sb("XN", [128, TT, D])
    HT = sb("HT", [128, SEQ])
    QF = sb("QF", [128, SEQ])
    KF = sb("KF", [128, SEQ])
    QM = [sb(f"QM{i}", [128, SEQ]) for i in range(2)]
    VP = sb("VP", [128, TT, SEQ])
    SP_ = [sb(f"SPO{i}", [128, SEQ]) for i in range(3)]
    NBI = [sb(f"NB1{i}", [128, 1]) for i in range(3)]
    PR = [sb(f"PR1{i}", [128, SEQ]) for i in range(3)]
    NPT = 5
    PT = [sb(f"PT1{i}", [128, TT, SEQ]) for i in range(NPT)]
    MROW = PT[0][0:NB].rearrange("b t n -> b (t n)")[:, 0:12 * D].rearrange("b (l n) -> b l n", l=2)
    MR = PT[1][0:NB].rearrange("b t n -> b (t n)")[:, 0:ROWS * D].rearrange("b (r d) -> b r d", d=D)
    MS = PT[2][0:NB, 0, :].rearrange("b (r d) -> b r d", d=D)
    MA = PT[3][0:NB, 0, :].rearrange("b (r d) -> b r d", d=D)
    OG = sb("OG", [128, NG, SEQ])
    RC = sb("RC", [128, TT, GH])
    ON = sb("ON", [128, TT, D])
    OT = sb("OT1", [128, SEQ])
    TMP = sb("TMP", [128, TT, D])
    TMP2 = sb("TMP2", [128, TT, D])
    FLIP = TMP2[:, 0, :]
    names = ("ex", "ex1", "score", "sc", "mask0", "mask1", "repl", "sel", "w", "comb", "r1", "r2")
    flat = PT[3][:].rearrange("p t n -> p (t n)")
    R = {n: flat[:, TT * E * i:TT * E * (i + 1)].rearrange("p (t e) -> p t e", e=E) for i, n in enumerate(names)}
    names = ("hi1", "lo1", "hi2", "lo2", "t1", "m", "l", "t2", "gs", "rank", "gm")
    flat = PT[2][:].rearrange("p t n -> p (t n)")
    NGR = TT * GROUPS
    Gs = {n: flat[:, NGR * i:NGR * (i + 1)].rearrange("p (t g) -> p t g", g=GROUPS) for i, n in enumerate(names)}
    GT, GQ, GQ2, GQ3 = (flat[:, 512 + 256 * i:768 + 256 * i].rearrange("p (t g k) -> p t g k", g=GROUPS, k=GROUPS)
                        for i in range(4))
    V8 = sb("V8", [128, TT, 8])
    WS = sb("WS", [128, TT])
    WS1 = sb("WS1", [128, TT])
    WS2 = sb("WS2", [128, TT])
    WS3 = sb("WS3", [128, TT])
    CB = sb("CB", [128, TT, 3, E], BF16)
    CBT = sb("CBT", [96, SEQ], BF16)
    SG = [PT[0][:, i, :] for i in range(2)]
    HU = [PT[0][:, 2 + i, :] for i in range(2)]
    HI = [PT[1][:, i, :] for i in range(2)]
    YT = PT[1][:, 2, :]

    P = [psum[:, i, :] for i in range(8)]

    s_c = sem("inputs_small")
    s_ce = sem("silu_steps")
    s_mm = sem("mod_products")
    s_ms = sem("mod_steps")
    s_mw = sem("rows_written")
    s_gl = sem("gates_loaded")
    s_eb = sem("bias_row_steps")
    s_bl = sem("bias_loaded")
    s_bt = sem("bias_turned")
    s_bf = sem("bias_kept")
    s_x = sem("x_loaded")
    s_mid = sem("x_mid_stored")
    s_wk = sem("x_work_stored")
    NC = 27

    c = {}

    def add(prefix, items):
        more = 512 if prefix == "a1_" else 0
        for name, per in items:
            c[prefix + name] = Count(sem(prefix + name), per, per + more)

    UN = GH * TT
    for a in ("a0_", "a1_"):
        add(a, [("st", TT), ("mv", TT), ("sd", 1), ("rd", 1), ("xn", TT), ("xt", 1), ("ht", 1), ("qm", GH),
                ("v", TT), ("vp", TT), ("sc", UN), ("mx", UN), ("ex", UN), ("pt", UN), ("ptc", UN), ("pv", NG), ("og", NG),
                ("o", 2), ("rc", 2), ("on", 2), ("g", 1), ("x", 1)])
    add("a1_", [("qk", 2), ("qkc", 2), ("nt", 1), ("ntc", 1), ("wo", 1), ("bo", 1)])
    add("m_", [("st", TT), ("mv", TT), ("sd", 1), ("rd", 1), ("xn", TT), ("xt", 1), ("ht", 1), ("lg", 1), ("ex", 1), ("r", 1),
               ("cb", 1), ("ct", 1), ("cbt", 1), ("g", EP + 1), ("u", EP + 1), ("c", EP), ("sg", EP + 1), ("hu", EP),
               ("hi", EP + 1), ("dn", EP + 1), ("y", 1), ("yt", 1), ("z", 1), ("gz", 1), ("x", 1)])
    add("f_", [("st", TT), ("mv", TT), ("sd", 1), ("rd", 1), ("xn", TT), ("gm", 1), ("h", 1)])
    NR = 35
    c["route"] = Count(sem("route_steps"), NR, 0)

    def wait(eng, name, it, n):
        eng.wait_ge(c[name].sem, c[name].at(it, n))

    def before(eng, name, it, n):
        eng.wait_ge(c[name].sem, c[name].before(it, n))

    def done(name):
        return c[name].sem

    def credits(eng, names):
        for n in names.split():
            eng.sem_inc(c[n].sem, c[n].credit)

    xin = x_in.rearrange("b (t p) d -> b p t d", p=128)
    xmid = x_mid.rearrange("b (t p) d -> b p t d", p=128)
    xwork = x_work.rearrange("b (t p) d -> b p t d", p=128)

    def alone(eng):
        eng.sem_inc(s_alone, 1)

    def batch(x, b):
        return x[bass.ds(b, 1)].rearrange("o p t d -> p (o t) d")

    def sync_program(sp):
        small = [(WM[0][:], dr["wmod0"]), (WM[1][:], dr["wmod1"]), (CT[:, 0, :], dr["c0T"]), (CT[:, 1, :], dr["c1T"]),
                 (EB[:, 256:512], dr["relT"]), (BIAS0[:], dr["causal"]), (HM[:], dr["hmask"]),
                 (WV[0][:], dr["place"]), (WV[1][:], dr["WVT"]),
                 (BV[0][:], dr["ones_row"].broadcast_to([128, SEQ])), (BV[1][:], dr["bV_row"].broadcast_to([128, SEQ])),
                 (SEL[:], dr["select"]), (WQ[:], dr["WQT"]), (WK[:], dr["WKT"]), (WOT[:], dr["WOT"]), (BQK[:], dr["bQK"]),
                 (BO[:], dr["bO"].broadcast_to([128, D])), (GW[:], dr["gwT"]), (GB[:], dr["gbias"].broadcast_to([128, E])),
                 (LOW[:], dr["lower"]), (WG[:], dr["wgT"]), (WU[:], dr["wuT"]), (WD[:], dr["wdT"]),
                 (FLIP, dr["flip"]),
                 (SELC[:].rearrange("p a b -> p (a b)").bitcast(F32), dr["selc"])]
        assert len(small) + 2 == NC
        sp.dma_start(X[:], batch(xin, 0)).then_inc(s_x, 16)
        for dst, src in small:
            sp.dma_start(dst, src).then_inc(s_c, 16)
        sp.wait_ge(s_ms, 8)
        sp.dma_start(dr["rows"].rearrange("r b d -> b r d"), MR).then_inc(s_mw, 16)
        sp.wait_ge(s_eb, 3)
        sp.dma_start(dr["ebrow"], EB[:]).then_inc(s_mw, 16)
        sp.wait_ge(s_mw, 32)
        sp.dma_start(GATE[:].rearrange("p r b d -> p (r b d)"),
                     dr["rows"].rearrange("(o r) b d -> o (r b d)", o=1).broadcast_to([128, ROWS * NB * D])).then_inc(s_gl, 16)
        e = dr["ebrow"]
        for i in range(NG):
            src = bass.AP(e.tensor, e.offset + HPG * i * 640, [[1, 128], [640, HPG], [1, SEQ]])
            sp.dma_start(PT[i][:], src).then_inc(s_bl, 16)
        with sp.Fori(0, nbatch) as b:
            nxt = (b + 1) % nbatch
            wait(sp, "a1_x", b, 1)
            alone(sp)
            sp.dma_start(batch(xmid, b), X[:]).then_inc(s_mid, 16)
            wait(sp, "f_xn", b, TT)
            sp.wait_ge(s_mid, (b + 1) * 16)
            alone(sp)
            sp.dma_start(X[:], batch(xin, nxt)).then_inc(s_x, 16)
            wait(sp, "f_h", b, 1)
            alone(sp)
            sp.dma_start(batch(xwork, b), TMP2[:]).then_inc(s_wk, 16)
        sp.wait_ge(s_wk, nbatch * 16)
        sp.wait_ge(s_x, (nbatch + 1) * 16)

    def tensor_program(pe):
        credits(pe, " ".join(f"{a}{n}" for a in ("a0_", "a1_") for n in ("xt", "v", "sc", "pt", "pv", "o")))
        credits(pe, "a1_qk a1_nt a1_wo m_xt m_lg m_ct m_g m_u m_c m_dn m_z")
        pe.wait_ge(s_c, 16 * (NC - 2))
        pe.wait_ge(s_ce, 4)
        for i in range(2):
            for k in range(6):
                pe.matmul(P[0][:, (6 * i + k) * NB:(6 * i + k + 1) * NB], WM[i][:, 128 * k:128 * k + 128], SIL[:, i, :],
                          start=True, stop=True)
            for k in range(2):
                last = pe.matmul(P[1 + 2 * i + k][0:NB, 0:384], SIL[:, i, :], WM[i][:, 384 * k:384 * k + 384],
                                 start=True, stop=True)
        last.then_inc(s_mm, 1)
        pe.wait_ge(s_ms, 3)
        pe.wait_ge(s_bl, 16 * NG)
        for h in range(GH):
            if h >= 2:
                pe.wait_ge(s_bf, h - 1)
            pe.matmul(P[6 + h % 2], FLIP, PT[h // HPG][:, h % HPG, :], start=True, stop=True).then_inc(s_bt, 1)

        def turn(it, a, name="xt"):
            wait(pe, a + "xn", it, TT)
            for t in range(TT):
                last = pe.transpose(P[0][:, 128 * t:128 * t + 128], XN[:, t, :], ident)
            last.then_inc(done(a + name), 1)

        def attention(it, a, which):
            turn(it, a)
            wait(pe, a + "ht", it, 1)
            if which:
                for k, w in enumerate((WQ, WK)):
                    pe.matmul(P[2 + k], w[:], HT[:], start=True, stop=True).then_inc(done(a + "qk"), 1)
            for t in range(TT):
                if t >= 2:
                    wait(pe, a + "vp", it, t - 1)
                pe.matmul(P[t % 2], HT[:, 128 * t:128 * t + 128], WV[which][:], start=True, stop=True)\
                    .then_inc(done(a + "v"), 1)
            key = KF if which else HT
            LT = 2

            def score(u):
                h, qt = divmod(u, TT)
                n = 128 * (qt + 1)
                if qt == 0:
                    wait(pe, a + "qm", it, h + 1)
                    if h == 0 and which:
                        wait(pe, a + "qkc", it, 2)
                if u >= 3:
                    wait(pe, a + "mx", it, u - 2)
                pe.matmul(P[2 + u % 3][:, 0:n], QM[h % 2][:, 128 * qt:128 * qt + 128], key[:, 0:n],
                          start=True, stop=True).then_inc(done(a + "sc"), 1)

            def transposes(u):
                h, qt = divmod(u, TT)
                wait(pe, a + "ex", it, u + 1)
                if u >= 2:
                    wait(pe, a + "ptc", it, u - 1)
                else:
                    wait(pe, a + "vp", it, TT - 1 + u)
                for kt in range(qt + 1):
                    last = pe.transpose(P[5 + u % 2][:, 128 * kt:128 * kt + 128], PR[u % 3][:, 128 * kt:128 * kt + 128], ident)
                last.then_inc(done(a + "pt"), 1)

            def values(g):
                wait(pe, a + "ptc", it, (g + 1) * HPG * TT)
                wait(pe, a + "vp", it, TT)
                if g:
                    wait(pe, a + "og", it, g)
                for kt in range(TT):
                    for j in range(HPG):
                        h = HPG * g + j
                        last = pe.matmul(P[7][32 * j:32 * j + 32, 128 * kt:SEQ], VP[:, kt, PADD * h:PADD * h + PADD],
                                         PT[h % NPT][:, kt, 128 * kt:SEQ], start=(kt == 0), stop=(kt == TT - 1))
                last.then_inc(done(a + "pv"), 1)

            for u in range(UN + LT):
                if u < UN:
                    score(u)
                if u >= LT:
                    transposes(u - LT)
                    if (u - LT) % 16 == 3 and u - LT > 16:
                        values((u - LT) // 16 - 1)
            values(NG - 1)
            for t in range(TT):
                if t == 0:
                    wait(pe, a + "og", it, NG)
                for g in range(NG):
                    last = pe.matmul(P[t // 2][:, SELW * (t % 2):SELW * (t % 2) + SELW], OG[:, g, 128 * t:128 * t + 128],
                                     SEL[:, g, :], start=(g == 0), stop=(g == NG - 1))
                if t % 2:
                    last.then_inc(done(a + "o"), 1)
            if which:
                wait(pe, a + "on", it, 2)
                for t in range(TT):
                    last = pe.transpose(P[2][:, 128 * t:128 * t + 128], ON[:, t, :], ident)
                last.then_inc(done(a + "nt"), 1)
                wait(pe, a + "ntc", it, 1)
                for t in range(TT):
                    last = pe.matmul(P[3][:, 128 * t:128 * t + 128], OT[:, 128 * t:128 * t + 128], WOT[:], start=True, stop=True)
                last.then_inc(done(a + "wo"), 1)

        def experts(it):
            turn(it, "m_")
            wait(pe, "m_ht", it, 1)
            for t in range(TT):
                last = pe.matmul(P[1][:, E * t:E * t + E], HT[:, 128 * t:128 * t + 128], GW[:], start=True, stop=True)
            last.then_inc(done("m_lg"), 1)

            def up(e):
                if e >= 2:
                    wait(pe, "m_sg", it, e - 1)
                pe.matmul(P[2 + e % 2], WG[:, e, :], HT[:], start=True, stop=True).then_inc(done("m_g"), 1)
                if e >= 2:
                    wait(pe, "m_hu", it, e - 1)
                pe.matmul(P[4 + e % 2], WU[:, e, :], HT[:], start=True, stop=True).then_inc(done("m_u"), 1)

            def weight(e):
                if e:
                    wait(pe, "m_hi", it, e)
                else:
                    wait(pe, "m_cbt", it, 1)
                pe.matmul(P[6], SELC[:, e, :], CBT[:], start=True, stop=True).then_inc(done("m_c"), 1)

            def down(e):
                wait(pe, "m_hi", it, e + 1)
                pe.matmul(P[7], WD[:, e, :], HI[e % 2], start=(e == 0), stop=(e == EP)).then_inc(done("m_dn"), 1)

            up(0)
            up(1)
            wait(pe, "m_cb", it, 1)
            for t in range(TT):
                last = pe.transpose(P[1].bitcast(BF16)[0:96, 128 * t:128 * t + 128],
                                    CB[:, t].rearrange("p a e -> p (a e)"), identb)
            last.then_inc(done("m_ct"), 1)
            for e in range(EP + 1):
                if e < EP:
                    weight(e)
                if 2 <= e + 1 <= EP:
                    up(e + 1)
                if e >= 1:
                    down(e - 1)
            down(EP)
            wait(pe, "m_yt", it, 1)
            for t in range(TT):
                last = pe.transpose(P[0][:, 128 * t:128 * t + 128], YT[:, 128 * t:128 * t + 128], ident)
            last.then_inc(done("m_z"), 1)

        with pe.Fori(0, nbatch) as it:
            attention(it, "a0_", 0)
            experts(it)
            attention(it, "a1_", 1)

    def scalar_program(act):
        credits(act, " ".join(f"{a}{n}" for a in ("a0_", "a1_") for n in ("ht", "ex", "og")))
        credits(act, "a0_sd a1_sd m_sd f_sd a1_qkc a1_ntc m_ht m_ex m_cbt m_sg m_yt")
        act.wait_ge(s_c, 16 * (NC - 2))
        act.wait_ge(s_eb, 1)
        act.activation(CE[:], CT[:], ACT.Exp, scale=-1.0).then_inc(s_ce, 1)
        act.wait_ge(s_ms, 3)

        def deviation(it, a):
            wait(act, a + "mv", it, TT)
            act.activation(SD[:], MV[:, :, 1], ACT.Sqrt, bias=EPSC[:]).then_inc(done(a + "sd"), 1)

        def modulated(it, a, layer, k):
            wait(act, a + "xt", it, 1)
            act.activation(HT[:], P[0], ACT.Identity, bias=MODT[:, layer, k, bass.ds(it, 1)],
                           scale=MODT[:, layer, k + 1, bass.ds(it, 1)]).then_inc(done(a + "ht"), 1)

        def attention(it, a, which):
            deviation(it, a)
            modulated(it, a, which, 0)
            if which:
                for k, dst in enumerate((QF, KF)):
                    wait(act, a + "qk", it, k + 1)
                    act.activation(dst[:], P[2 + k], ACT.Identity, bias=BQK[:, k:k + 1]).then_inc(done(a + "qkc"), 1)
            LC = 2

            def exps(u):
                h, qt = divmod(u, TT)
                n = 128 * (qt + 1)
                wait(act, a + "mx", it, u + 1)
                if u >= 3:
                    wait(act, a + "pt", it, u - 2)
                act.activation(PR[u % 3][:, 0:n], SP_[u % 3][:, 0:n], ACT.Exp, bias=NBI[u % 3][:], scale=-1.0)\
                    .then_inc(done(a + "ex"), 1)

            for u in range(UN):
                exps(u)
                if (u - 4) % 16 == 7 and u > 20:
                    out_copy(act, it, a, (u - 4) // 16 - 1)
            out_copy(act, it, a, NG - 1)
            if which:
                wait(act, a + "nt", it, 1)
                act.activation(OT[:], P[2], ACT.Copy).then_inc(done(a + "ntc"), 1)

        def out_copy(act, it, a, g):
            wait(act, a + "pv", it, g + 1)
            if g == 0:
                pass
            act.activation(OG[:, g, :], P[7], ACT.Copy).then_inc(done(a + "og"), 1)

        def experts(it):
            deviation(it, "m_")
            modulated(it, "m_", 0, 3)
            wait(act, "m_lg", it, 1)
            act.activation(R["ex"].rearrange("p t e -> p (t e)"), P[1][:, 0:TT * E], ACT.Exp, scale=-1.0)\
                .then_inc(done("m_ex"), 1)
            for e in range(EP + 1):
                wait(act, "m_g", it, e + 1)
                if e >= 2:
                    wait(act, "m_hu", it, e - 1)
                act.activation(SG[e % 2], P[2 + e % 2], ACT.Silu).then_inc(done("m_sg"), 1)
                if e == 0:
                    wait(act, "m_ct", it, 1)
                    act.activation(CBT[:], P[1].bitcast(BF16)[0:96, 0:SEQ], ACT.Copy).then_inc(done("m_cbt"), 1)
            wait(act, "m_dn", it, EP + 1)
            act.activation(YT, P[7], ACT.Copy).then_inc(done("m_yt"), 1)

        with act.Fori(0, nbatch) as it:
            attention(it, "a0_", 0)
            experts(it)
            attention(it, "a1_", 1)
            deviation(it, "f_")

    def vector_program(ve):
        credits(ve, " ".join(f"{a}{n}" for a in ("a0_", "a1_", "m_", "f_") for n in ("st", "mv", "rd", "xn")))
        credits(ve, " ".join(f"{a}{n}" for a in ("a0_", "a1_") for n in ("vp", "mx", "ptc", "rc", "on", "g", "x")))
        credits(ve, "a1_bo m_r m_cb m_hu m_hi m_gz m_x f_gm f_h")
        ve.memset(EPSC[:], EPS).then_inc(s_eb, 1)
        ve.wait_ge(s_c, 16 * (NC - 2))
        ve.tensor_copy(EB[:, 0:256], EB[:, 256:257].broadcast_to([GH, 256])).then_inc(s_eb, 1)
        ve.memset(EB[:, 512:640], -1e30).then_inc(s_eb, 1)
        ve.wait_ge(s_ce, 1)
        ve.tensor_scalar(CE[:], CE[:], 1.0, None, ALU.add).then_inc(s_ce, 1)
        ve.wait_ge(s_ce, 2)
        ve.reciprocal(CE[:], CE[:]).then_inc(s_ce, 1)
        ve.wait_ge(s_ce, 3)
        ve.tensor_tensor(SIL[:], CE[:], CT[:], ALU.mult).then_inc(s_ce, 1)
        ve.wait_ge(s_mm, 1)
        ve.tensor_copy(MODT[:].rearrange("p l k b -> p (l k b)"), P[0][:, 0:12 * NB]).then_inc(s_ms, 1)
        ve.wait_ge(s_ms, 1)
        for k in (1, 4):
            ve.tensor_scalar(MODT[:, :, k, :], MODT[:, :, k, :], 1.0, None, ALU.add).then_inc(s_ms, 1)
        for i in range(2):
            for k in range(2):
                last = ve.tensor_copy(MROW[:, i, 384 * k:384 * k + 384], P[1 + 2 * i + k][0:NB, 0:384])
        last.then_inc(s_ms, 1)
        ve.wait_ge(s_ms, 4)
        g = MROW.rearrange("b l (k d) -> b l k d", d=D)[:, :, 2:6:3, :]
        ms, ma, mr = (t.rearrange("b (l k) d -> b l k d", l=2) for t in (MS, MA, MR[:, 0:4, :]))
        ve.tensor_scalar(ms, g, 0.0, 2.0, ALU.is_ge, ALU.mult).then_inc(s_ms, 1)
        ve.scalar_tensor_tensor(ma, g, -1.0, g, ALU.mult, ALU.max).then_inc(s_ms, 1)
        ve.wait_ge(s_ms, 6)
        ve.tensor_scalar(ma, ma, 0.25, None, ALU.max).then_inc(s_ms, 1)
        ve.tensor_scalar(MR[:, 4, :], MROW[:, 1, 4 * D:5 * D], 1.0, None, ALU.add)
        ve.tensor_copy(MR[:, 5, :], MROW[:, 1, 3 * D:4 * D])
        ve.wait_ge(s_ms, 7)
        ve.scalar_tensor_tensor(mr, ms, -1.0, ma, ALU.add, ALU.mult).then_inc(s_ms, 1)

        def norm(it, a, ready):
            ready()
            for t in range(TT):
                ve.bn_stats(ST[:, t, :], X[:, t, :]).then_inc(done(a + "st"), 1)
            for t in range(TT):
                wait(ve, a + "st", it, t + 1)
                alone(ve)
                ve.bn_aggr(MV[:, t, :], ST[:, t, :]).then_inc(done(a + "mv"), 1)
            wait(ve, a + "sd", it, 1)
            ve.reciprocal(RD[:], SD[:]).then_inc(done(a + "rd"), 1)
            wait(ve, a + "rd", it, 1)
            for t in range(TT):
                ve.tensor_scalar(XN[:, t, :], X[:, t, :], MV[:, t, 0:1], RD[:, t:t + 1], ALU.subtract, ALU.mult)\
                    .then_inc(done(a + "xn"), 1)

        def attention(it, a, which, ready):
            norm(it, a, ready)
            for t in range(TT):
                wait(ve, a + "v", it, t + 1)
                ve.tensor_tensor(VP[:, t, :], P[t % 2], BV[which][:], ALU.add).then_inc(done(a + "vp"), 1)

            def maxima(u):
                h, qt = divmod(u, TT)
                n = 128 * (qt + 1)
                wait(ve, a + "sc", it, u + 1)
                if u >= 3:
                    wait(ve, a + "ex", it, u - 2)
                alone(ve)
                bias = BIAS1[:, h, SEQ - n:SEQ] if which else BIAS0[:, SEQ - n:SEQ]
                ve.tensor_tensor_reduce(out=SP_[u % 3][:, 0:n], in0=P[2 + u % 3][:, 0:n], in1=bias, scale=-1.0,
                                        scalar=3e38, op0=ALU.add, op1=ALU.min, accum_out=NBI[u % 3][:])\
                    .then_inc(done(a + "mx"), 1)

            def copies(u):
                h, qt = divmod(u, TT)
                wait(ve, a + "pt", it, u + 1)
                if qt == 0 and h >= NPT:
                    wait(ve, a + "pv", it, (h - NPT) // HPG + 1)
                ve.tensor_copy(PT[h % NPT][:, 0:qt + 1, 128 * qt:128 * qt + 128],
                               P[5 + u % 2][:, 0:128 * (qt + 1)].rearrange("p (k q) -> p k q", q=128))\
                    .then_inc(done(a + "ptc"), 1)

            LC = 3
            for u in range(UN + LC):
                if u < UN:
                    maxima(u)
                if u >= LC:
                    copies(u - LC)
            for k in range(2):
                wait(ve, a + "o", it, k + 1)
                o = P[k][:, 0:2 * SELW].rearrange("p (t w) -> p t w", w=SELW)
                ve.reciprocal(RC[:, 2 * k:2 * k + 2, :], o[:, :, D:SELW]).then_inc(done(a + "rc"), 1)
                wait(ve, a + "rc", it, k + 1)
                for t in range(2):
                    last = ve.tensor_tensor(ON[:, 2 * k + t, :].rearrange("p (h d) -> p h d", d=GD),
                                            o[:, t, 0:D].rearrange("p (h d) -> p h d", d=GD),
                                            RC[:, 2 * k + t, :].unsqueeze(2).broadcast_to([128, GH, GD]), ALU.mult)
                last.then_inc(done(a + "on"), 1)
            src = ON
            if which:
                wait(ve, a + "wo", it, 1)
                ve.tensor_tensor(TMP[:], P[3].rearrange("p (t d) -> p t d", d=D), BO[:].unsqueeze(1).broadcast_to([128, TT, D]),
                                 ALU.add).then_inc(done(a + "bo"), 1)
                wait(ve, a + "bo", it, 1)
                src = TMP
            else:
                wait(ve, a + "on", it, 2)
            gated(it, a, src[:], 2 * which)

        def gate(r, it):
            return GATE[:, r, bass.ds(it, 1), :].broadcast_to([128, TT, D])

        def gated(it, a, src, r, names=("g", "x")):
            ve.tensor_tensor(TMP2[:], src, gate(r, it), ALU.mult).then_inc(done(a + names[0]), 1)
            wait(ve, a + names[0], it, 1)
            ve.tensor_tensor(X[:], X[:], TMP2[:], ALU.add).then_inc(done(a + names[1]), 1)

        def route(it):
            n = [0]

            def step(ins):
                n[0] += 1
                ins.then_inc(done("route"), 1)

            def sync():
                wait(ve, "route", it, n[0])

            tt, ts = ve.tensor_tensor, ve.tensor_scalar
            wait(ve, "m_ex", it, 1)
            step(ts(R["ex1"], R["ex"], 1.0, None, ALU.add))
            sync()
            step(ve.reciprocal(R["score"], R["ex1"]))
            sync()
            step(tt(R["sc"], R["score"], GB[:].unsqueeze(1).broadcast_to([128, TT, E]), ALU.add))
            sync()
            v = R["sc"].rearrange("p t (g k) -> p t g k", k=4)
            for dst, i, op in (("hi1", 0, ALU.max), ("lo1", 0, ALU.min), ("hi2", 2, ALU.max), ("lo2", 2, ALU.min)):
                step(tt(Gs[dst], v[:, :, :, i], v[:, :, :, i + 1], op))
            sync()
            for dst, x, y, op in (("t1", "hi1", "hi2", ALU.max), ("m", "hi1", "hi2", ALU.min), ("l", "lo1", "lo2", ALU.max)):
                step(tt(Gs[dst], Gs[x], Gs[y], op))
            sync()
            step(tt(Gs["t2"], Gs["m"], Gs["l"], ALU.max))
            sync()
            step(tt(Gs["gs"], Gs["t1"], Gs["t2"], ALU.add))
            sync()
            other = Gs["gs"].unsqueeze(2).broadcast_to([128, TT, GROUPS, GROUPS])
            own = Gs["gs"].unsqueeze(3).broadcast_to([128, TT, GROUPS, GROUPS])
            step(tt(GT, other, own, ALU.is_gt))
            step(tt(GQ, other, own, ALU.is_equal))
            sync()
            step(tt(GQ2, GQ, LOW[:].unsqueeze(1).broadcast_to([128, TT, GROUPS, GROUPS]), ALU.mult))
            sync()
            step(tt(GQ3, GT, GQ2, ALU.add))
            sync()
            step(ve.tensor_reduce(Gs["rank"], GQ3, AX.X, ALU.add))
            sync()
            step(ts(Gs["gm"], Gs["rank"], TKG - 0.5, None, ALU.is_lt))
            sync()
            step(tt(R["mask0"].rearrange("p t (g k) -> p t g k", k=4), v,
                    Gs["gm"].unsqueeze(3).broadcast_to([128, TT, GROUPS, 4]), ALU.mult))
            sync()
            step(ts(R["mask1"], R["mask0"], 0.0, None, ALU.add))
            sync()
            alone(ve)
            for t in range(TT):
                step(ve.max(V8[:, t, :], R["mask1"][:, t, :]))
            sync()
            alone(ve)
            for t in range(TT):
                step(ve.match_replace(R["repl"][:, t, :], V8[:, t, :], R["mask1"][:, t, :], -1e30))
            sync()
            step(ts(R["sel"], R["repl"], -5e29, None, ALU.is_lt))
            sync()
            step(tt(R["w"], R["sel"], R["score"], ALU.mult))
            sync()
            step(ve.tensor_reduce(WS[:], R["w"], AX.X, ALU.add))
            sync()
            step(ts(WS1[:], WS[:], 1e-20, None, ALU.add))
            sync()
            step(ve.reciprocal(WS2[:], WS1[:]))
            sync()
            step(ts(WS3[:], WS2[:], SCALE, None, ALU.mult))
            sync()
            step(tt(R["comb"], R["w"], WS3[:].unsqueeze(2).broadcast_to([128, TT, E]), ALU.mult))
            sync()
            assert n[0] == NR, n[0]
            ve.tensor_copy(CB[:, :, 0, :], R["comb"]).then_inc(s_split, 1)
            ve.wait_ge(s_split, it * 4 + 1)
            tt(R["r1"], R["comb"], CB[:, :, 0, :], ALU.subtract).then_inc(s_split, 1)
            ve.wait_ge(s_split, it * 4 + 2)
            ve.tensor_copy(CB[:, :, 1, :], R["r1"]).then_inc(s_split, 1)
            ve.wait_ge(s_split, it * 4 + 3)
            tt(R["r2"], R["r1"], CB[:, :, 1, :], ALU.subtract).then_inc(s_split, 1)
            ve.wait_ge(s_split, it * 4 + 4)
            ve.tensor_copy(CB[:, :, 2, :], R["r2"]).then_inc(done("m_cb"), 1)

        def experts(it):
            norm(it, "m_", lambda: wait(ve, "a0_x", it, 1))
            route(it)
            for e in range(EP + 1):
                wait(ve, "m_sg", it, e + 1)
                wait(ve, "m_u", it, e + 1)
                if e >= 2:
                    wait(ve, "m_dn", it, e - 1)
                dst = HU if e < EP else HI
                ve.tensor_tensor(dst[e % 2], P[4 + e % 2], SG[e % 2], ALU.mult)\
                    .then_inc(done("m_hu" if e < EP else "m_hi"), 1)
                if e < EP:
                    wait(ve, "m_hu", it, e + 1)
                    wait(ve, "m_c", it, e + 1)
                    ve.tensor_tensor(HI[e % 2], P[6], HU[e % 2], ALU.mult).then_inc(done("m_hi"), 1)
            wait(ve, "m_z", it, 1)
            gated(it, "m_", P[0].rearrange("p (t d) -> p t d", d=D), 1, ("gz", "x"))

        def modulated(it):
            norm(it, "f_", lambda: wait(ve, "a1_x", it, 1))
            wait(ve, "f_xn", it, TT)
            ve.tensor_tensor(TMP[:], XN[:], gate(4, it), ALU.mult).then_inc(done("f_gm"), 1)
            wait(ve, "f_gm", it, 1)
            ve.tensor_tensor(TMP2[:], TMP[:], gate(5, it), ALU.add).then_inc(done("f_h"), 1)

        for h in range(GH):
            ve.wait_ge(s_bt, h + 1)
            ve.tensor_copy(BIAS1[:, h, :], P[6 + h % 2]).then_inc(s_bf, 1)
        ve.wait_ge(s_gl, 16)
        ve.wait_ge(s_bf, GH)
        with ve.Fori(0, nbatch) as it:
            ve.wait_ge(s_wk, it * 16)
            attention(it, "a0_", 0, lambda: ve.wait_ge(s_x, (it + 1) * 16))
            experts(it)
            attention(it, "a1_", 1, lambda: wait(ve, "m_x", it, 1))
            modulated(it)

    def gpsimd_program(pool):
        credits(pool, "a0_qm a1_qm")
        pool.wait_ge(s_c, 16 * (NC - 2))

        def masked(it, a, which):
            wait(pool, a + "qkc" if which else a + "ht", it, 1)
            q = QF if which else HT
            for h in range(GH):
                if h >= 2:
                    wait(pool, a + "sc", it, TT * (h - 1))
                alone(pool)
                pool.tensor_scalar(QM[h % 2][:], q[:], HM[:, h:h + 1], 0.0, ALU.mult, ALU.add).then_inc(done(a + "qm"), 1)

        with pool.Fori(0, nbatch) as it:
            masked(it, "a0_", 0)
            masked(it, "a1_", 1)

    s_split = sem("split_steps")
    return dict(sync=sync_program, tensor=tensor_program, scalar=scalar_program, vector=vector_program, gpsimd=gpsimd_program)


def local_layers(sb, sem, s_alone, dr, ident, identb, psum, x_out, nlayers, nbatch):
    PS = psum
    QKV = [PS[:, 0, :], PS[:, 1, :]]
    TRA = PS[:, 2, :]
    TRP = PS[:, 3, :]
    SB = [PS[:, 4, :], PS[:, 5, :]]
    OV = PS[:, 6, :]
    MISC = PS[:, 7, :]

    WQKV = [sb(f"WQKV{i}", [128, 3 * INNER]) for i in range(2)]
    WO = [sb(f"WO{i}", [128, PAIRS, D]) for i in range(2)]
    W1 = [sb(f"W1{i}", [128, 2 * DI]) for i in range(2)]
    W2 = [sb(f"W2{i}", [128, 3, D]) for i in range(2)]
    SM = [sb(f"SM{i}", [128, 8]) for i in range(2)]
    B2 = [sb(f"B2{i}", [128, D]) for i in range(2)]
    QS = [sb(f"QS{i}", [128, 4, LD]) for i in range(2)]
    ROPE0 = sb("ROPE0", [128, TT, 4, LD])
    ROPE = sb("ROPE", [128, TT, 4, LD])
    MASKB = sb("MASKB", [128, 2, 2, KEYS], BF16)
    CEN = sb("CEN", [128, 128])
    AVG = sb("AVG", [128, 128])
    EPSC = sb("EPSC", [128, 1])

    XA = sb("XA", [128, TT, D])
    XR = sb("XR", [128, TT, D])
    XO = sb("XO", [128, TT, D])
    XB = sb("XB", [128, TT, D])
    XS = sb("XS", [128, SEQ + 1])
    XF = sb("XF", [128, SEQ + 1])
    RAW = [sb(f"RAW{i}", [128, 512]) for i in range(3)]
    SQR = [sb(f"SQR{i}", [128, 512]) for i in range(2)]
    T1 = [sb(f"T1{i}", [128, 512]) for i in range(2)]
    T2 = [sb(f"T2{i}", [128, 512]) for i in range(2)]
    SS = sb("SS", [128, TT, 2 * LH])
    RN = sb("RN", [128, TT, 2 * LH])
    ROT = sb("ROT", [128, TT, 4, 512])
    V = sb("V", [128, TT, INNER])
    QT = [sb(f"QT{i}", [128, PAIRS, 128]) for i in range(2)]
    KD = [sb(f"KD{i}", [128, PAIRS, 2, KEYS]) for i in range(2)]
    NP = 4
    PR = [sb(f"PR{i}", [128, 2, KEYS]) for i in range(NP)]
    MX = [sb(f"MX{i}", [128, 2]) for i in range(NP)]
    NBI = [sb(f"NBI{i}", [128, 2]) for i in range(NP)]
    SU = [sb(f"SU{i}", [128, 2]) for i in range(NP)]
    RS = [sb(f"RS{i}", [128, 2]) for i in range(NP)]
    PT = [sb(f"PT{i}", [128, 2, 128]) for i in range(2)]
    PTE = [sb(f"PTE{i}", [128, 2, WIN]) for i in range(2)]
    OT = [sb(f"OT{i}", [128, PAIRS, 128]) for i in range(2)]
    SQF = sb("SQF", [128, SEQ])
    STD = sb("STD", [128, SEQ])
    RSTD = sb("RSTD", [128, SEQ])
    XN0 = sb("XN0", [128, SEQ])
    XN1 = sb("XN1", [128, SEQ])
    GE = [sb(f"GE{i}", [128, SEQ]) for i in range(2)]
    HID = sb("HID", [128, 3, SEQ])

    UN = TT * PAIRS
    s_tab = sem("local_tables")
    s_w = [sem(f"local_weights{i}") for i in range(2)]
    NW = 10
    s_xa = sem("xa_loaded")
    s_xr = sem("xr_loaded")
    s_st = sem("x_stored")
    s_avg = sem("average_matrix_ready")
    s_fill = sem("local_buffers_filled")
    c = {}
    for name, per in [
        ("xt", 1), ("xs", 2), ("qkv", 6 * TT), ("raw", 6 * TT), ("sqr", 4 * TT), ("ssum", 4 * TT),
        ("t1", 4 * TT), ("t2", 4 * TT), ("rot", 4 * TT), ("norm", 1), ("nmax", 1), ("rn", 1), ("rnq", 1), ("kn", TT),
        ("qkt", 4 * TT), ("qkc", 4 * TT), ("kprev", 2 * (TT - 1)),
        ("sc", UN), ("mx", UN), ("nb", UN), ("ex", UN), ("rs", UN), ("pn", UN), ("pt", UN),
        ("ptm", UN), ("pte", UN - PAIRS), ("ov", 2 * TT), ("ovc", 2 * TT), ("wo", TT), ("res", TT),
        ("ft", 1), ("xf", 2), ("cen", 1), ("sqf", 1), ("var", 1), ("std", 1), ("rstd", 1), ("xn0", 1), ("xn1", 1),
        ("w1", 6), ("ge", 3), ("hid", 3), ("w2", 1), ("xb", 1), ("xo", 1),
    ]:
        c[name] = Count(sem(f"l_{name}"), per, per)
    s_rope = Count(sem("rope_scaled"), 1)

    def alone(eng):
        eng.sem_inc(s_alone, 1)

    def credits(eng, names):
        for n in names.split():
            eng.sem_inc(c[n].sem, c[n].per)

    def wait(eng, name, it, n):
        eng.wait_ge(c[name].sem, c[name].at(it, n))

    def wait_before(eng, name, it, n):
        eng.wait_ge(c[name].sem, c[name].before(it, n))

    def earlier(eng, name, it, n):
        eng.wait_ge(c[name].sem, c[name].at(it, n))

    def layers(eng, per_layer, body):
        with eng.Fori(0, nlayers // 2) as lp:
            for par in range(2):
                per_layer(lp, par)
                alone(eng)
                with eng.Fori(0, nbatch) as b:
                    body(lp * (2 * nbatch) + (b + par * nbatch), par, b)

    def batch(x, b):
        return x[bass.ds(b, 1)].rearrange("o p t d -> p (o t) d")

    xout = x_out.rearrange("b (t p) d -> b p t d", p=128)

    def sync_program(sp):
        sp.dma_start(ROPE0[:], dr["rope"]).then_inc(s_tab, 16)
        sp.dma_start(MASKB[:].rearrange("p a b c -> p (a b c)").bitcast(F32), dr["mask"]).then_inc(s_tab, 16)
        sp.dma_start(CEN[:], dr["cen"]).then_inc(s_tab, 16)

        def weights(layer, par):
            for dst, src in [
                (WQKV[par][:], dr["Wqkv"][bass.ds(layer, 1), :, :].rearrange("o k n -> k (o n)")),
                (WO[par][:], dr["Wo"][bass.ds(layer, 1), :, :].rearrange("o (a p) n -> p (o a) n", p=128)),
                (W1[par][:], dr["W1"][bass.ds(layer, 1), :, :].rearrange("o k n -> k (o n)")),
                (W2[par][:, 0:2, :], dr["W2"][bass.ds(layer, 1), 0:256, :].rearrange("o (a p) n -> p (o a) n", p=128)),
                (W2[par][0:DI - 256, 2, :], dr["W2"][bass.ds(layer, 1), 256:DI, :].rearrange("o p n -> p (o n)")),
                (SM[par][:], dr["small"][bass.ds(layer, 1), :, :].rearrange("o k n -> k (o n)")),
                (B2[par][:], dr["b2"][bass.ds(layer, 1), :].broadcast_to([128, D])),
                (QS[par][:, 0, :], dr["qs"][bass.ds(layer, 1), 0:LD].broadcast_to([128, LD])),
                (QS[par][:, 1:3, :].rearrange("p a d -> p (a d)"), dr["qs"][bass.ds(layer, 1), LD:3 * LD].broadcast_to([128, 2 * LD])),
                (QS[par][:, 3, :], dr["qs"][bass.ds(layer, 1), 3 * LD:4 * LD].broadcast_to([128, LD])),
            ]:
                sp.dma_start(dst, src).then_inc(s_w[par], 16)

        sp.sem_inc(s_st, 16 * (nbatch - 1))
        weights(0, 0)
        sp.dma_start(XA[:], batch(xout, 0)).then_inc(s_xa, 16)
        sp.dma_start(XR[:], batch(xout, 0)).then_inc(s_xr, 16)
        with sp.Fori(0, nlayers // 2) as lp:
            for par in range(2):
                if par == 0:
                    first = lp * (2 * nbatch)
                    for name in ("wo", "xo"):
                        sp.wait_ge(c[name].sem, c[name].before(first, c[name].per))
                        alone(sp)
                    weights(lp * 2 + 1, 1)
                else:
                    first = lp * (2 * nbatch) + nbatch
                    for name in ("wo", "xo"):
                        sp.wait_ge(c[name].sem, c[name].before(first, c[name].per))
                        alone(sp)
                    weights((lp * 2 + 2) % nlayers, 0)
                with sp.Fori(0, nbatch) as b:
                    it = lp * (2 * nbatch) + (b + par * nbatch)
                    nxt = (b + 1) % nbatch
                    wait(sp, "xt", it, 1)
                    sp.wait_ge(s_st, (it + 1) * 16)
                    alone(sp)
                    sp.dma_start(XA[:], batch(xout, nxt)).then_inc(s_xa, 16)
                    wait(sp, "ft", it, 1)
                    wait(sp, "xb", it, 1)
                    alone(sp)
                    sp.dma_start(XR[:], batch(xout, nxt)).then_inc(s_xr, 16)
                    wait(sp, "xo", it, 1)
                    alone(sp)
                    sp.dma_start(batch(xout, b), XO[:]).then_inc(s_st, 16)
        sp.wait_ge(s_st, 16 * (nlayers * nbatch + nbatch - 1))
        sp.wait_ge(s_xa, 16 * (nlayers * nbatch + 1))
        sp.wait_ge(s_xr, 16 * (nlayers * nbatch + 1))
        sp.wait_ge(s_w[0], 16 * NW * (nlayers // 2 + 1))

    def tensor_program(pe):
        credits(pe, "xt qkv qkt sc pt ov wo ft cen var w1 w2")
        pe.wait_ge(s_avg, 1)
        pe.wait_ge(s_fill, 5)
        pe.wait_ge(s_tab, 48)

        def transpose_x(it):
            pe.wait_ge(s_xa, (it + 1) * 16)
            wait_before(pe, "qkc", it, 4 * TT)
            wait_before(pe, "xf", it, 2)
            for j in range(TT):
                last = pe.transpose(TRA[:, 128 * j:128 * j + 128], XA[:, j, :], ident)
            last.then_inc(c["xt"].sem, 1)

        def project(it, par, j):
            for k in range(6):
                n = 6 * j + k
                if n == 0:
                    wait(pe, "xs", it, 2)
                if n >= 2:
                    wait(pe, "raw", it, n - 1)
                else:
                    wait_before(pe, "hid" if n == 0 else "xo", it, 3 if n == 0 else 1)
                pe.matmul(QKV[n % 2], XS[:, 128 * j:128 * j + 128], WQKV[par][:, 512 * k:512 * k + 512],
                          start=True, stop=True).then_inc(c["qkv"].sem, 1)

        def transpose_qk(it, j, ks=range(4)):
            for k in ks:
                n = 4 * j + k
                if k == 0:
                    wait(pe, "rot", it, 4 * j + 4)
                if k == 2:
                    wait(pe, "kn", it, j + 1)
                if n == 0:
                    wait(pe, "xs", it, 2)
                else:
                    wait(pe, "qkc", it, n)
                for i in range(4):
                    last = pe.transpose(TRA[:, 128 * i:128 * i + 128], ROT[:, j, k, 128 * i:128 * i + 128], ident)
                last.then_inc(c["qkt"].sem, 1)

        def scores(it, u):
            j, p = divmod(u, PAIRS)
            if p == 0:
                wait(pe, "qkc", it, 4 * (j + 1))
                if j:
                    wait(pe, "kprev", it, 2 * j)
            earlier(pe, "ex", it, u - 1)
            pe.matmul(SB[u % 2][:, 0:2 * KEYS], identb, MASKB[:, min(j, 1)].rearrange("p a c -> p (a c)"),
                      start=True, stop=False)
            pe.matmul(SB[u % 2][:, 0:2 * KEYS], QT[j % 2][:, p, :],
                      KD[j % 2][:, p].rearrange("p a c -> p (a c)"),
                      start=False, stop=True).then_inc(c["sc"].sem, 1)

        def transpose_p(it, u):
            j, p = divmod(u, PAIRS)
            wait(pe, "pn", it, u + 1)
            earlier(pe, "ptm", it, u)
            if u > PAIRS:
                wait(pe, "pte", it, u - PAIRS)
            elif u == 0:
                wait_before(pe, "pte", it, UN - PAIRS)
            for hh in range(2):
                last = pe.transpose(TRP[:, 128 * hh:128 * hh + 128], PR[u % NP][:, hh, WIN:KEYS], ident)
            if j:
                for hh in range(2):
                    last = pe.transpose(TRP[0:WIN, 256 + WIN * hh:256 + WIN * hh + WIN],
                                        PR[u % NP][0:WIN, hh, 0:WIN], ident[0:WIN, 0:WIN])
            last.then_inc(c["pt"].sem, 1)

        def values(it, u):
            j, p = divmod(u, PAIRS)
            wait(pe, "ptm", it, u + 1)
            if j:
                wait(pe, "pte", it, u + 1 - PAIRS)
            if u == 0:
                wait(pe, "raw", it, 6 * TT)
            if p % 4 == 0:
                earlier(pe, "ovc", it, u // 4)
            for hh in range(2):
                rows = slice(64 * hh, 64 * hh + 64)
                col = 128 * (p % 4)
                h = 2 * p + hh
                last = pe.matmul(OV[rows, col:col + 128], V[:, j, 64 * h:64 * h + 64], PT[u % 2][:, hh, :],
                                 start=True, stop=(j == 0))
                if j:
                    last = pe.matmul(OV[rows, col:col + WIN], V[96:128, j - 1, 64 * h:64 * h + 64],
                                     PTE[u % 2][96:128, hh, :], start=False, stop=True)
            if p % 4 == 3:
                last.then_inc(c["ov"].sem, 1)

        def project_out(it, par, j):
            wait(pe, "ovc", it, 2 * j + 2)
            if j:
                wait(pe, "res", it, j)
            else:
                wait_before(pe, "xn0", it, 1)
            for p in range(PAIRS):
                last = pe.matmul(MISC[:, 0:D], OT[j % 2][:, p, :], WO[par][:, p, :],
                                 start=(p == 0), stop=(p == PAIRS - 1))
            last.then_inc(c["wo"].sem, 1)

        def feed_forward(it, par):
            wait(pe, "res", it, TT)
            wait(pe, "qkc", it, 4 * TT)
            for j in range(TT):
                last = pe.transpose(TRA[:, 128 * j:128 * j + 128], XR[:, j, :], ident)
            last.then_inc(c["ft"].sem, 1)
            wait(pe, "xf", it, 2)
            pe.matmul(MISC, CEN[:], XF[:, 0:SEQ], start=True, stop=True).then_inc(c["cen"].sem, 1)
            wait(pe, "sqf", it, 1)
            wait(pe, "raw", it, 6 * TT)
            pe.matmul(QKV[0], AVG[:], SQF[:], start=True, stop=True).then_inc(c["var"].sem, 1)
            wait(pe, "xn1", it, 1)
            for i, (at, m) in enumerate(BLK):
                if i:
                    wait(pe, "ge", it, i)
                pe.matmul(QKV[1][0:m, :], W1[par][:, DI + at:DI + at + m], XN1[:], start=True, stop=True)\
                    .then_inc(c["w1"].sem, 1)
                if i:
                    wait(pe, "hid", it, i)
                else:
                    wait(pe, "std", it, 1)
                pe.matmul(QKV[0][0:m, :], W1[par][:, at:at + m], XN1[:], start=True, stop=True)\
                    .then_inc(c["w1"].sem, 1)
            wait(pe, "hid", it, 3)
            wait(pe, "ge", it, 3)
            for j in range(TT):
                for i, (at, m) in enumerate(BLK):
                    last = pe.matmul(QKV[1][:, 128 * j:128 * j + 128], HID[0:m, i, 128 * j:128 * j + 128],
                                     W2[par][0:m, i, :], start=(i == 0), stop=(i == 2))
            last.then_inc(c["w2"].sem, 1)

        def per_layer(lp, par):
            pe.wait_ge(s_w[par], (lp + 1) * (16 * NW))

        def body(it, par, b):
            transpose_x(it)
            for j in range(TT):
                project(it, par, j)
            transpose_qk(it, 0)
            LT, LV = 3, 4
            for u in range(UN + LV):
                if u < UN:
                    scores(it, u)
                    if 2 <= u % PAIRS < 6 and u // PAIRS + 1 < TT:
                        transpose_qk(it, u // PAIRS + 1, [u % PAIRS - 2])
                if LT <= u < UN + LT:
                    transpose_p(it, u - LT)
                if u >= LV:
                    values(it, u - LV)
                    if (u - LV) % PAIRS == 2 and u - LV > PAIRS:
                        project_out(it, par, (u - LV) // PAIRS - 1)
            project_out(it, par, TT - 1)
            feed_forward(it, par)

        layers(pe, per_layer, body)

    def scalar_program(act):
        credits(act, "xs raw norm ex pte ovc qkc xf sqf std ge")
        act.wait_ge(s_fill, 5)

        def shifted(it, dst, name, src_name, reader):
            wait(act, src_name, it, 1)
            wait_before(act, reader[0], it, reader[1])
            act.activation(dst[0:64, 0:SEQ], TRA[0:64, :], ACT.Copy).then_inc(c[name].sem, 1)
            act.activation(dst[64:128, 1:SEQ], TRA[64:128, 0:SEQ - 1], ACT.Copy).then_inc(c[name].sem, 1)

        def raw(it, n):
            j, k = divmod(n, 6)
            wait(act, "qkv", it, n + 1)
            if k < 4:
                m = 4 * j + k
                earlier(act, "t2", it, m - 2)
                act.activation(RAW[m % 3][:], QKV[n % 2], ACT.Copy).then_inc(c["raw"].sem, 1)
            else:
                if n == 4:
                    wait_before(act, "ov", it, 2 * TT)
                act.activation(V[:, j, 512 * (k - 4):512 * (k - 4) + 512], QKV[n % 2], ACT.Copy)\
                    .then_inc(c["raw"].sem, 1)

        def qk_copies(it, j, ks=range(4)):
            for k in ks:
                n = 4 * j + k
                wait(act, "qkt", it, n + 1)
                if k < 2:
                    if k == 0:
                        earlier(act, "sc", it, PAIRS * (j - 1))
                    act.activation(QT[j % 2][:, 4 * k:4 * k + 4, :].rearrange("p a n -> p (a n)"), TRA, ACT.Copy)\
                        .then_inc(c["qkc"].sem, 1)
                else:
                    g = slice(4 * (k - 2), 4 * (k - 2) + 4)
                    if k == 2 and j:
                        wait(act, "kprev", it, 2 * j - 2) if j > 1 else None
                    src = TRA.rearrange("p (a n) -> p a n", a=4)
                    act.activation(KD[j % 2][0:64, g, 0, WIN:KEYS], src[0:64], ACT.Copy)
                    act.activation(KD[j % 2][64:128, g, 1, WIN:KEYS], src[64:128], ACT.Copy)\
                        .then_inc(c["qkc"].sem, 1)

        def exps(it, u):
            j, p = divmod(u, PAIRS)
            wait(act, "nb", it, u + 1)
            earlier(act, "pt", it, u + 1 - NP)
            earlier(act, "rs", it, u + 1 - NP)
            for hh in range(2):
                last = act.activation(PR[u % NP][:, hh, :], SB[u % 2][:, KEYS * hh:KEYS * hh + KEYS], ACT.Exp,
                                      bias=NBI[u % NP][:, hh:hh + 1], scale=RN[:, j, 2 * p + hh:2 * p + hh + 1],
                                      accum_out=SU[u % NP][:, hh:hh + 1])
            last.then_inc(c["ex"].sem, 1)

        def edge(it, u):
            wait(act, "ptm", it, u + 1)
            earlier(act, "ov", it, max(0, (u - 2) // 4)) if False else None
            act.activation(PTE[u % 2][96:128, :, :].rearrange("p a n -> p (a n)"), TRP[0:WIN, 256:256 + 2 * WIN],
                           ACT.Copy).then_inc(c["pte"].sem, 1)

        def out_copy(it, g):
            wait(act, "ov", it, g + 1)
            if g % 2 == 0:
                earlier(act, "wo", it, g // 2 - 1)
            act.activation(OT[g // 2 % 2][:, 4 * (g % 2):4 * (g % 2) + 4, :].rearrange("p a n -> p (a n)"), OV,
                           ACT.Copy).then_inc(c["ovc"].sem, 1)

        def per_layer(lp, par):
            act.wait_ge(s_w[par], (lp + 1) * (16 * NW))

        def body(it, par, b):
            shifted(it, XS, "xs", "xt", ("qkv", 6 * TT))
            for n in range(6 * TT):
                raw(it, n)
            wait(act, "ssum", it, 4 * TT)
            wait_before(act, "nmax", it, 1)
            act.activation(SS[:], SS[:], ACT.Sqrt).then_inc(c["norm"].sem, 1)
            qk_copies(it, 0)
            for u in range(UN + 5):
                if u < UN:
                    exps(it, u)
                    if 2 <= u % PAIRS < 6 and u // PAIRS + 1 < TT:
                        qk_copies(it, u // PAIRS + 1, [u % PAIRS - 2])
                v = u - 3
                if PAIRS <= v < UN:
                    edge(it, v)
                v = u - 5
                if 0 <= v < UN and v % 4 == 3:
                    out_copy(it, v // 4)
            shifted(it, XF, "xf", "ft", ("cen", 1))
            wait(act, "cen", it, 1)
            wait_before(act, "var", it, 1)
            act.activation(SQF[:], MISC, ACT.Square).then_inc(c["sqf"].sem, 1)
            wait(act, "var", it, 1)
            wait_before(act, "rstd", it, 1)
            act.activation(STD[:], QKV[0], ACT.Sqrt, bias=EPSC[:]).then_inc(c["std"].sem, 1)
            for i, (at, m) in enumerate(BLK):
                wait(act, "w1", it, 2 * i + 1)
                earlier(act, "hid", it, i - 1)
                act.activation(GE[i % 2][0:m, :], QKV[1][0:m, :], ACT.Gelu, bias=SM[par][0:m, 3 + i:4 + i])\
                    .then_inc(c["ge"].sem, 1)

        layers(act, per_layer, body)

    def vector_program(ve):
        credits(ve, "sqr ssum t1 t2 nmax rn rnq mx nb rs ptm res rstd xn0 xn1 hid xo kprev")
        ve.memset(AVG[:], 1.0 / D).then_inc(s_avg, 1)

        def heads(ap):
            return ap.rearrange("p (h d) -> p h d", d=LD)

        def products(it, m):
            j, k = divmod(m, 4)
            x = RAW[m % 3]
            wait(ve, "raw", it, 6 * j + k + 1)
            earlier(ve, "ssum", it, m - 1)
            ve.tensor_tensor(SQR[m % 2][:], x[:], x[:], ALU.mult).then_inc(c["sqr"].sem, 1)
            earlier(ve, "rot", it, m - 1)
            tab = ROPE[:, j, 2 * (k // 2)].unsqueeze(1).broadcast_to([128, 8, LD])
            ve.tensor_tensor(heads(T1[m % 2][:]), heads(x[:]), tab, ALU.mult).then_inc(c["t1"].sem, 1)
            xs = x[:].rearrange("p (h a d) -> p h a d", a=2, d=LD // 2)
            ts_ = T2[m % 2][:].rearrange("p (h a d) -> p h a d", a=2, d=LD // 2)
            for a in range(2):
                tab = ROPE[:, j, 2 * (k // 2) + 1, 32 * a:32 * a + 32].unsqueeze(1).broadcast_to([128, 8, 32])
                last = ve.tensor_tensor(ts_[:, :, a, :], xs[:, :, 1 - a, :], tab, ALU.mult)
            last.then_inc(c["t2"].sem, 1)
            wait(ve, "sqr", it, m + 1)
            if m == 0:
                wait_before(ve, "rnq", it, 1)
            ve.tensor_reduce(SS[:, j, 8 * k:8 * k + 8], heads(SQR[m % 2][:]), AX.X, ALU.add).then_inc(c["ssum"].sem, 1)

        def norms(it):
            wait(ve, "norm", it, 1)
            ve.tensor_scalar(SS[:], SS[:], 1e-12, None, ALU.max).then_inc(c["nmax"].sem, 1)
            wait(ve, "nmax", it, 1)
            wait_before(ve, "ex", it, UN)
            wait_before(ve, "kn", it, TT)
            ve.reciprocal(RN[:], SS[:]).then_inc(c["rn"].sem, 1)
            wait(ve, "rn", it, 1)
            ve.tensor_scalar(RN[:, :, 0:LH], RN[:, :, 0:LH], 8.0, None, ALU.mult).then_inc(c["rnq"].sem, 1)

        def maxima(it, u):
            j, p = divmod(u, PAIRS)
            wait(ve, "sc", it, u + 1)
            earlier(ve, "nb", it, u + 1 - NP)
            ve.tensor_reduce(MX[u % NP][:], SB[u % 2][:, 0:2 * KEYS].rearrange("p (a c) -> p a c", a=2), AX.X,
                             ALU.max).then_inc(c["mx"].sem, 1)
            wait(ve, "mx", it, u + 1)
            earlier(ve, "ex", it, u + 1 - NP)
            ve.scalar_tensor_tensor(NBI[u % NP][:], MX[u % NP][:], -1.0, RN[:, j, 2 * p:2 * p + 2],
                                    ALU.mult, ALU.mult).then_inc(c["nb"].sem, 1)

        def inverse(it, u):
            wait(ve, "ex", it, u + 1)
            earlier(ve, "pn", it, u + 1 - NP)
            ve.reciprocal(RS[u % NP][:], SU[u % NP][:]).then_inc(c["rs"].sem, 1)

        def p_copy(it, u):
            wait(ve, "pt", it, u + 1)
            ve.tensor_copy(PT[u % 2][:].rearrange("p a n -> p (a n)"), TRP[:, 0:256]).then_inc(c["ptm"].sem, 1)

        def key_edge(it, j):
            wait(ve, "qkc", it, 4 * (j + 1))
            earlier(ve, "sc", it, PAIRS * j)
            for hh in range(2):
                rows = slice(64 * hh, 64 * hh + 64)
                ve.tensor_copy(KD[(j + 1) % 2][rows, :, hh, 0:WIN], KD[j % 2][rows, :, hh, KEYS - WIN:KEYS])\
                    .then_inc(c["kprev"].sem, 1)

        def residual(it, j):
            wait(ve, "wo", it, j + 1)
            if j == 0:
                ve.wait_ge(s_xr, (it + 1) * 16)
            ve.tensor_tensor(XR[:, j, :], XR[:, j, :], MISC[:, 0:D], ALU.add).then_inc(c["res"].sem, 1)

        def feed_forward(it, par):
            wait(ve, "std", it, 1)
            ve.reciprocal(RSTD[:], STD[:]).then_inc(c["rstd"].sem, 1)
            wait(ve, "rstd", it, 1)
            ve.tensor_tensor(XN0[:], MISC, RSTD[:], ALU.mult).then_inc(c["xn0"].sem, 1)
            wait(ve, "xn0", it, 1)
            ve.tensor_scalar(XN1[:], XN0[:], SM[par][:, 6:7], SM[par][:, 7:8], ALU.mult, ALU.add)\
                .then_inc(c["xn1"].sem, 1)
            for i, (at, m) in enumerate(BLK):
                wait(ve, "ge", it, i + 1)
                wait(ve, "w1", it, 2 * i + 2)
                ve.scalar_tensor_tensor(HID[0:m, i, :], QKV[0][0:m, :], SM[par][0:m, i:i + 1], GE[i % 2][0:m, :],
                                        ALU.add, ALU.mult).then_inc(c["hid"].sem, 1)
            wait(ve, "w2", it, 1)
            wait(ve, "xb", it, 1)
            ve.wait_ge(s_st, (it + nbatch - 1) * 16)
            ve.tensor_tensor(XO[:].rearrange("p t d -> p (t d)"), QKV[1], XB[:].rearrange("p t d -> p (t d)"),
                             ALU.add).then_inc(c["xo"].sem, 1)

        def per_layer(lp, par):
            ve.wait_ge(s_w[par], (lp + 1) * (16 * NW))
            ve.wait_ge(s_rope.sem, (lp * 2 + (par + 1)) * 4)

        def body(it, par, b):
            for m in range(4 * TT):
                products(it, m)
            norms(it)
            for u in range(UN + 4):
                if u < UN:
                    if u % PAIRS == 0 and u:
                        pass
                    maxima(it, u)
                if u % PAIRS == 6 and u // PAIRS + 1 < TT:
                    key_edge_late = u // PAIRS
                v = u - 1
                if 0 <= v < UN:
                    inverse(it, v)
                if u % PAIRS == 6 and u // PAIRS + 1 < TT:
                    key_edge(it, u // PAIRS)
                v = u - 3
                if 0 <= v < UN:
                    p_copy(it, v)
                v = u - 4
                if v > PAIRS and v % PAIRS == 3:
                    residual(it, v // PAIRS - 1)
            residual(it, TT - 1)
            feed_forward(it, par)

        layers(ve, per_layer, body)

    def gpsimd_program(pool):
        credits(pool, "rot kn pn xb")
        for n, (part, value) in enumerate([(EPSC[:], EPS), (XS[64:128, 0:1], 0.0), (XF[64:128, 0:1], 0.0),
                                           (KD[0][:], 0.0), (KD[1][:], 0.0)]):
            if n:
                pool.wait_ge(s_fill, n)
            pool.memset(part, value).then_inc(s_fill, 1)

        def per_layer(lp, par):
            pool.wait_ge(s_w[par], (lp + 1) * (16 * NW))
            if True:
                pool.wait_ge(s_tab, 48)
            first = lp * (2 * nbatch) + par * nbatch
            wait_before(pool, "t2", first, 4 * TT)
            for i in range(4):
                pool.tensor_tensor(ROPE[:, :, i, :], ROPE0[:, :, i, :],
                                   QS[par][:, i, :].unsqueeze(1).broadcast_to([128, TT, LD]),
                                   ALU.mult).then_inc(s_rope.sem, 1)

        def body(it, par, b):
            for m in range(4 * TT):
                j, k = divmod(m, 4)
                wait(pool, "t1", it, m + 1)
                wait(pool, "t2", it, m + 1)
                if m == 0:
                    wait_before(pool, "qkt", it, 4 * TT)
                pool.tensor_tensor(ROT[:, j, k, :], T1[m % 2][:], T2[m % 2][:], ALU.add).then_inc(c["rot"].sem, 1)
            wait(pool, "rnq", it, 1)
            wait(pool, "rot", it, 4 * TT)
            for j in range(TT):
                k = ROT[:, j, 2:4, :].rearrange("p a n -> p (a n)").rearrange("p (h d) -> p h d", d=LD)
                pool.tensor_tensor(k, k, RN[:, j, LH:2 * LH].unsqueeze(2).broadcast_to([128, LH, LD]),
                                   ALU.mult).then_inc(c["kn"].sem, 1)
            for u in range(UN):
                wait(pool, "rs", it, u + 1)
                pool.tensor_tensor(PR[u % NP][:], PR[u % NP][:],
                                   RS[u % NP][:].unsqueeze(2).broadcast_to([128, 2, KEYS]),
                                   ALU.mult).then_inc(c["pn"].sem, 1)
            wait(pool, "res", it, TT)
            wait_before(pool, "xo", it, 1)
            pool.tensor_tensor(XB[:], XR[:], B2[par][:].unsqueeze(1).broadcast_to([128, TT, D]),
                               ALU.add).then_inc(c["xb"].sem, 1)

        layers(pool, per_layer, body)

    return dict(sync=sync_program, tensor=tensor_program, scalar=scalar_program, vector=vector_program,
                gpsimd=gpsimd_program)


def last_sum(sb, sem, dr, x_mid, x_work, out):
    G3 = sb("G3", [128, NB, D])
    XM = sb("XM", [128, NB, TT, D])
    XW = sb("XW", [128, NB, TT, D])
    s_in = sem("last_inputs_loaded")
    s_p, s_s, s_o = sem("gated"), sem("summed"), sem("out_stored")

    def batch(x, b):
        return x.rearrange("b (t p) d -> b p t d", p=128)[bass.ds(b, 1)].rearrange("o p t d -> p (o t) d")

    def sync_program(sp):
        sp.dma_start(G3[:], dr["rows"][3:4].broadcast_to([128, NB, D])).then_inc(s_in, 16)
        for b in range(NB):
            sp.dma_start(XM[:, b], batch(x_mid, b)).then_inc(s_in, 16)
            sp.dma_start(XW[:, b], batch(x_work, b)).then_inc(s_in, 16)
        for b in range(NB):
            sp.wait_ge(s_s, b + 1)
            sp.dma_start(batch(out, b), XM[:, b]).then_inc(s_o, 16)
        sp.wait_ge(s_o, 16 * NB)

    def vector_program(ve):
        ve.wait_ge(s_in, 16 * (2 * NB + 1))
        for b in range(NB):
            ve.tensor_tensor(XW[:, b], XW[:, b], G3[:, b:b + 1, :].broadcast_to([128, TT, D]), ALU.mult).then_inc(s_p, 1)
        for b in range(NB):
            ve.wait_ge(s_p, b + 1)
            ve.tensor_tensor(XM[:, b], XM[:, b], XW[:, b], ALU.add).then_inc(s_s, 1)

    return dict(sync=sync_program, vector=vector_program)


def program(nc, dr, x, out):
    for name, shape in (("rows", [ROWS, NB, D]), ("ebrow", [GH, 640])):
        dr[name] = nc.dram_tensor("scratch_" + name, shape, F32, kind="Internal").ap()
    x_mid = nc.dram_tensor("scratch_x_mid", [NB, SEQ, D], F32, kind="Internal").ap()
    x_work = nc.dram_tensor("scratch_x_work", [NB, SEQ, D], F32, kind="Internal").ap()

    with ExitStack() as whole:
        def sem(name):
            return whole.enter_context(nc.semaphore(name))

        def allocator(stack, prefix):
            def sb(name, shape, dt=F32):
                return stack.enter_context(nc.sbuf_tensor(prefix + name, shape, dt))
            return sb

        psum = whole.enter_context(nc.psum_tensor("banks", [128, 8, 512], F32))
        sb = allocator(whole, "w_")
        ident, identb = sb("ident", [128, 128]), sb("identb", [128, 128], BF16)
        s_ident = sem("identity_steps")
        s_alone = sem("nothing_waits_for_this")

        with ExitStack() as stack:
            p = blocks(allocator(stack, "b_"), sem, s_alone, dr, ident[:], identb[:], psum, x, x_mid, x_work, NB)
            block = stack.enter_context(nc.Block())

            @block.sync
            def _(sp):
                p["sync"](sp)

            @block.tensor
            def _(pe):
                pe.wait_ge(s_ident, 3)
                p["tensor"](pe)

            @block.scalar
            def _(act):
                p["scalar"](act)

            @block.vector
            def _(ve):
                p["vector"](ve)

            @block.gpsimd
            def _(pool):
                pool.memset(ident[:], 0.0).then_inc(s_ident, 1)
                pool.wait_ge(s_ident, 1)
                pool.affine_select(out=ident[:], in_=ident[:], compare_op=ALU.not_equal, fill=1.0, base=0,
                                   pattern=[[-1, 128]], channel_multiplier=1).then_inc(s_ident, 1)
                pool.wait_ge(s_ident, 2)
                pool.tensor_copy(identb[:], ident[:]).then_inc(s_ident, 1)
                p["gpsimd"](pool)

        with ExitStack() as stack:
            q = local_layers(allocator(stack, "l_"), sem, s_alone, dr, ident[:], identb[:], psum, x_work, DEPTH, NB)
            block = stack.enter_context(nc.Block())

            @block.sync
            def _(sp):
                q["sync"](sp)

            @block.tensor
            def _(pe):
                q["tensor"](pe)

            @block.scalar
            def _(act):
                q["scalar"](act)

            @block.vector
            def _(ve):
                q["vector"](ve)

            @block.gpsimd
            def _(pool):
                q["gpsimd"](pool)

        with ExitStack() as stack:
            r = last_sum(allocator(stack, "s_"), sem, dr, x_mid, x_work, out)
            block = stack.enter_context(nc.Block())

            @block.sync
            def _(sp):
                r["sync"](sp)

            @block.vector
            def _(ve):
                r["vector"](ve)


def rope_tables():
    half = np.arange(0, LD, 2, dtype=np.float32)
    freq = (1.0 / 10000.0 ** (half / LD)).astype(np.float32)
    t = np.arange(SEQ, dtype=np.float32)
    angle = t[:, None] * freq[None]
    angle = np.concatenate([angle, angle], -1)
    base = ((half + 0.4 * LD) / (1.4 * LD)).astype(np.float32)
    scale = base[None] ** ((t - SEQ // 2) / (WIN // 2))[:, None]
    scale = np.concatenate([scale, scale], -1)
    cos, sin = np.cos(angle), np.sin(angle) * np.where(np.arange(LD) < LD // 2, -1, 1)
    r = np.stack([cos * scale, sin * scale, cos / scale, sin / scale], 1).astype(np.float32)
    return r.reshape(TT, 128, 4, LD).transpose(1, 0, 2, 3)


def bf16_pairs(a):
    bits = (np.ascontiguousarray(a, dtype=np.float32).view(np.uint32) >> 16).astype(np.uint16)
    return np.ascontiguousarray(bits).view(np.float32)


def constants():
    p, col = np.arange(128), np.arange(SEQ)
    head_col = PADD * (p // GD) + p % GD
    c = {"rope": rope_tables(), "cen": np.eye(D, dtype=np.float32) - np.float32(1 / D)}
    i, k = p[:, None], np.arange(KEYS)[None]
    band = (i <= k) & (k <= i + WIN)
    out_of_band = [np.where(ok, 0.0, MASKED) for ok in (band & (k >= WIN), band)]
    c["mask"] = bf16_pairs(np.stack([np.stack([m, m], 1) for m in out_of_band], 1).reshape(128, 4 * KEYS))
    c["causal"] = np.where(col[None] - (SEQ - 128) > i, np.float32(MASKED), np.float32(0))
    c["hmask"] = np.where(p[:, None] // GD == np.arange(GH)[None], np.float32(GD ** -0.5), np.float32(0))
    c["place"] = np.where(head_col[:, None] == col[None], np.float32(1), np.float32(0))
    c["ones_row"] = np.where(col % PADD == GD, np.float32(1), np.float32(0))[None]
    select = np.zeros((128, NG, SELW), np.float32)
    for h in range(GH):
        g, j = divmod(h, HPG)
        select[PADD * j + np.arange(GD), g, GD * h + np.arange(GD)] = 1
        select[PADD * j + GD, g, D + h] = 1
    c["select"] = select
    c["flip"] = np.eye(128, dtype=np.float32)[::-1]
    c["lower"] = np.broadcast_to(np.tril(np.ones((GROUPS, GROUPS), np.float32), -1), (128, GROUPS, GROUPS))
    e = np.arange(3 * E)[:, None, None] % E
    c["selc"] = bf16_pairs((e == 2 * np.arange(EP)[None, :, None] + np.arange(128)[None, None, :] // EI)
                           .astype(np.float32).reshape(3 * E, EP * 128))
    return {n: np.ascontiguousarray(a, dtype=np.float32) for n, a in c.items()}, head_col


def layout(v):
    a, head_col = constants()
    a["wmod0"], a["wmod1"] = v["L0_wmod"], v["L1_wmod"]
    a["c0T"], a["c1T"] = v["L0_c"].T, v["L1_c"].T
    a["relT"] = v["L1_attn_rel_pos_table"][255:511][::-1].T
    a["WVT"] = np.zeros((D, SEQ), np.float32)
    a["WVT"][:, head_col] = v["L1_attn_WV"].T
    a["bV_row"] = a["ones_row"].copy()
    a["bV_row"][0, head_col] = v["L1_attn_bV"]
    a["WQT"], a["WKT"], a["WOT"] = v["L1_attn_WQ"].T, v["L1_attn_WK"].T, v["L1_attn_WO"].T
    a["bQK"] = np.stack([v["L1_attn_bQ"], v["L1_attn_bK"]], 1)
    a["bO"], a["gbias"] = v["L1_attn_bO"][None], v["L0_ffn_gate_bias"][None]
    a["gwT"] = v["L0_ffn_gate_w"].T
    for name, w, shared in (("wgT", "w_gate", "sh_gate"), ("wuT", "w_up", "sh_up")):
        w = v["L0_ffn_" + w].reshape(EP, 2 * EI, D)
        a[name] = np.concatenate([w, v["L0_ffn_" + shared][None]], 0).transpose(2, 0, 1)
    down = v["L0_ffn_w_down"].transpose(0, 2, 1).reshape(EP, 2 * EI, D)
    a["wdT"] = np.concatenate([down, v["L0_ffn_sh_down"].T[None]], 0).transpose(1, 0, 2)
    for name in ("Wqkv", "Wo", "W1", "W2", "b2"):
        a[name] = v["L1_ffn_" + name]
    b1 = v["L1_ffn_b1"]
    a["small"] = np.zeros((DEPTH, 128, 8), np.float32)
    for i, (at, m) in enumerate(BLK):
        a["small"][:, :m, i] = b1[:, at:at + m]
        a["small"][:, :m, 3 + i] = b1[:, DI + at:DI + at + m]
    a["small"][:, :, 6], a["small"][:, :, 7] = v["L1_ffn_ln_g"], v["L1_ffn_ln_b"]
    q, k = v["L1_ffn_q_scale"], v["L1_ffn_k_scale"]
    half = LD // 2
    a["qs"] = np.concatenate([q, q[:, half:], q[:, :half], k, k[:, half:], k[:, :half]], 1)
    return {n: np.ascontiguousarray(x) for n, x in a.items()}


def kernel(**inputs):
    import concourse.bacc as bacc
    from concourse.bass_utils import run_bass_kernel_spmd

    v = {name: np.asarray(a) for name, a in inputs.items()}
    arrays = layout(v)
    arrays["x"] = np.ascontiguousarray(v["L0_attn_x"])
    nc = bacc.Bacc("TRN2", target_bir_lowering=False, num_devices=1)
    dr = {n: nc.dram_tensor("in_" + n, a.shape, F32, kind="ExternalInput").ap() for n, a in arrays.items()}
    out = nc.dram_tensor("out", (NB, SEQ, D), F32, kind="ExternalOutput").ap()
    program(nc, dr, dr["x"], out)
    r = run_bass_kernel_spmd(nc, [{"in_" + n: a for n, a in arrays.items()}], core_ids=[0])
    return r.results[0]["out"]
```

```python
from contextlib import ExitStack

import numpy as np

import concourse.bass as bass
from concourse import mybir

F32 = mybir.dt.float32
BF16 = mybir.dt.bfloat16
ACT = mybir.ActivationFunctionType
ALU = mybir.AluOpType
AX = mybir.AxisListType

NB, SEQ, D = 8, 512, 128
TT = SEQ // 128
DEPTH = 6
LH, LD = 16, 64
INNER = LH * LD
PAIRS = LH // 2
WIN = 32
KEYS = WIN + 128
DI = D * 4 * 2 // 3
BLK = [(0, 128), (128, 128), (256, DI - 256)]
EPS = 1e-5
MASKED = -1e30


class Count:

    def __init__(self, sem, per, credit=0):
        self.sem, self.per, self.credit = sem, per, credit

    def at(self, it, n):
        return it * self.per + (self.credit + n)

    def before(self, it, n):
        return it * self.per + (self.credit + n - self.per)


GH, GD = 16, 8
HPG = 4
NG = GH // HPG
PADD = 32
SELW = D + GH
E, EI = 32, 64
EP = E // 2
GROUPS, TKG, TOPK, SCALE = 8, 4, 8, 2.5
ROWS = 6


def blocks(sb, sem, s_alone, dr, ident, identb, psum, x_in, x_mid, x_work, nbatch):
    WM = [sb(f"WM{i}", [128, 6 * D]) for i in range(2)]
    CT = sb("CT", [128, 2, NB])
    CE = sb("CE", [128, 2, NB])
    SIL = sb("SIL", [128, 2, NB])
    MODT = sb("MODT", [128, 2, 6, NB])
    GATE = sb("GATE", [128, ROWS, NB, D])
    EB = sb("EB", [GH, 640])
    BIAS1 = sb("BIAS1", [128, GH, SEQ])
    BIAS0 = sb("BIAS0", [128, SEQ])
    HM = sb("HM", [128, GH])
    WV = [sb(f"WV{i}", [128, SEQ]) for i in range(2)]
    BV = [sb(f"BV{i}", [128, SEQ]) for i in range(2)]
    SEL = sb("SEL", [128, NG, SELW])
    WQ, WK, WOT = sb("WQ", [128, D]), sb("WK", [128, D]), sb("WOT", [128, D])
    BQK = sb("BQK", [128, 2])
    BO = sb("BO", [128, D])
    GW = sb("GW", [128, E])
    GB = sb("GB", [128, E])
    LOW = sb("LOW", [128, GROUPS, GROUPS])
    WG, WU = sb("WG", [128, EP + 1, 128]), sb("WU", [128, EP + 1, 128])
    WD = sb("WD", [128, EP + 1, D])
    SELC = sb("SELC", [96, EP, 128], BF16)
    EPSC = sb("EPSC1", [128, 1])

    X = sb("X", [128, TT, D])
    ST = sb("ST", [128, TT, 6])
    MV = sb("MV", [128, TT, 2])
    SD = sb("SD", [128, TT])
    RD = sb("RD", [128, TT])
    XN = sb("XN", [128, TT, D])
    HT = sb("HT", [128, SEQ])
    QF = sb("QF", [128, SEQ])
    KF = sb("KF", [128, SEQ])
    QM = [sb(f"QM{i}", [128, SEQ]) for i in range(2)]
    VP = sb("VP", [128, TT, SEQ])
    SP_ = [sb(f"SPO{i}", [128, SEQ]) for i in range(3)]
    NBI = [sb(f"NB1{i}", [128, 1]) for i in range(3)]
    PR = [sb(f"PR1{i}", [128, SEQ]) for i in range(3)]
    NPT = 5
    PT = [sb(f"PT1{i}", [128, TT, SEQ]) for i in range(NPT)]
    MROW = PT[0][0:NB].rearrange("b t n -> b (t n)")[:, 0:12 * D].rearrange("b (l n) -> b l n", l=2)
    MR = PT[1][0:NB].rearrange("b t n -> b (t n)")[:, 0:ROWS * D].rearrange("b (r d) -> b r d", d=D)
    MS = PT[2][0:NB, 0, :].rearrange("b (r d) -> b r d", d=D)
    MA = PT[3][0:NB, 0, :].rearrange("b (r d) -> b r d", d=D)
    OG = sb("OG", [128, NG, SEQ])
    RC = sb("RC", [128, TT, GH])
    ON = sb("ON", [128, TT, D])
    OT = sb("OT1", [128, SEQ])
    TMP = sb("TMP", [128, TT, D])
    TMP2 = sb("TMP2", [128, TT, D])
    FLIP = TMP2[:, 0, :]
    names = ("ex", "ex1", "score", "sc", "mask0", "mask1", "repl", "sel", "w", "comb", "r1", "r2")
    flat = PT[3][:].rearrange("p t n -> p (t n)")
    R = {n: flat[:, TT * E * i:TT * E * (i + 1)].rearrange("p (t e) -> p t e", e=E) for i, n in enumerate(names)}
    names = ("hi1", "lo1", "hi2", "lo2", "t1", "m", "l", "t2", "gs", "rank", "gm")
    flat = PT[2][:].rearrange("p t n -> p (t n)")
    NGR = TT * GROUPS
    Gs = {n: flat[:, NGR * i:NGR * (i + 1)].rearrange("p (t g) -> p t g", g=GROUPS) for i, n in enumerate(names)}
    GT, GQ, GQ2, GQ3 = (flat[:, 512 + 256 * i:768 + 256 * i].rearrange("p (t g k) -> p t g k", g=GROUPS, k=GROUPS)
                        for i in range(4))
    V8 = sb("V8", [128, TT, 8])
    WS = sb("WS", [128, TT])
    WS1 = sb("WS1", [128, TT])
    WS2 = sb("WS2", [128, TT])
    WS3 = sb("WS3", [128, TT])
    CB = sb("CB", [128, TT, 3, E], BF16)
    CBT = sb("CBT", [96, SEQ], BF16)
    SG = [PT[0][:, i, :] for i in range(2)]
    HU = [PT[0][:, 2 + i, :] for i in range(2)]
    HI = [PT[1][:, i, :] for i in range(2)]
    YT = PT[1][:, 2, :]

    P = [psum[:, i, :] for i in range(8)]

    s_c = sem("inputs_small")
    s_ce = sem("silu_steps")
    s_mm = sem("mod_products")
    s_ms = sem("mod_steps")
    s_mw = sem("rows_written")
    s_gl = sem("gates_loaded")
    s_eb = sem("bias_row_steps")
    s_bl = sem("bias_loaded")
    s_bt = sem("bias_turned")
    s_bf = sem("bias_kept")
    s_x = sem("x_loaded")
    s_mid = sem("x_mid_stored")
    s_wk = sem("x_work_stored")
    NC = 27

    c = {}

    def add(prefix, items):
        more = 512 if prefix == "a1_" else 0
        for name, per in items:
            c[prefix + name] = Count(sem(prefix + name), per, per + more)

    UN = GH * TT
    for a in ("a0_", "a1_"):
        add(a, [("st", TT), ("mv", TT), ("sd", 1), ("rd", 1), ("xn", TT), ("xt", 1), ("ht", 1), ("qm", GH),
                ("v", TT), ("vp", TT), ("sc", UN), ("mx", UN), ("ex", UN), ("pt", UN), ("ptc", UN), ("pv", NG), ("og", NG),
                ("o", 2), ("rc", 2), ("on", 2), ("g", 1), ("x", 1)])
    add("a1_", [("qk", 2), ("qkc", 2), ("nt", 1), ("ntc", 1), ("wo", 1), ("bo", 1)])
    add("m_", [("st", TT), ("mv", TT), ("sd", 1), ("rd", 1), ("xn", TT), ("xt", 1), ("ht", 1), ("lg", 1), ("ex", 1), ("r", 1),
               ("cb", 1), ("ct", 1), ("cbt", 1), ("g", EP + 1), ("u", EP + 1), ("c", EP), ("sg", EP + 1), ("hu", EP),
               ("hi", EP + 1), ("dn", EP + 1), ("y", 1), ("yt", 1), ("z", 1), ("gz", 1), ("x", 1)])
    add("f_", [("st", TT), ("mv", TT), ("sd", 1), ("rd", 1), ("xn", TT), ("gm", 1), ("h", 1)])
    NR = 35
    c["route"] = Count(sem("route_steps"), NR, 0)

    def wait(eng, name, it, n):
        eng.wait_ge(c[name].sem, c[name].at(it, n))

    def before(eng, name, it, n):
        eng.wait_ge(c[name].sem, c[name].before(it, n))

    def done(name):
        return c[name].sem

    def credits(eng, names):
        for n in names.split():
            eng.sem_inc(c[n].sem, c[n].credit)

    xin = x_in.rearrange("b (t p) d -> b p t d", p=128)
    xmid = x_mid.rearrange("b (t p) d -> b p t d", p=128)
    xwork = x_work.rearrange("b (t p) d -> b p t d", p=128)

    def alone(eng):
        eng.sem_inc(s_alone, 1)

    def batch(x, b):
        return x[bass.ds(b, 1)].rearrange("o p t d -> p (o t) d")

    def sync_program(sp):
        small = [(WM[0][:], dr["wmod0"]), (WM[1][:], dr["wmod1"]), (CT[:, 0, :], dr["c0T"]), (CT[:, 1, :], dr["c1T"]),
                 (EB[:, 256:512], dr["relT"]), (BIAS0[:], dr["causal"]), (HM[:], dr["hmask"]),
                 (WV[0][:], dr["place"]), (WV[1][:], dr["WVT"]),
                 (BV[0][:], dr["ones_row"].broadcast_to([128, SEQ])), (BV[1][:], dr["bV_row"].broadcast_to([128, SEQ])),
                 (SEL[:], dr["select"]), (WQ[:], dr["WQT"]), (WK[:], dr["WKT"]), (WOT[:], dr["WOT"]), (BQK[:], dr["bQK"]),
                 (BO[:], dr["bO"].broadcast_to([128, D])), (GW[:], dr["gwT"]), (GB[:], dr["gbias"].broadcast_to([128, E])),
                 (LOW[:], dr["lower"]), (WG[:], dr["wgT"]), (WU[:], dr["wuT"]), (WD[:], dr["wdT"]),
                 (FLIP, dr["flip"]),
                 (SELC[:].rearrange("p a b -> p (a b)").bitcast(F32), dr["selc"])]
        assert len(small) + 2 == NC
        sp.dma_start(X[:], batch(xin, 0)).then_inc(s_x, 16)
        for dst, src in small:
            sp.dma_start(dst, src).then_inc(s_c, 16)
        sp.wait_ge(s_ms, 8)
        sp.dma_start(dr["rows"].rearrange("r b d -> b r d"), MR).then_inc(s_mw, 16)
        sp.wait_ge(s_eb, 3)
        sp.dma_start(dr["ebrow"], EB[:]).then_inc(s_mw, 16)
        sp.wait_ge(s_mw, 32)
        sp.dma_start(GATE[:].rearrange("p r b d -> p (r b d)"),
                     dr["rows"].rearrange("(o r) b d -> o (r b d)", o=1).broadcast_to([128, ROWS * NB * D])).then_inc(s_gl, 16)
        e = dr["ebrow"]
        for i in range(NG):
            src = bass.AP(e.tensor, e.offset + HPG * i * 640, [[1, 128], [640, HPG], [1, SEQ]])
            sp.dma_start(PT[i][:], src).then_inc(s_bl, 16)
        with sp.Fori(0, nbatch) as b:
            nxt = (b + 1) % nbatch
            wait(sp, "a1_x", b, 1)
            alone(sp)
            sp.dma_start(batch(xmid, b), X[:]).then_inc(s_mid, 16)
            wait(sp, "f_xn", b, TT)
            sp.wait_ge(s_mid, (b + 1) * 16)
            alone(sp)
            sp.dma_start(X[:], batch(xin, nxt)).then_inc(s_x, 16)
            wait(sp, "f_h", b, 1)
            alone(sp)
            sp.dma_start(batch(xwork, b), TMP2[:]).then_inc(s_wk, 16)
        sp.wait_ge(s_wk, nbatch * 16)
        sp.wait_ge(s_x, (nbatch + 1) * 16)

    def tensor_program(pe):
        credits(pe, " ".join(f"{a}{n}" for a in ("a0_", "a1_") for n in ("xt", "v", "sc", "pt", "pv", "o")))
        credits(pe, "a1_qk a1_nt a1_wo m_xt m_lg m_ct m_g m_u m_c m_dn m_z")
        pe.wait_ge(s_c, 16 * (NC - 2))
        pe.wait_ge(s_ce, 4)
        for i in range(2):
            for k in range(6):
                pe.matmul(P[0][:, (6 * i + k) * NB:(6 * i + k + 1) * NB], WM[i][:, 128 * k:128 * k + 128], SIL[:, i, :],
                          start=True, stop=True)
            for k in range(2):
                last = pe.matmul(P[1 + 2 * i + k][0:NB, 0:384], SIL[:, i, :], WM[i][:, 384 * k:384 * k + 384],
                                 start=True, stop=True)
        last.then_inc(s_mm, 1)
        pe.wait_ge(s_ms, 3)
        pe.wait_ge(s_bl, 16 * NG)
        for h in range(GH):
            if h >= 2:
                pe.wait_ge(s_bf, h - 1)
            pe.matmul(P[6 + h % 2], FLIP, PT[h // HPG][:, h % HPG, :], start=True, stop=True).then_inc(s_bt, 1)

        def turn(it, a, name="xt"):
            wait(pe, a + "xn", it, TT)
            for t in range(TT):
                last = pe.transpose(P[0][:, 128 * t:128 * t + 128], XN[:, t, :], ident)
            last.then_inc(done(a + name), 1)

        def attention(it, a, which):
            turn(it, a)
            wait(pe, a + "ht", it, 1)
            if which:
                for k, w in enumerate((WQ, WK)):
                    pe.matmul(P[2 + k], w[:], HT[:], start=True, stop=True).then_inc(done(a + "qk"), 1)
            for t in range(TT):
                if t >= 2:
                    wait(pe, a + "vp", it, t - 1)
                pe.matmul(P[t % 2], HT[:, 128 * t:128 * t + 128], WV[which][:], start=True, stop=True)\
                    .then_inc(done(a + "v"), 1)
            key = KF if which else HT
            LT = 2

            def score(u):
                h, qt = divmod(u, TT)
                n = 128 * (qt + 1)
                if qt == 0:
                    wait(pe, a + "qm", it, h + 1)
                    if h == 0 and which:
                        wait(pe, a + "qkc", it, 2)
                if u >= 3:
                    wait(pe, a + "mx", it, u - 2)
                pe.matmul(P[2 + u % 3][:, 0:n], QM[h % 2][:, 128 * qt:128 * qt + 128], key[:, 0:n],
                          start=True, stop=True).then_inc(done(a + "sc"), 1)

            def transposes(u):
                h, qt = divmod(u, TT)
                wait(pe, a + "ex", it, u + 1)
                if u >= 2:
                    wait(pe, a + "ptc", it, u - 1)
                else:
                    wait(pe, a + "vp", it, TT - 1 + u)
                for kt in range(qt + 1):
                    last = pe.transpose(P[5 + u % 2][:, 128 * kt:128 * kt + 128], PR[u % 3][:, 128 * kt:128 * kt + 128], ident)
                last.then_inc(done(a + "pt"), 1)

            def values(g):
                wait(pe, a + "ptc", it, (g + 1) * HPG * TT)
                wait(pe, a + "vp", it, TT)
                if g:
                    wait(pe, a + "og", it, g)
                for kt in range(TT):
                    for j in range(HPG):
                        h = HPG * g + j
                        last = pe.matmul(P[7][32 * j:32 * j + 32, 128 * kt:SEQ], VP[:, kt, PADD * h:PADD * h + PADD],
                                         PT[h % NPT][:, kt, 128 * kt:SEQ], start=(kt == 0), stop=(kt == TT - 1))
                last.then_inc(done(a + "pv"), 1)

            for u in range(UN + LT):
                if u < UN:
                    score(u)
                if u >= LT:
                    transposes(u - LT)
                    if (u - LT) % 16 == 3 and u - LT > 16:
                        values((u - LT) // 16 - 1)
            values(NG - 1)
            for t in range(TT):
                if t == 0:
                    wait(pe, a + "og", it, NG)
                for g in range(NG):
                    last = pe.matmul(P[t // 2][:, SELW * (t % 2):SELW * (t % 2) + SELW], OG[:, g, 128 * t:128 * t + 128],
                                     SEL[:, g, :], start=(g == 0), stop=(g == NG - 1))
                if t % 2:
                    last.then_inc(done(a + "o"), 1)
            if which:
                wait(pe, a + "on", it, 2)
                for t in range(TT):
                    last = pe.transpose(P[2][:, 128 * t:128 * t + 128], ON[:, t, :], ident)
                last.then_inc(done(a + "nt"), 1)
                wait(pe, a + "ntc", it, 1)
                for t in range(TT):
                    last = pe.matmul(P[3][:, 128 * t:128 * t + 128], OT[:, 128 * t:128 * t + 128], WOT[:], start=True, stop=True)
                last.then_inc(done(a + "wo"), 1)

        def experts(it):
            turn(it, "m_")
            wait(pe, "m_ht", it, 1)
            for t in range(TT):
                last = pe.matmul(P[1][:, E * t:E * t + E], HT[:, 128 * t:128 * t + 128], GW[:], start=True, stop=True)
            last.then_inc(done("m_lg"), 1)

            def up(e):
                if e >= 2:
                    wait(pe, "m_sg", it, e - 1)
                pe.matmul(P[2 + e % 2], WG[:, e, :], HT[:], start=True, stop=True).then_inc(done("m_g"), 1)
                if e >= 2:
                    wait(pe, "m_hu", it, e - 1)
                pe.matmul(P[4 + e % 2], WU[:, e, :], HT[:], start=True, stop=True).then_inc(done("m_u"), 1)

            def weight(e):
                if e:
                    wait(pe, "m_hi", it, e)
                else:
                    wait(pe, "m_cbt", it, 1)
                pe.matmul(P[6], SELC[:, e, :], CBT[:], start=True, stop=True).then_inc(done("m_c"), 1)

            def down(e):
                wait(pe, "m_hi", it, e + 1)
                pe.matmul(P[7], WD[:, e, :], HI[e % 2], start=(e == 0), stop=(e == EP)).then_inc(done("m_dn"), 1)

            up(0)
            up(1)
            wait(pe, "m_cb", it, 1)
            for t in range(TT):
                last = pe.transpose(P[1].bitcast(BF16)[0:96, 128 * t:128 * t + 128],
                                    CB[:, t].rearrange("p a e -> p (a e)"), identb)
            last.then_inc(done("m_ct"), 1)
            for e in range(EP + 1):
                if e < EP:
                    weight(e)
                if 2 <= e + 1 <= EP:
                    up(e + 1)
                if e >= 1:
                    down(e - 1)
            down(EP)
            wait(pe, "m_yt", it, 1)
            for t in range(TT):
                last = pe.transpose(P[0][:, 128 * t:128 * t + 128], YT[:, 128 * t:128 * t + 128], ident)
            last.then_inc(done("m_z"), 1)

        with pe.Fori(0, nbatch) as it:
            attention(it, "a0_", 0)
            experts(it)
            attention(it, "a1_", 1)

    def scalar_program(act):
        credits(act, " ".join(f"{a}{n}" for a in ("a0_", "a1_") for n in ("ht", "ex", "og")))
        credits(act, "a0_sd a1_sd m_sd f_sd a1_qkc a1_ntc m_ht m_ex m_cbt m_sg m_yt")
        act.wait_ge(s_c, 16 * (NC - 2))
        act.wait_ge(s_eb, 1)
        act.activation(CE[:], CT[:], ACT.Exp, scale=-1.0).then_inc(s_ce, 1)
        act.wait_ge(s_ms, 3)

        def deviation(it, a):
            wait(act, a + "mv", it, TT)
            act.activation(SD[:], MV[:, :, 1], ACT.Sqrt, bias=EPSC[:]).then_inc(done(a + "sd"), 1)

        def modulated(it, a, layer, k):
            wait(act, a + "xt", it, 1)
            act.activation(HT[:], P[0], ACT.Identity, bias=MODT[:, layer, k, bass.ds(it, 1)],
                           scale=MODT[:, layer, k + 1, bass.ds(it, 1)]).then_inc(done(a + "ht"), 1)

        def attention(it, a, which):
            deviation(it, a)
            modulated(it, a, which, 0)
            if which:
                for k, dst in enumerate((QF, KF)):
                    wait(act, a + "qk", it, k + 1)
                    act.activation(dst[:], P[2 + k], ACT.Identity, bias=BQK[:, k:k + 1]).then_inc(done(a + "qkc"), 1)
            LC = 2

            def exps(u):
                h, qt = divmod(u, TT)
                n = 128 * (qt + 1)
                wait(act, a + "mx", it, u + 1)
                if u >= 3:
                    wait(act, a + "pt", it, u - 2)
                act.activation(PR[u % 3][:, 0:n], SP_[u % 3][:, 0:n], ACT.Exp, bias=NBI[u % 3][:], scale=-1.0)\
                    .then_inc(done(a + "ex"), 1)

            for u in range(UN):
                exps(u)
                if (u - 4) % 16 == 7 and u > 20:
                    out_copy(act, it, a, (u - 4) // 16 - 1)
            out_copy(act, it, a, NG - 1)
            if which:
                wait(act, a + "nt", it, 1)
                act.activation(OT[:], P[2], ACT.Copy).then_inc(done(a + "ntc"), 1)

        def out_copy(act, it, a, g):
            wait(act, a + "pv", it, g + 1)
            if g == 0:
                pass
            act.activation(OG[:, g, :], P[7], ACT.Copy).then_inc(done(a + "og"), 1)

        def experts(it):
            deviation(it, "m_")
            modulated(it, "m_", 0, 3)
            wait(act, "m_lg", it, 1)
            act.activation(R["ex"].rearrange("p t e -> p (t e)"), P[1][:, 0:TT * E], ACT.Exp, scale=-1.0)\
                .then_inc(done("m_ex"), 1)
            for e in range(EP + 1):
                wait(act, "m_g", it, e + 1)
                if e >= 2:
                    wait(act, "m_hu", it, e - 1)
                act.activation(SG[e % 2], P[2 + e % 2], ACT.Silu).then_inc(done("m_sg"), 1)
                if e == 0:
                    wait(act, "m_ct", it, 1)
                    act.activation(CBT[:], P[1].bitcast(BF16)[0:96, 0:SEQ], ACT.Copy).then_inc(done("m_cbt"), 1)
            wait(act, "m_dn", it, EP + 1)
            act.activation(YT, P[7], ACT.Copy).then_inc(done("m_yt"), 1)

        with act.Fori(0, nbatch) as it:
            attention(it, "a0_", 0)
            experts(it)
            attention(it, "a1_", 1)
            deviation(it, "f_")

    def vector_program(ve):
        credits(ve, " ".join(f"{a}{n}" for a in ("a0_", "a1_", "m_", "f_") for n in ("st", "mv", "rd", "xn")))
        credits(ve, " ".join(f"{a}{n}" for a in ("a0_", "a1_") for n in ("vp", "mx", "ptc", "rc", "on", "g", "x")))
        credits(ve, "a1_bo m_r m_cb m_hu m_hi m_gz m_x f_gm f_h")
        ve.memset(EPSC[:], EPS).then_inc(s_eb, 1)
        ve.wait_ge(s_c, 16 * (NC - 2))
        ve.tensor_copy(EB[:, 0:256], EB[:, 256:257].broadcast_to([GH, 256])).then_inc(s_eb, 1)
        ve.memset(EB[:, 512:640], -1e30).then_inc(s_eb, 1)
        ve.wait_ge(s_ce, 1)
        ve.tensor_scalar(CE[:], CE[:], 1.0, None, ALU.add).then_inc(s_ce, 1)
        ve.wait_ge(s_ce, 2)
        ve.reciprocal(CE[:], CE[:]).then_inc(s_ce, 1)
        ve.wait_ge(s_ce, 3)
        ve.tensor_tensor(SIL[:], CE[:], CT[:], ALU.mult).then_inc(s_ce, 1)
        ve.wait_ge(s_mm, 1)
        ve.tensor_copy(MODT[:].rearrange("p l k b -> p (l k b)"), P[0][:, 0:12 * NB]).then_inc(s_ms, 1)
        ve.wait_ge(s_ms, 1)
        for k in (1, 4):
            ve.tensor_scalar(MODT[:, :, k, :], MODT[:, :, k, :], 1.0, None, ALU.add).then_inc(s_ms, 1)
        for i in range(2):
            for k in range(2):
                last = ve.tensor_copy(MROW[:, i, 384 * k:384 * k + 384], P[1 + 2 * i + k][0:NB, 0:384])
        last.then_inc(s_ms, 1)
        ve.wait_ge(s_ms, 4)
        g = MROW.rearrange("b l (k d) -> b l k d", d=D)[:, :, 2:6:3, :]
        ms, ma, mr = (t.rearrange("b (l k) d -> b l k d", l=2) for t in (MS, MA, MR[:, 0:4, :]))
        ve.tensor_scalar(ms, g, 0.0, 2.0, ALU.is_ge, ALU.mult).then_inc(s_ms, 1)
        ve.scalar_tensor_tensor(ma, g, -1.0, g, ALU.mult, ALU.max).then_inc(s_ms, 1)
        ve.wait_ge(s_ms, 6)
        ve.tensor_scalar(ma, ma, 0.25, None, ALU.max).then_inc(s_ms, 1)
        ve.tensor_scalar(MR[:, 4, :], MROW[:, 1, 4 * D:5 * D], 1.0, None, ALU.add)
        ve.tensor_copy(MR[:, 5, :], MROW[:, 1, 3 * D:4 * D])
        ve.wait_ge(s_ms, 7)
        ve.scalar_tensor_tensor(mr, ms, -1.0, ma, ALU.add, ALU.mult).then_inc(s_ms, 1)

        def norm(it, a, ready):
            ready()
            for t in range(TT):
                ve.bn_stats(ST[:, t, :], X[:, t, :]).then_inc(done(a + "st"), 1)
            for t in range(TT):
                wait(ve, a + "st", it, t + 1)
                alone(ve)
                ve.bn_aggr(MV[:, t, :], ST[:, t, :]).then_inc(done(a + "mv"), 1)
            wait(ve, a + "sd", it, 1)
            ve.reciprocal(RD[:], SD[:]).then_inc(done(a + "rd"), 1)
            wait(ve, a + "rd", it, 1)
            for t in range(TT):
                ve.tensor_scalar(XN[:, t, :], X[:, t, :], MV[:, t, 0:1], RD[:, t:t + 1], ALU.subtract, ALU.mult)\
                    .then_inc(done(a + "xn"), 1)

        def attention(it, a, which, ready):
            norm(it, a, ready)
            for t in range(TT):
                wait(ve, a + "v", it, t + 1)
                ve.tensor_tensor(VP[:, t, :], P[t % 2], BV[which][:], ALU.add).then_inc(done(a + "vp"), 1)

            def maxima(u):
                h, qt = divmod(u, TT)
                n = 128 * (qt + 1)
                wait(ve, a + "sc", it, u + 1)
                if u >= 3:
                    wait(ve, a + "ex", it, u - 2)
                alone(ve)
                bias = BIAS1[:, h, SEQ - n:SEQ] if which else BIAS0[:, SEQ - n:SEQ]
                ve.tensor_tensor_reduce(out=SP_[u % 3][:, 0:n], in0=P[2 + u % 3][:, 0:n], in1=bias, scale=-1.0,
                                        scalar=3e38, op0=ALU.add, op1=ALU.min, accum_out=NBI[u % 3][:])\
                    .then_inc(done(a + "mx"), 1)

            def copies(u):
                h, qt = divmod(u, TT)
                wait(ve, a + "pt", it, u + 1)
                if qt == 0 and h >= NPT:
                    wait(ve, a + "pv", it, (h - NPT) // HPG + 1)
                ve.tensor_copy(PT[h % NPT][:, 0:qt + 1, 128 * qt:128 * qt + 128],
                               P[5 + u % 2][:, 0:128 * (qt + 1)].rearrange("p (k q) -> p k q", q=128))\
                    .then_inc(done(a + "ptc"), 1)

            LC = 3
            for u in range(UN + LC):
                if u < UN:
                    maxima(u)
                if u >= LC:
                    copies(u - LC)
            for k in range(2):
                wait(ve, a + "o", it, k + 1)
                o = P[k][:, 0:2 * SELW].rearrange("p (t w) -> p t w", w=SELW)
                ve.reciprocal(RC[:, 2 * k:2 * k + 2, :], o[:, :, D:SELW]).then_inc(done(a + "rc"), 1)
                wait(ve, a + "rc", it, k + 1)
                for t in range(2):
                    last = ve.tensor_tensor(ON[:, 2 * k + t, :].rearrange("p (h d) -> p h d", d=GD),
                                            o[:, t, 0:D].rearrange("p (h d) -> p h d", d=GD),
                                            RC[:, 2 * k + t, :].unsqueeze(2).broadcast_to([128, GH, GD]), ALU.mult)
                last.then_inc(done(a + "on"), 1)
            src = ON
            if which:
                wait(ve, a + "wo", it, 1)
                ve.tensor_tensor(TMP[:], P[3].rearrange("p (t d) -> p t d", d=D), BO[:].unsqueeze(1).broadcast_to([128, TT, D]),
                                 ALU.add).then_inc(done(a + "bo"), 1)
                wait(ve, a + "bo", it, 1)
                src = TMP
            else:
                wait(ve, a + "on", it, 2)
            gated(it, a, src[:], 2 * which)

        def gate(r, it):
            return GATE[:, r, bass.ds(it, 1), :].broadcast_to([128, TT, D])

        def gated(it, a, src, r, names=("g", "x")):
            ve.tensor_tensor(TMP2[:], src, gate(r, it), ALU.mult).then_inc(done(a + names[0]), 1)
            wait(ve, a + names[0], it, 1)
            ve.tensor_tensor(X[:], X[:], TMP2[:], ALU.add).then_inc(done(a + names[1]), 1)

        def route(it):
            n = [0]

            def step(ins):
                n[0] += 1
                ins.then_inc(done("route"), 1)

            def sync():
                wait(ve, "route", it, n[0])

            tt, ts = ve.tensor_tensor, ve.tensor_scalar
            wait(ve, "m_ex", it, 1)
            step(ts(R["ex1"], R["ex"], 1.0, None, ALU.add))
            sync()
            step(ve.reciprocal(R["score"], R["ex1"]))
            sync()
            step(tt(R["sc"], R["score"], GB[:].unsqueeze(1).broadcast_to([128, TT, E]), ALU.add))
            sync()
            v = R["sc"].rearrange("p t (g k) -> p t g k", k=4)
            for dst, i, op in (("hi1", 0, ALU.max), ("lo1", 0, ALU.min), ("hi2", 2, ALU.max), ("lo2", 2, ALU.min)):
                step(tt(Gs[dst], v[:, :, :, i], v[:, :, :, i + 1], op))
            sync()
            for dst, x, y, op in (("t1", "hi1", "hi2", ALU.max), ("m", "hi1", "hi2", ALU.min), ("l", "lo1", "lo2", ALU.max)):
                step(tt(Gs[dst], Gs[x], Gs[y], op))
            sync()
            step(tt(Gs["t2"], Gs["m"], Gs["l"], ALU.max))
            sync()
            step(tt(Gs["gs"], Gs["t1"], Gs["t2"], ALU.add))
            sync()
            other = Gs["gs"].unsqueeze(2).broadcast_to([128, TT, GROUPS, GROUPS])
            own = Gs["gs"].unsqueeze(3).broadcast_to([128, TT, GROUPS, GROUPS])
            step(tt(GT, other, own, ALU.is_gt))
            step(tt(GQ, other, own, ALU.is_equal))
            sync()
            step(tt(GQ2, GQ, LOW[:].unsqueeze(1).broadcast_to([128, TT, GROUPS, GROUPS]), ALU.mult))
            sync()
            step(tt(GQ3, GT, GQ2, ALU.add))
            sync()
            step(ve.tensor_reduce(Gs["rank"], GQ3, AX.X, ALU.add))
            sync()
            step(ts(Gs["gm"], Gs["rank"], TKG - 0.5, None, ALU.is_lt))
            sync()
            step(tt(R["mask0"].rearrange("p t (g k) -> p t g k", k=4), v,
                    Gs["gm"].unsqueeze(3).broadcast_to([128, TT, GROUPS, 4]), ALU.mult))
            sync()
            step(ts(R["mask1"], R["mask0"], 0.0, None, ALU.add))
            sync()
            alone(ve)
            for t in range(TT):
                step(ve.max(V8[:, t, :], R["mask1"][:, t, :]))
            sync()
            alone(ve)
            for t in range(TT):
                step(ve.match_replace(R["repl"][:, t, :], V8[:, t, :], R["mask1"][:, t, :], -1e30))
            sync()
            step(ts(R["sel"], R["repl"], -5e29, None, ALU.is_lt))
            sync()
            step(tt(R["w"], R["sel"], R["score"], ALU.mult))
            sync()
            step(ve.tensor_reduce(WS[:], R["w"], AX.X, ALU.add))
            sync()
            step(ts(WS1[:], WS[:], 1e-20, None, ALU.add))
            sync()
            step(ve.reciprocal(WS2[:], WS1[:]))
            sync()
            step(ts(WS3[:], WS2[:], SCALE, None, ALU.mult))
            sync()
            step(tt(R["comb"], R["w"], WS3[:].unsqueeze(2).broadcast_to([128, TT, E]), ALU.mult))
            sync()
            assert n[0] == NR, n[0]
            ve.tensor_copy(CB[:, :, 0, :], R["comb"]).then_inc(s_split, 1)
            ve.wait_ge(s_split, it * 4 + 1)
            tt(R["r1"], R["comb"], CB[:, :, 0, :], ALU.subtract).then_inc(s_split, 1)
            ve.wait_ge(s_split, it * 4 + 2)
            ve.tensor_copy(CB[:, :, 1, :], R["r1"]).then_inc(s_split, 1)
            ve.wait_ge(s_split, it * 4 + 3)
            tt(R["r2"], R["r1"], CB[:, :, 1, :], ALU.subtract).then_inc(s_split, 1)
            ve.wait_ge(s_split, it * 4 + 4)
            ve.tensor_copy(CB[:, :, 2, :], R["r2"]).then_inc(done("m_cb"), 1)

        def experts(it):
            norm(it, "m_", lambda: wait(ve, "a0_x", it, 1))
            route(it)
            for e in range(EP + 1):
                wait(ve, "m_sg", it, e + 1)
                wait(ve, "m_u", it, e + 1)
                if e >= 2:
                    wait(ve, "m_dn", it, e - 1)
                dst = HU if e < EP else HI
                ve.tensor_tensor(dst[e % 2], P[4 + e % 2], SG[e % 2], ALU.mult)\
                    .then_inc(done("m_hu" if e < EP else "m_hi"), 1)
                if e < EP:
                    wait(ve, "m_hu", it, e + 1)
                    wait(ve, "m_c", it, e + 1)
                    ve.tensor_tensor(HI[e % 2], P[6], HU[e % 2], ALU.mult).then_inc(done("m_hi"), 1)
            wait(ve, "m_z", it, 1)
            gated(it, "m_", P[0].rearrange("p (t d) -> p t d", d=D), 1, ("gz", "x"))

        def modulated(it):
            norm(it, "f_", lambda: wait(ve, "a1_x", it, 1))
            wait(ve, "f_xn", it, TT)
            ve.tensor_tensor(TMP[:], XN[:], gate(4, it), ALU.mult).then_inc(done("f_gm"), 1)
            wait(ve, "f_gm", it, 1)
            ve.tensor_tensor(TMP2[:], TMP[:], gate(5, it), ALU.add).then_inc(done("f_h"), 1)

        for h in range(GH):
            ve.wait_ge(s_bt, h + 1)
            ve.tensor_copy(BIAS1[:, h, :], P[6 + h % 2]).then_inc(s_bf, 1)
        ve.wait_ge(s_gl, 16)
        ve.wait_ge(s_bf, GH)
        with ve.Fori(0, nbatch) as it:
            ve.wait_ge(s_wk, it * 16)
            attention(it, "a0_", 0, lambda: ve.wait_ge(s_x, (it + 1) * 16))
            experts(it)
            attention(it, "a1_", 1, lambda: wait(ve, "m_x", it, 1))
            modulated(it)

    def gpsimd_program(pool):
        credits(pool, "a0_qm a1_qm")
        pool.wait_ge(s_c, 16 * (NC - 2))

        def masked(it, a, which):
            wait(pool, a + "qkc" if which else a + "ht", it, 1)
            q = QF if which else HT
            for h in range(GH):
                if h >= 2:
                    wait(pool, a + "sc", it, TT * (h - 1))
                alone(pool)
                pool.tensor_scalar(QM[h % 2][:], q[:], HM[:, h:h + 1], 0.0, ALU.mult, ALU.add).then_inc(done(a + "qm"), 1)

        with pool.Fori(0, nbatch) as it:
            masked(it, "a0_", 0)
            masked(it, "a1_", 1)

    s_split = sem("split_steps")
    return dict(sync=sync_program, tensor=tensor_program, scalar=scalar_program, vector=vector_program, gpsimd=gpsimd_program)


def local_layers(sb, sem, s_alone, dr, ident, identb, psum, x_out, nlayers, nbatch):
    PS = psum
    SHARED = [PS[:, i, :] for i in range(3)]
    TRP = PS[:, 3, :]
    SB = [PS[:, 4, :], PS[:, 5, :]]
    OV = [PS[:, 6, :], PS[:, 7, :]]
    CX = OV[0]
    GATE = [SB[1], OV[0], SB[1]]
    LIN = [SB[0], TRP, SB[0]]
    FO = OV[1]

    WQKV = [sb(f"WQKV{i}", [128, 3 * INNER]) for i in range(2)]
    WO = [sb(f"WO{i}", [128, PAIRS, D]) for i in range(2)]
    W1 = [sb(f"W1{i}", [128, 2 * DI]) for i in range(2)]
    W2 = [sb(f"W2{i}", [128, 3, D]) for i in range(2)]
    SM = [sb(f"SM{i}", [128, 8]) for i in range(2)]
    B2 = [sb(f"B2{i}", [128, D]) for i in range(2)]
    QS = [sb(f"QS{i}", [128, 4, LD]) for i in range(2)]
    ROPE0 = sb("ROPE0", [128, TT, 4, LD])
    ROPE = sb("ROPE", [128, TT, 4, LD])
    MASKB = sb("MASKB", [128, 2, 2, KEYS], BF16)
    CEN = sb("CEN", [128, 128])
    AVG = sb("AVG", [128, 128])
    EPSC = sb("EPSC", [128, 1])

    XA = sb("XA", [128, TT, D])
    XR = sb("XR", [128, TT, D])
    XO = sb("XO", [128, TT, D])
    XB = sb("XB", [128, TT, D])
    XS = sb("XS", [128, SEQ + 1])
    XF = sb("XF", [128, SEQ + 1])
    RAW = [sb(f"RAW{i}", [128, 512]) for i in range(3)]
    SQR = [sb(f"SQR{i}", [128, 512]) for i in range(2)]
    T1 = [sb(f"T1{i}", [128, 512]) for i in range(2)]
    T2 = [sb(f"T2{i}", [128, 512]) for i in range(2)]
    SS = sb("SS", [128, TT, 2 * LH])
    RN = sb("RN", [128, TT, 2 * LH])
    ROT = sb("ROT", [128, TT, 4, 512])
    V = sb("V", [128, TT, INNER])
    QT = [sb(f"QT{i}", [128, PAIRS, 128]) for i in range(2)]
    KD = [sb(f"KD{i}", [128, PAIRS, 2, KEYS]) for i in range(2)]
    NP = 4
    PR = [sb(f"PR{i}", [128, 2, KEYS]) for i in range(NP)]
    MX = [sb(f"MX{i}", [128, 2]) for i in range(NP)]
    NBI = [sb(f"NBI{i}", [128, 2]) for i in range(NP)]
    SU = [sb(f"SU{i}", [128, 2]) for i in range(NP)]
    RS = [sb(f"RS{i}", [128, 2]) for i in range(NP)]
    PT = [sb(f"PT{i}", [128, 2, 128]) for i in range(2)]
    PTE = [sb(f"PTE{i}", [128, 2, WIN]) for i in range(2)]
    OT = [sb(f"OT{i}", [128, PAIRS, 128]) for i in range(2)]
    SQF = sb("SQF", [128, TT, D])
    VAR = sb("VAR", [128, TT])
    STD = sb("STD", [128, TT])
    RSTD = sb("RSTD", [128, TT])
    XN0 = sb("XN0", [128, TT, D])
    WARM = sb("WARM", [128, 1])
    XN1 = sb("XN1", [128, SEQ])
    GE = [sb(f"GE{i}", [128, SEQ]) for i in range(2)]
    HID = sb("HID", [128, 3, SEQ])

    UN = TT * PAIRS

    AHEAD = {0: [(0, 0)], 2: [(0, 1)], 4: [(0, 2)], 7: [(0, 3)], 9: [(1, 0)], 11: [(1, 1)], 14: [(1, 2)],
             16: [(1, 3)], 18: [(2, 0)], 21: [(2, 1)], 22: [(0, 4)], 23: [(2, 2)], 24: [(0, 5)], 25: [(2, 3)],
             28: [(3, 0)], 29: [(1, 4)], 30: [(3, 1)], 31: [(1, 5)], 32: [(3, 2)], 35: [(3, 3)]}
    FILL = [(j, k) for j in (TT - 2, TT - 1) for k in (4, 5)]
    ORDER = [a for u in range(UN + 4) for a in AHEAD.get(u, [])] + FILL
    TURN = {a: n for n, a in enumerate(ORDER)}
    LT, LV = 3, 4

    TURNS = []
    for u in range(UN + LV):
        j, p = divmod(u, PAIRS)
        if 2 <= p < 6 and j + 1 < TT:
            TURNS.append(("qk", j + 1, p - 2))
        TURNS += [("project", *a) for a in AHEAD.get(u, [])]
        if (u - LV) % PAIRS == 2 and u - LV > PAIRS:
            TURNS.append(("out", (u - LV) // PAIRS - 1, 0))
    TURNS += [("out", TT - 1, 0)] + [("project", *a) for a in FILL] + [("qk", 0, k) for k in range(4)] + [("x", 0, 0)]
    assert len(TURNS) % 3 == 0

    def bank(*turn):
        return SHARED[TURNS.index(turn) % 3]
    s_tab = sem("local_tables")
    s_w = [sem(f"local_weights{i}") for i in range(2)]
    NW = 10
    s_xa = sem("xa_loaded")
    s_xr = sem("xr_loaded")
    s_st = sem("x_stored")
    s_avg = sem("average_matrix_ready")
    s_fill = sem("local_buffers_filled")
    c = {}
    for name, per in [
        ("xt", 1), ("xs", 2), ("qkv", 6 * TT), ("raw", 6 * TT), ("sqr", 4 * TT), ("ssum", 4 * TT),
        ("t1", 4 * TT), ("t2", 4 * TT), ("rot", 4 * TT), ("norm", 1), ("nmax", 1), ("rn", 1), ("rnq", 1), ("kn", TT),
        ("qkt", 4 * TT), ("qkc", 4 * TT), ("kprev", 2 * (TT - 1)),
        ("sc", UN), ("mx", UN), ("nb", UN), ("ex", UN), ("rs", UN), ("pn", UN), ("pt", UN),
        ("ptm", UN), ("pte", UN - PAIRS), ("ov", 2 * TT), ("ovc", 2 * TT), ("wo", TT), ("res", TT),
        ("ft", 1), ("xf", 2), ("cen", 1), ("sqf", 1), ("xnt", 1), ("std", 1), ("rstd", 1), ("xn0", 1), ("xn1", 1),
        ("w1", 6), ("ge", 3), ("hid", 3), ("w2", 1), ("xb", 1), ("xo", 1),
    ]:
        c[name] = Count(sem(f"l_{name}"), per, per)
    s_rope = Count(sem("rope_scaled"), 1)

    def alone(eng):
        eng.sem_inc(s_alone, 1)

    def credits(eng, names):
        for n in names.split():
            eng.sem_inc(c[n].sem, c[n].per)

    def wait(eng, name, it, n):
        eng.wait_ge(c[name].sem, c[name].at(it, n))

    def wait_before(eng, name, it, n):
        eng.wait_ge(c[name].sem, c[name].before(it, n))

    def earlier(eng, name, it, n):
        eng.wait_ge(c[name].sem, c[name].at(it, n))

    def bank_free(eng, it, *turn):
        i = TURNS.index(turn) - 3
        what, j, k = TURNS[i]
        of = it if i >= 0 else it - 1
        if what == "qk":
            wait(eng, "qkc", of if j else of + 1, 4 * j + k + 1)
        elif what == "x":
            wait(eng, "xs", of + 2, 2)
        elif what == "project":
            wait(eng, "raw", of + 1, TURN[j, k] + 1)
        else:
            wait(eng, "res", of, j + 1)

    def layers(eng, next_weights, body):
        with eng.Fori(0, nlayers // 2) as lp:
            for par in range(2):
                alone(eng)
                with eng.Fori(0, nbatch - 1) as b:
                    body(lp * (2 * nbatch) + (b + par * nbatch), par, par)
                next_weights(lp, par)
                alone(eng)
                body(lp * (2 * nbatch) + (nbatch - 1 + par * nbatch), par, 1 - par)

    def weights_loaded(eng, lp, par):
        eng.wait_ge(s_w[1 - par], (lp + (1 + par)) * (16 * NW))

    def batch(x, b):
        return x[bass.ds(b, 1)].rearrange("o p t d -> p (o t) d")

    xout = x_out.rearrange("b (t p) d -> b p t d", p=128)

    def sync_program(sp):
        sp.dma_start(ROPE0[:], dr["rope"]).then_inc(s_tab, 16)
        sp.dma_start(MASKB[:].rearrange("p a b c -> p (a b c)").bitcast(F32), dr["mask"]).then_inc(s_tab, 16)
        sp.dma_start(CEN[:], dr["cen"]).then_inc(s_tab, 16)

        def weights(layer, par):
            for dst, src in [
                (WQKV[par][:], dr["Wqkv"][bass.ds(layer, 1), :, :].rearrange("o k n -> k (o n)")),
                (WO[par][:], dr["Wo"][bass.ds(layer, 1), :, :].rearrange("o (a p) n -> p (o a) n", p=128)),
                (W1[par][:], dr["W1"][bass.ds(layer, 1), :, :].rearrange("o k n -> k (o n)")),
                (W2[par][:, 0:2, :], dr["W2"][bass.ds(layer, 1), 0:256, :].rearrange("o (a p) n -> p (o a) n", p=128)),
                (W2[par][0:DI - 256, 2, :], dr["W2"][bass.ds(layer, 1), 256:DI, :].rearrange("o p n -> p (o n)")),
                (SM[par][:], dr["small"][bass.ds(layer, 1), :, :].rearrange("o k n -> k (o n)")),
                (B2[par][:], dr["b2"][bass.ds(layer, 1), :].broadcast_to([128, D])),
                (QS[par][:, 0, :], dr["qs"][bass.ds(layer, 1), 0:LD].broadcast_to([128, LD])),
                (QS[par][:, 1:3, :].rearrange("p a d -> p (a d)"), dr["qs"][bass.ds(layer, 1), LD:3 * LD].broadcast_to([128, 2 * LD])),
                (QS[par][:, 3, :], dr["qs"][bass.ds(layer, 1), 3 * LD:4 * LD].broadcast_to([128, LD])),
            ]:
                sp.dma_start(dst, src).then_inc(s_w[par], 16)

        sp.sem_inc(s_st, 16 * (nbatch - 1))
        weights(0, 0)
        sp.dma_start(XA[:], batch(xout, 0)).then_inc(s_xa, 16)
        sp.dma_start(XR[:], batch(xout, 0)).then_inc(s_xr, 16)
        for i in range(2):
            wait(sp, "xt", i, 1)
            sp.dma_start(XA[:], batch(xout, i + 1)).then_inc(s_xa, 16)

        def body(it, b):
            wait(sp, "ft", it, 1)
            wait(sp, "xb", it, 1)
            alone(sp)
            sp.dma_start(XR[:], batch(xout, (b + 1) % nbatch)).then_inc(s_xr, 16)
            wait(sp, "xt", it + 2, 1)
            sp.wait_ge(s_st, (it + 3) * 16)
            alone(sp)
            sp.dma_start(XA[:], batch(xout, (b + 3) % nbatch)).then_inc(s_xa, 16)
            wait(sp, "xo", it, 1)
            alone(sp)
            sp.dma_start(batch(xout, b), XO[:]).then_inc(s_st, 16)

        with sp.Fori(0, nlayers // 2) as lp:
            for par in range(2):
                first = lp * (2 * nbatch) + par * nbatch
                for name in ("wo", "xo"):
                    wait_before(sp, name, first, c[name].per)
                    alone(sp)
                weights((lp * 2 + (1 + par)) % nlayers if par else lp * 2 + 1, 1 - par)
                with sp.Fori(0, nbatch - 1) as b:
                    body(lp * (2 * nbatch) + (b + par * nbatch), b)
                body(lp * (2 * nbatch) + (nbatch - 1 + par * nbatch), nbatch - 1)
        sp.wait_ge(s_st, 16 * (nlayers * nbatch + nbatch - 1))
        sp.wait_ge(s_xa, 16 * (nlayers * nbatch + 3))
        sp.wait_ge(s_xr, 16 * (nlayers * nbatch + 1))
        sp.wait_ge(s_w[0], 16 * NW * (nlayers // 2 + 1))

    def tensor_program(pe):
        credits(pe, "xt qkv qkt sc pt ov wo ft cen xnt w1 w2")
        pe.wait_ge(s_avg, 1)
        pe.wait_ge(s_fill, 5)
        pe.wait_ge(s_tab, 48)

        def transpose_x(it):
            pe.wait_ge(s_xa, (it + 1) * 16)
            for j in range(TT):
                last = pe.transpose(bank("x", 0, 0)[:, 128 * j:128 * j + 128], XA[:, j, :], ident)
            last.then_inc(c["xt"].sem, 1)

        def project(it, par, j, k):
            n = TURN[j, k]
            if n == 0:
                wait(pe, "xs", it, 2)
            pe.matmul(bank("project", j, k), XS[:, 128 * j:128 * j + 128], WQKV[par][:, 512 * k:512 * k + 512],
                      start=True, stop=True).then_inc(c["qkv"].sem, 1)

        def project_ahead(it, ahead, turns):
            for j, k in turns:
                bank_free(pe, it, "project", j, k)
                project(it + 1, ahead, j, k)

        def transpose_qk(it, j, k):
            turn = it
            if j == 0:
                it = it + 1
            if k == 0:
                wait(pe, "rot", it, 4 * j + 4)
            if k == 2:
                wait(pe, "kn", it, j + 1)
            bank_free(pe, turn, "qk", j, k)
            for i in range(4):
                last = pe.transpose(bank("qk", j, k)[:, 128 * i:128 * i + 128], ROT[:, j, k, 128 * i:128 * i + 128],
                                    ident)
            last.then_inc(c["qkt"].sem, 1)

        def scores(it, u):
            j, p = divmod(u, PAIRS)
            if p == 0:
                wait(pe, "qkc", it, 4 * (j + 1))
                if j:
                    wait(pe, "kprev", it, 2 * j)
            if u >= 2:
                wait(pe, "ex", it, u - 1)
            elif u == 0:
                wait_before(pe, "hid", it, 3)
            else:
                wait_before(pe, "ge", it, 3)
            pe.matmul(SB[u % 2][:, 0:2 * KEYS], identb, MASKB[:, min(j, 1)].rearrange("p a c -> p (a c)"),
                      start=True, stop=False)
            pe.matmul(SB[u % 2][:, 0:2 * KEYS], QT[j % 2][:, p, :],
                      KD[j % 2][:, p].rearrange("p a c -> p (a c)"),
                      start=False, stop=True).then_inc(c["sc"].sem, 1)

        def transpose_p(it, u):
            j, p = divmod(u, PAIRS)
            wait(pe, "pn", it, u + 1)
            earlier(pe, "ptm", it, u)
            if u > PAIRS:
                wait(pe, "pte", it, u - PAIRS)
            elif u == 0:
                wait_before(pe, "hid", it, 2)
            for hh in range(2):
                last = pe.transpose(TRP[:, 128 * hh:128 * hh + 128], PR[u % NP][:, hh, WIN:KEYS], ident)
            if j:
                for hh in range(2):
                    last = pe.transpose(TRP[0:WIN, 256 + WIN * hh:256 + WIN * hh + WIN],
                                        PR[u % NP][0:WIN, hh, 0:WIN], ident[0:WIN, 0:WIN])
            last.then_inc(c["pt"].sem, 1)

        def values(it, u):
            j, p = divmod(u, PAIRS)
            wait(pe, "ptm", it, u + 1)
            if j:
                wait(pe, "pte", it, u + 1 - PAIRS)
            if u == 0:
                wait(pe, "raw", it, 6 * TT)
            if p % 4 == 0:
                earlier(pe, "ovc", it, u // 4 - 1)
            if u == 0:
                wait_before(pe, "ge", it, 2)
            if u == 4:
                wait_before(pe, "xo", it, 1)
            for hh in range(2):
                rows = slice(64 * hh, 64 * hh + 64)
                col = 128 * (p % 4)
                h = 2 * p + hh
                last = pe.matmul(OV[u // 4 % 2][rows, col:col + 128], V[:, j, 64 * h:64 * h + 64], PT[u % 2][:, hh, :],
                                 start=True, stop=(j == 0))
                if j:
                    last = pe.matmul(OV[u // 4 % 2][rows, col:col + WIN], V[96:128, j - 1, 64 * h:64 * h + 64],
                                     PTE[u % 2][96:128, hh, :], start=False, stop=True)
            if p % 4 == 3:
                last.then_inc(c["ov"].sem, 1)

        def project_out(it, par, j):
            wait(pe, "ovc", it, 2 * (j + 1))
            bank_free(pe, it, "out", j, 0)
            for p in range(PAIRS):
                last = pe.matmul(bank("out", j, 0)[:, 0:D], OT[j % 2][:, p, :], WO[par][:, p, :],
                                 start=(p == 0), stop=(p == PAIRS - 1))
            last.then_inc(c["wo"].sem, 1)

        def feed_forward(it, par, ahead):
            wait(pe, "res", it, TT)
            wait(pe, "ptm", it, UN)
            wait(pe, "pte", it, UN - PAIRS)
            for j in range(TT):
                last = pe.transpose(TRP[:, 128 * j:128 * j + 128], XR[:, j, :], ident)
            last.then_inc(c["ft"].sem, 1)
            project_ahead(it, ahead, FILL[0:1])
            wait(pe, "xf", it, 2)
            for j in range(TT):
                last = pe.matmul(CX[:, 128 * j:128 * j + 128], XF[:, 128 * j:128 * j + 128], CEN[:],
                                 start=True, stop=True)
            last.then_inc(c["cen"].sem, 1)
            project_ahead(it, ahead, FILL[1:3])
            wait(pe, "xn0", it, 1)
            wait(pe, "ex", it, UN)
            for j in range(TT):
                last = pe.transpose(SB[0][:, 128 * j:128 * j + 128], XN0[:, j, :], ident)
            last.then_inc(c["xnt"].sem, 1)
            project_ahead(it, ahead, FILL[3:4])
            wait(pe, "xn1", it, 1)
            for i, (at, m) in enumerate(BLK):
                if i == 2:
                    wait(pe, "ge", it, 1)
                pe.matmul(GATE[i][0:m, :], W1[par][:, DI + at:DI + at + m], XN1[:], start=True, stop=True)\
                    .then_inc(c["w1"].sem, 1)
                if i == 2:
                    wait(pe, "hid", it, 1)
                pe.matmul(LIN[i][0:m, :], W1[par][:, at:at + m], XN1[:], start=True, stop=True)\
                    .then_inc(c["w1"].sem, 1)
                if i:
                    transpose_qk(it, 0, i - 1)
            transpose_qk(it, 0, 2)
            transpose_qk(it, 0, 3)
            wait(pe, "hid", it, 3)
            for j in range(TT):
                for i, (at, m) in enumerate(BLK):
                    last = pe.matmul(FO[:, 128 * j:128 * j + 128], HID[0:m, i, 128 * j:128 * j + 128],
                                     W2[par][0:m, i, :], start=(i == 0), stop=(i == 2))
            last.then_inc(c["w2"].sem, 1)
            bank_free(pe, it, "x", 0, 0)
            transpose_x(it + 2)

        def next_weights(lp, par):
            weights_loaded(pe, lp, par)

        def body(it, par, ahead):
            for u in range(UN + LV):
                if u < UN:
                    scores(it, u)
                    if 2 <= u % PAIRS < 6 and u // PAIRS + 1 < TT:
                        transpose_qk(it, u // PAIRS + 1, u % PAIRS - 2)
                project_ahead(it, ahead, AHEAD.get(u, []))
                if LT <= u < UN + LT:
                    transpose_p(it, u - LT)
                if u >= LV:
                    values(it, u - LV)
                    if (u - LV) % PAIRS == 2 and u - LV > PAIRS:
                        project_out(it, par, (u - LV) // PAIRS - 1)
            project_out(it, par, TT - 1)
            feed_forward(it, par, ahead)

        pe.wait_ge(s_w[0], 16 * NW)
        transpose_x(0)
        for n, (j, k) in enumerate(ORDER):
            if n:
                wait(pe, "raw", 0, n)
            project(0, 0, j, k)
        for k in range(4):
            transpose_qk(-1, 0, k)
        bank_free(pe, -1, "x", 0, 0)
        transpose_x(1)
        layers(pe, next_weights, body)

    def scalar_program(act):
        credits(act, "xs raw sqr norm ex pte ovc qkc xf sqf std ge")
        act.wait_ge(s_fill, 5)

        def shifted(it, dst, bank, name, src_name, reader):
            wait(act, src_name, it, 1)
            wait_before(act, reader[0], it, reader[1])
            act.activation(dst[0:64, 0:SEQ], bank[0:64, :], ACT.Copy).then_inc(c[name].sem, 1)
            act.activation(dst[64:128, 1:SEQ], bank[64:128, 0:SEQ - 1], ACT.Copy).then_inc(c[name].sem, 1)

        def raw(it, turns):
            for j, k in turns:
                n = TURN[j, k]
                wait(act, "qkv", it, n + 1)
                if k < 4:
                    m = 4 * j + k
                    earlier(act, "ssum", it, m - 1)
                    act.activation(SQR[m % 2][:], bank("project", j, k), ACT.Square).then_inc(c["sqr"].sem, 1)
                    earlier(act, "t2", it, m - 2)
                    act.activation(RAW[m % 3][:], bank("project", j, k), ACT.Copy).then_inc(c["raw"].sem, 1)
                else:
                    wait_before(act, "ov", it, 2 * min(j + 2, TT))
                    act.activation(V[:, j, 512 * (k - 4):512 * (k - 4) + 512], bank("project", j, k), ACT.Copy)\
                        .then_inc(c["raw"].sem, 1)

        def load_table(function):
            act.activation(WARM[:], EPSC[:], function)

        def norms(it):
            wait(act, "ssum", it, 4 * TT)
            wait_before(act, "nmax", it, 1)
            act.activation(SS[:], SS[:], ACT.Sqrt).then_inc(c["norm"].sem, 1)

        def qk_copies(it, j, ks=range(4)):
            for k in ks:
                n = 4 * j + k
                wait(act, "qkt", it, n + 1)
                if k < 2:
                    if k == 0:
                        earlier(act, "sc", it, PAIRS * (j - 1))
                    act.activation(QT[j % 2][:, 4 * k:4 * k + 4, :].rearrange("p a n -> p (a n)"), bank("qk", j, k), ACT.Copy)\
                        .then_inc(c["qkc"].sem, 1)
                else:
                    g = slice(4 * (k - 2), 4 * (k - 2) + 4)
                    if k == 2 and j:
                        wait(act, "kprev", it, 2 * j - 2) if j > 1 else None
                    src = bank("qk", j, k).rearrange("p (a n) -> p a n", a=4)
                    act.activation(KD[j % 2][0:64, g, 0, WIN:KEYS], src[0:64], ACT.Copy)
                    act.activation(KD[j % 2][64:128, g, 1, WIN:KEYS], src[64:128], ACT.Copy)\
                        .then_inc(c["qkc"].sem, 1)

        def exps(it, u):
            j, p = divmod(u, PAIRS)
            wait(act, "nb", it, u + 1)
            earlier(act, "pt", it, u + 1 - NP)
            earlier(act, "rs", it, u + 1 - NP)
            for hh in range(2):
                last = act.activation(PR[u % NP][:, hh, :], SB[u % 2][:, KEYS * hh:KEYS * hh + KEYS], ACT.Exp,
                                      bias=NBI[u % NP][:, hh:hh + 1], scale=RN[:, j, 2 * p + hh:2 * p + hh + 1],
                                      accum_out=SU[u % NP][:, hh:hh + 1])
            last.then_inc(c["ex"].sem, 1)

        def edge(it, u):
            wait(act, "ptm", it, u + 1)
            earlier(act, "ov", it, max(0, (u - 2) // 4)) if False else None
            act.activation(PTE[u % 2][96:128, :, :].rearrange("p a n -> p (a n)"), TRP[0:WIN, 256:256 + 2 * WIN],
                           ACT.Copy).then_inc(c["pte"].sem, 1)

        def out_copy(it, g):
            j, half = divmod(g, 2)
            wait(act, "ov", it, g + 1)
            if half == 0:
                earlier(act, "wo", it, j - 1)
            act.activation(OT[j % 2][:, 4 * half:4 * half + 4, :].rearrange("p a n -> p (a n)"), OV[g % 2],
                           ACT.Copy).then_inc(c["ovc"].sem, 1)

        def next_weights(lp, par):
            weights_loaded(act, lp, par)

        def body(it, par, ahead):
            for u in range(UN + 5):
                if u < UN:
                    exps(it, u)
                    if 2 <= u % PAIRS < 6 and u // PAIRS + 1 < TT:
                        qk_copies(it, u // PAIRS + 1, [u % PAIRS - 2])
                raw(it + 1, AHEAD.get(u, []))
                v = u - 3
                if PAIRS <= v < UN:
                    edge(it, v)
                v = u - 5
                if 0 <= v < UN and v % 4 == 3:
                    out_copy(it, v // 4)
            load_table(ACT.Sqrt)
            shifted(it, XF, TRP, "xf", "ft", ("cen", 1))
            raw(it + 1, FILL[0:1])
            wait(act, "cen", it, 1)
            wait_before(act, "std", it, 1)
            for j in range(TT):
                last = act.activation(SQF[:, j, :], CX[:, 128 * j:128 * j + 128], ACT.Square, accum_out=VAR[:, j:j + 1])
            last.then_inc(c["sqf"].sem, 1)
            wait(act, "sqf", it, 1)
            wait_before(act, "rstd", it, 1)
            act.activation(STD[:], VAR[:], ACT.Sqrt, bias=EPSC[:], scale=1.0 / D).then_inc(c["std"].sem, 1)
            raw(it + 1, FILL[1:2])
            norms(it + 1)
            raw(it + 1, FILL[2:3])
            load_table(ACT.Gelu)
            raw(it + 1, FILL[3:4])
            for i, (at, m) in enumerate(BLK):
                wait(act, "w1", it, 2 * i + 1)
                earlier(act, "hid", it, i - 1)
                act.activation(GE[i % 2][0:m, :], GATE[i][0:m, :], ACT.Gelu, bias=SM[par][0:m, 3 + i:4 + i])\
                    .then_inc(c["ge"].sem, 1)
                if i:
                    qk_copies(it + 1, 0, [i - 1])
            load_table(ACT.Exp)
            qk_copies(it + 1, 0, [2, 3])
            shifted(it + 2, XS, bank("x", 0, 0), "xs", "xt", ("qkv", 6 * TT))

        act.wait_ge(s_w[0], 16 * NW)
        shifted(0, XS, bank("x", 0, 0), "xs", "xt", ("qkv", 6 * TT))
        raw(0, ORDER)
        norms(0)
        qk_copies(0, 0)
        shifted(1, XS, bank("x", 0, 0), "xs", "xt", ("qkv", 6 * TT))
        layers(act, next_weights, body)

    def vector_program(ve):
        credits(ve, "ssum t1 t2 nmax rn rnq mx nb rs ptm res rstd xn0 xn1 hid xo kprev")
        ve.memset(AVG[:], 1.0 / D).then_inc(s_avg, 1)

        def heads(ap):
            return ap.rearrange("p (h d) -> p h d", d=LD)

        def products_start(it, m):
            j, k = divmod(m, 4)
            x = RAW[m % 3]
            wait(ve, "raw", it, TURN[j, k] + 1)
            earlier(ve, "rot", it, m - 1)
            tab = ROPE[:, j, 2 * (k // 2)].unsqueeze(1).broadcast_to([128, 8, LD])
            ve.tensor_tensor(heads(T1[m % 2][:]), heads(x[:]), tab, ALU.mult).then_inc(c["t1"].sem, 1)

        def products_end(it, m):
            j, k = divmod(m, 4)
            x = RAW[m % 3]
            xs = x[:].rearrange("p (h a d) -> p h a d", a=2, d=LD // 2)
            ts_ = T2[m % 2][:].rearrange("p (h a d) -> p h a d", a=2, d=LD // 2)
            for a in range(2):
                tab = ROPE[:, j, 2 * (k // 2) + 1, 32 * a:32 * a + 32].unsqueeze(1).broadcast_to([128, 8, 32])
                last = ve.tensor_tensor(ts_[:, :, a, :], xs[:, :, 1 - a, :], tab, ALU.mult)
            last.then_inc(c["t2"].sem, 1)
            wait(ve, "sqr", it, m + 1)
            if m == 0:
                wait_before(ve, "rnq", it, 1)
            ve.tensor_reduce(SS[:, j, 8 * k:8 * k + 8], heads(SQR[m % 2][:]), AX.X, ALU.add).then_inc(c["ssum"].sem, 1)

        def norms(it):
            wait(ve, "norm", it, 1)
            ve.tensor_scalar(SS[:], SS[:], 1e-12, None, ALU.max).then_inc(c["nmax"].sem, 1)
            wait(ve, "nmax", it, 1)
            wait_before(ve, "ex", it, UN)
            wait_before(ve, "kn", it, TT)
            ve.reciprocal(RN[:], SS[:]).then_inc(c["rn"].sem, 1)
            wait(ve, "rn", it, 1)
            ve.tensor_scalar(RN[:, :, 0:LH], RN[:, :, 0:LH], 8.0, None, ALU.mult).then_inc(c["rnq"].sem, 1)

        def maxima(it, u):
            j, p = divmod(u, PAIRS)
            wait(ve, "sc", it, u + 1)
            earlier(ve, "nb", it, u + 1 - NP)
            ve.tensor_reduce(MX[u % NP][:], SB[u % 2][:, 0:2 * KEYS].rearrange("p (a c) -> p a c", a=2), AX.X,
                             ALU.max).then_inc(c["mx"].sem, 1)
            wait(ve, "mx", it, u + 1)
            earlier(ve, "ex", it, u + 1 - NP)
            ve.scalar_tensor_tensor(NBI[u % NP][:], MX[u % NP][:], -1.0, RN[:, j, 2 * p:2 * p + 2],
                                    ALU.mult, ALU.mult).then_inc(c["nb"].sem, 1)

        def inverse(it, u):
            wait(ve, "ex", it, u + 1)
            earlier(ve, "pn", it, u + 1 - NP)
            ve.reciprocal(RS[u % NP][:], SU[u % NP][:]).then_inc(c["rs"].sem, 1)

        def p_copy(it, u):
            wait(ve, "pt", it, u + 1)
            ve.tensor_copy(PT[u % 2][:].rearrange("p a n -> p (a n)"), TRP[:, 0:256]).then_inc(c["ptm"].sem, 1)

        def key_edge(it, j):
            wait(ve, "qkc", it, 4 * (j + 1))
            earlier(ve, "sc", it, PAIRS * j)
            for hh in range(2):
                rows = slice(64 * hh, 64 * hh + 64)
                ve.tensor_copy(KD[(j + 1) % 2][rows, :, hh, 0:WIN], KD[j % 2][rows, :, hh, KEYS - WIN:KEYS])\
                    .then_inc(c["kprev"].sem, 1)

        def residual(it, j):
            wait(ve, "wo", it, j + 1)
            if j == 0:
                ve.wait_ge(s_xr, (it + 1) * 16)
            ve.tensor_tensor(XR[:, j, :], XR[:, j, :], bank("out", j, 0)[:, 0:D], ALU.add).then_inc(c["res"].sem, 1)

        def feed_forward(it, par):
            wait(ve, "std", it, 1)
            ve.reciprocal(RSTD[:], STD[:]).then_inc(c["rstd"].sem, 1)
            wait(ve, "rstd", it, 1)
            for j in range(TT):
                last = ve.tensor_scalar(XN0[:, j, :], CX[:, 128 * j:128 * j + 128], RSTD[:, j:j + 1], None, ALU.mult)
            last.then_inc(c["xn0"].sem, 1)
            wait(ve, "xnt", it, 1)
            ve.tensor_scalar(XN1[:], SB[0], SM[par][:, 6:7], SM[par][:, 7:8], ALU.mult, ALU.add)\
                .then_inc(c["xn1"].sem, 1)
            norms(it + 1)
            for i, (at, m) in enumerate(BLK):
                wait(ve, "ge", it, i + 1)
                wait(ve, "w1", it, 2 * i + 2)
                ve.scalar_tensor_tensor(HID[0:m, i, :], LIN[i][0:m, :], SM[par][0:m, i:i + 1], GE[i % 2][0:m, :],
                                        ALU.add, ALU.mult).then_inc(c["hid"].sem, 1)
            wait(ve, "w2", it, 1)
            wait(ve, "xb", it, 1)
            ve.wait_ge(s_st, (it + nbatch - 1) * 16)
            ve.tensor_tensor(XO[:].rearrange("p t d -> p (t d)"), FO, XB[:].rearrange("p t d -> p (t d)"),
                             ALU.add).then_inc(c["xo"].sem, 1)

        def next_weights(lp, par):
            weights_loaded(ve, lp, par)
            ve.wait_ge(s_rope.sem, (lp * 2 + (par + 2)) * 4)

        def body(it, par, ahead):
            for u in range(UN + 4):
                if u < UN:
                    maxima(it, u)
                v = u - 1
                if 0 <= v < UN:
                    inverse(it, v)
                if u % PAIRS == 6 and u // PAIRS + 1 < TT:
                    key_edge(it, u // PAIRS)
                v = u - 3
                if 0 <= v < UN:
                    p_copy(it, v)
                for j, k in AHEAD.get(u - 1, []):
                    if k < 4:
                        products_start(it + 1, 4 * j + k)
                for j, k in AHEAD.get(u - 2, []):
                    if k < 4:
                        products_end(it + 1, 4 * j + k)
                v = u - 4
                if v > PAIRS and v % PAIRS == 3:
                    residual(it, v // PAIRS - 1)
            products_start(it + 1, 4 * TT - 1)
            residual(it, TT - 1)
            products_end(it + 1, 4 * TT - 1)
            feed_forward(it, par)

        ve.wait_ge(s_w[0], 16 * NW)
        ve.wait_ge(s_rope.sem, 4)
        for m in range(4 * TT):
            products_start(0, m)
            products_end(0, m)
        norms(0)
        layers(ve, next_weights, body)

    def gpsimd_program(pool):
        credits(pool, "rot kn pn xb")
        for n, (part, value) in enumerate([(EPSC[:], EPS), (XS[64:128, 0:1], 0.0), (XF[64:128, 0:1], 0.0),
                                           (KD[0][:], 0.0), (KD[1][:], 0.0)]):
            if n:
                pool.wait_ge(s_fill, n)
            pool.memset(part, value).then_inc(s_fill, 1)

        def rope_tables(par):
            for i in range(4):
                pool.tensor_tensor(ROPE[:, :, i, :], ROPE0[:, :, i, :],
                                   QS[par][:, i, :].unsqueeze(1).broadcast_to([128, TT, LD]),
                                   ALU.mult).then_inc(s_rope.sem, 1)

        def rotate(it, m):
            j, k = divmod(m, 4)
            wait(pool, "t1", it, m + 1)
            wait(pool, "t2", it, m + 1)
            if k == 0:
                wait_before(pool, "qkt", it, 4 * (j + 1))
            pool.tensor_tensor(ROT[:, j, k, :], T1[m % 2][:], T2[m % 2][:], ALU.add).then_inc(c["rot"].sem, 1)

        def scale_keys(it):
            wait(pool, "rnq", it, 1)
            wait(pool, "rot", it, 4 * TT)
            for j in range(TT):
                k = ROT[:, j, 2:4, :].rearrange("p a n -> p (a n)").rearrange("p (h d) -> p h d", d=LD)
                pool.tensor_tensor(k, k, RN[:, j, LH:2 * LH].unsqueeze(2).broadcast_to([128, LH, LD]),
                                   ALU.mult).then_inc(c["kn"].sem, 1)

        def next_weights(lp, par):
            weights_loaded(pool, lp, par)
            wait(pool, "t2", lp * (2 * nbatch) + (nbatch - 1 + par * nbatch), 4 * TT)
            rope_tables(1 - par)

        def body(it, par, ahead):
            for u in range(UN + 6):
                if u < UN:
                    wait(pool, "rs", it, u + 1)
                    pool.tensor_tensor(PR[u % NP][:], PR[u % NP][:],
                                       RS[u % NP][:].unsqueeze(2).broadcast_to([128, 2, KEYS]),
                                       ALU.mult).then_inc(c["pn"].sem, 1)
                for j, k in AHEAD.get(u - 2, []):
                    if k < 4:
                        rotate(it + 1, 4 * j + k)
            wait(pool, "res", it, TT)
            wait_before(pool, "xo", it, 1)
            pool.tensor_tensor(XB[:], XR[:], B2[par][:].unsqueeze(1).broadcast_to([128, TT, D]),
                               ALU.add).then_inc(c["xb"].sem, 1)
            scale_keys(it + 1)

        pool.wait_ge(s_w[0], 16 * NW)
        pool.wait_ge(s_tab, 48)
        rope_tables(0)
        for m in range(4 * TT):
            rotate(0, m)
        scale_keys(0)
        layers(pool, next_weights, body)

    return dict(sync=sync_program, tensor=tensor_program, scalar=scalar_program, vector=vector_program,
                gpsimd=gpsimd_program)


def last_sum(sb, sem, dr, x_mid, x_work, out):
    G3 = sb("G3", [128, NB, D])
    XM = sb("XM", [128, NB, TT, D])
    XW = sb("XW", [128, NB, TT, D])
    s_in = sem("last_inputs_loaded")
    s_p, s_s, s_o = sem("gated"), sem("summed"), sem("out_stored")

    def batch(x, b):
        return x.rearrange("b (t p) d -> b p t d", p=128)[bass.ds(b, 1)].rearrange("o p t d -> p (o t) d")

    def sync_program(sp):
        sp.dma_start(G3[:], dr["rows"][3:4].broadcast_to([128, NB, D])).then_inc(s_in, 16)
        for b in range(NB):
            sp.dma_start(XM[:, b], batch(x_mid, b)).then_inc(s_in, 16)
            sp.dma_start(XW[:, b], batch(x_work, b)).then_inc(s_in, 16)
        for b in range(NB):
            sp.wait_ge(s_s, b + 1)
            sp.dma_start(batch(out, b), XM[:, b]).then_inc(s_o, 16)
        sp.wait_ge(s_o, 16 * NB)

    def vector_program(ve):
        ve.wait_ge(s_in, 16 * (2 * NB + 1))
        for b in range(NB):
            ve.tensor_tensor(XW[:, b], XW[:, b], G3[:, b:b + 1, :].broadcast_to([128, TT, D]), ALU.mult).then_inc(s_p, 1)
        for b in range(NB):
            ve.wait_ge(s_p, b + 1)
            ve.tensor_tensor(XM[:, b], XM[:, b], XW[:, b], ALU.add).then_inc(s_s, 1)

    return dict(sync=sync_program, vector=vector_program)


def program(nc, dr, x, out):
    for name, shape in (("rows", [ROWS, NB, D]), ("ebrow", [GH, 640])):
        dr[name] = nc.dram_tensor("scratch_" + name, shape, F32, kind="Internal").ap()
    x_mid = nc.dram_tensor("scratch_x_mid", [NB, SEQ, D], F32, kind="Internal").ap()
    x_work = nc.dram_tensor("scratch_x_work", [NB, SEQ, D], F32, kind="Internal").ap()

    with ExitStack() as whole:
        def sem(name):
            return whole.enter_context(nc.semaphore(name))

        def allocator(stack, prefix):
            def sb(name, shape, dt=F32):
                return stack.enter_context(nc.sbuf_tensor(prefix + name, shape, dt))
            return sb

        psum = whole.enter_context(nc.psum_tensor("banks", [128, 8, 512], F32))
        sb = allocator(whole, "w_")
        ident, identb = sb("ident", [128, 128]), sb("identb", [128, 128], BF16)
        s_ident = sem("identity_steps")
        s_alone = sem("nothing_waits_for_this")

        with ExitStack() as stack:
            p = blocks(allocator(stack, "b_"), sem, s_alone, dr, ident[:], identb[:], psum, x, x_mid, x_work, NB)
            block = stack.enter_context(nc.Block())

            @block.sync
            def _(sp):
                p["sync"](sp)

            @block.tensor
            def _(pe):
                pe.wait_ge(s_ident, 3)
                p["tensor"](pe)

            @block.scalar
            def _(act):
                p["scalar"](act)

            @block.vector
            def _(ve):
                p["vector"](ve)

            @block.gpsimd
            def _(pool):
                pool.memset(ident[:], 0.0).then_inc(s_ident, 1)
                pool.wait_ge(s_ident, 1)
                pool.affine_select(out=ident[:], in_=ident[:], compare_op=ALU.not_equal, fill=1.0, base=0,
                                   pattern=[[-1, 128]], channel_multiplier=1).then_inc(s_ident, 1)
                pool.wait_ge(s_ident, 2)
                pool.tensor_copy(identb[:], ident[:]).then_inc(s_ident, 1)
                p["gpsimd"](pool)

        with ExitStack() as stack:
            q = local_layers(allocator(stack, "l_"), sem, s_alone, dr, ident[:], identb[:], psum, x_work, DEPTH, NB)
            block = stack.enter_context(nc.Block())

            @block.sync
            def _(sp):
                q["sync"](sp)

            @block.tensor
            def _(pe):
                q["tensor"](pe)

            @block.scalar
            def _(act):
                q["scalar"](act)

            @block.vector
            def _(ve):
                q["vector"](ve)

            @block.gpsimd
            def _(pool):
                q["gpsimd"](pool)

        with ExitStack() as stack:
            r = last_sum(allocator(stack, "s_"), sem, dr, x_mid, x_work, out)
            block = stack.enter_context(nc.Block())

            @block.sync
            def _(sp):
                r["sync"](sp)

            @block.vector
            def _(ve):
                r["vector"](ve)


def rope_tables():
    half = np.arange(0, LD, 2, dtype=np.float32)
    freq = (1.0 / 10000.0 ** (half / LD)).astype(np.float32)
    t = np.arange(SEQ, dtype=np.float32)
    angle = t[:, None] * freq[None]
    angle = np.concatenate([angle, angle], -1)
    base = ((half + 0.4 * LD) / (1.4 * LD)).astype(np.float32)
    scale = base[None] ** ((t - SEQ // 2) / (WIN // 2))[:, None]
    scale = np.concatenate([scale, scale], -1)
    cos, sin = np.cos(angle), np.sin(angle) * np.where(np.arange(LD) < LD // 2, -1, 1)
    r = np.stack([cos * scale, sin * scale, cos / scale, sin / scale], 1).astype(np.float32)
    return r.reshape(TT, 128, 4, LD).transpose(1, 0, 2, 3)


def bf16_pairs(a):
    bits = (np.ascontiguousarray(a, dtype=np.float32).view(np.uint32) >> 16).astype(np.uint16)
    return np.ascontiguousarray(bits).view(np.float32)


def constants():
    p, col = np.arange(128), np.arange(SEQ)
    head_col = PADD * (p // GD) + p % GD
    c = {"rope": rope_tables(), "cen": np.eye(D, dtype=np.float32) - np.float32(1 / D)}
    i, k = p[:, None], np.arange(KEYS)[None]
    band = (i <= k) & (k <= i + WIN)
    out_of_band = [np.where(ok, 0.0, MASKED) for ok in (band & (k >= WIN), band)]
    c["mask"] = bf16_pairs(np.stack([np.stack([m, m], 1) for m in out_of_band], 1).reshape(128, 4 * KEYS))
    c["causal"] = np.where(col[None] - (SEQ - 128) > i, np.float32(MASKED), np.float32(0))
    c["hmask"] = np.where(p[:, None] // GD == np.arange(GH)[None], np.float32(GD ** -0.5), np.float32(0))
    c["place"] = np.where(head_col[:, None] == col[None], np.float32(1), np.float32(0))
    c["ones_row"] = np.where(col % PADD == GD, np.float32(1), np.float32(0))[None]
    select = np.zeros((128, NG, SELW), np.float32)
    for h in range(GH):
        g, j = divmod(h, HPG)
        select[PADD * j + np.arange(GD), g, GD * h + np.arange(GD)] = 1
        select[PADD * j + GD, g, D + h] = 1
    c["select"] = select
    c["flip"] = np.eye(128, dtype=np.float32)[::-1]
    c["lower"] = np.broadcast_to(np.tril(np.ones((GROUPS, GROUPS), np.float32), -1), (128, GROUPS, GROUPS))
    e = np.arange(3 * E)[:, None, None] % E
    c["selc"] = bf16_pairs((e == 2 * np.arange(EP)[None, :, None] + np.arange(128)[None, None, :] // EI)
                           .astype(np.float32).reshape(3 * E, EP * 128))
    return {n: np.ascontiguousarray(a, dtype=np.float32) for n, a in c.items()}, head_col


def layout(v):
    a, head_col = constants()
    a["wmod0"], a["wmod1"] = v["L0_wmod"], v["L1_wmod"]
    a["c0T"], a["c1T"] = v["L0_c"].T, v["L1_c"].T
    a["relT"] = v["L1_attn_rel_pos_table"][255:511][::-1].T
    a["WVT"] = np.zeros((D, SEQ), np.float32)
    a["WVT"][:, head_col] = v["L1_attn_WV"].T
    a["bV_row"] = a["ones_row"].copy()
    a["bV_row"][0, head_col] = v["L1_attn_bV"]
    a["WQT"], a["WKT"], a["WOT"] = v["L1_attn_WQ"].T, v["L1_attn_WK"].T, v["L1_attn_WO"].T
    a["bQK"] = np.stack([v["L1_attn_bQ"], v["L1_attn_bK"]], 1)
    a["bO"], a["gbias"] = v["L1_attn_bO"][None], v["L0_ffn_gate_bias"][None]
    a["gwT"] = v["L0_ffn_gate_w"].T
    for name, w, shared in (("wgT", "w_gate", "sh_gate"), ("wuT", "w_up", "sh_up")):
        w = v["L0_ffn_" + w].reshape(EP, 2 * EI, D)
        a[name] = np.concatenate([w, v["L0_ffn_" + shared][None]], 0).transpose(2, 0, 1)
    down = v["L0_ffn_w_down"].transpose(0, 2, 1).reshape(EP, 2 * EI, D)
    a["wdT"] = np.concatenate([down, v["L0_ffn_sh_down"].T[None]], 0).transpose(1, 0, 2)
    for name in ("Wqkv", "Wo", "W1", "W2", "b2"):
        a[name] = v["L1_ffn_" + name]
    b1 = v["L1_ffn_b1"]
    a["small"] = np.zeros((DEPTH, 128, 8), np.float32)
    for i, (at, m) in enumerate(BLK):
        a["small"][:, :m, i] = b1[:, at:at + m]
        a["small"][:, :m, 3 + i] = b1[:, DI + at:DI + at + m]
    a["small"][:, :, 6], a["small"][:, :, 7] = v["L1_ffn_ln_g"], v["L1_ffn_ln_b"]
    q, k = v["L1_ffn_q_scale"], v["L1_ffn_k_scale"]
    half = LD // 2
    a["qs"] = np.concatenate([q, q[:, half:], q[:, :half], k, k[:, half:], k[:, :half]], 1)
    return {n: np.ascontiguousarray(x) for n, x in a.items()}


def kernel(**inputs):
    import concourse.bacc as bacc
    from concourse.bass_utils import run_bass_kernel_spmd

    v = {name: np.asarray(a) for name, a in inputs.items()}
    arrays = layout(v)
    arrays["x"] = np.ascontiguousarray(v["L0_attn_x"])
    nc = bacc.Bacc("TRN2", target_bir_lowering=False, num_devices=1)
    dr = {n: nc.dram_tensor("in_" + n, a.shape, F32, kind="ExternalInput").ap() for n, a in arrays.items()}
    out = nc.dram_tensor("out", (NB, SEQ, D), F32, kind="ExternalOutput").ap()
    program(nc, dr, dr["x"], out)
    r = run_bass_kernel_spmd(nc, [{"in_" + n: a for n, a in arrays.items()}], core_ids=[0])
    return r.results[0]["out"]
```

```python
from contextlib import ExitStack

import numpy as np

import concourse.bass as bass
from concourse import mybir

F32 = mybir.dt.float32
BF16 = mybir.dt.bfloat16
ACT = mybir.ActivationFunctionType
ALU = mybir.AluOpType
AX = mybir.AxisListType

NB, SEQ, D = 8, 512, 128
TT = SEQ // 128
DEPTH = 6
LH, LD = 16, 64
INNER = LH * LD
PAIRS = LH // 2
WIN = 32
KEYS = WIN + 128
DI = D * 4 * 2 // 3
BLK = [(0, 128), (128, 128), (256, DI - 256)]
EPS = 1e-5
MASKED = -1e30


class Count:

    def __init__(self, sem, per, credit=0):
        self.sem, self.per, self.credit = sem, per, credit

    def at(self, it, n):
        return it * self.per + (self.credit + n)

    def before(self, it, n):
        return it * self.per + (self.credit + n - self.per)


GH, GD = 16, 8
HPG = 4
NG = GH // HPG
PADD = 32
SELW = D + GH
E, EI = 32, 64
EP = E // 2
GROUPS, TKG, TOPK, SCALE = 8, 4, 8, 2.5
ROWS = 6


def blocks(sb, sem, s_alone, dr, ident, identb, psum, x_in, x_mid, x_work, nbatch):
    WM = [sb(f"WM{i}", [128, 6 * D]) for i in range(2)]
    CT = sb("CT", [128, 2, NB])
    CE = sb("CE", [128, 2, NB])
    SIL = sb("SIL", [128, 2, NB])
    MODT = sb("MODT", [128, 2, 6, NB])
    GATE = sb("GATE", [128, ROWS, NB, D])
    EB = sb("EB", [GH, 640])
    BIAS1 = sb("BIAS1", [128, GH, SEQ])
    BIAS0 = sb("BIAS0", [128, SEQ])
    HM = sb("HM", [128, GH])
    WV = [sb(f"WV{i}", [128, SEQ]) for i in range(2)]
    BV = [sb(f"BV{i}", [128, SEQ]) for i in range(2)]
    SEL = sb("SEL", [128, NG, SELW])
    WQ, WK, WOT = sb("WQ", [128, D]), sb("WK", [128, D]), sb("WOT", [128, D])
    BQK = sb("BQK", [128, 2])
    BO = sb("BO", [128, D])
    GW = sb("GW", [128, E])
    GB = sb("GB", [128, E])
    LOW = sb("LOW", [128, GROUPS, GROUPS])
    WG, WU = sb("WG", [128, EP + 1, 128]), sb("WU", [128, EP + 1, 128])
    WD = sb("WD", [128, EP + 1, D])
    SELC = sb("SELC", [96, EP, 128], BF16)
    EPSC = sb("EPSC1", [128, 1])

    X = sb("X", [128, TT, D])
    XNEXT = sb("XNEXT", [128, TT, D])
    XN0 = WM[0][:, 0:TT * D].rearrange("p (t d) -> p t d", d=D)
    ST0 = sb("ST0", [128, TT, 6])
    MV0 = sb("MV0", [128, TT, 2])
    SD0 = sb("SD0", [128, TT])
    RD0 = sb("RD0", [128, TT])
    ST = sb("ST", [128, TT, 6])
    MV = sb("MV", [128, TT, 2])
    SD = sb("SD", [128, TT])
    RD = sb("RD", [128, TT])
    XN = sb("XN", [128, TT, D])
    HT = sb("HT", [128, SEQ])
    QF = sb("QF", [128, SEQ])
    KF = sb("KF", [128, SEQ])
    NS = 4
    QM = [sb(f"QM{i}", [128, SEQ]) for i in range(2)]
    VP = sb("VP", [128, TT, SEQ])
    SP_ = [sb(f"SPO{i}", [128, SEQ]) for i in range(NS)]
    NBI = [sb(f"NB1{i}", [128, 1]) for i in range(NS)]
    PR = [sb(f"PR1{i}", [128, SEQ]) for i in range(NS)]
    NPT = 5
    PT = [sb(f"PT1{i}", [128, TT, SEQ]) for i in range(NPT)]
    MROW = PT[0][0:NB].rearrange("b t n -> b (t n)")[:, 0:12 * D].rearrange("b (l n) -> b l n", l=2)
    MR = PT[1][0:NB].rearrange("b t n -> b (t n)")[:, 0:ROWS * D].rearrange("b (r d) -> b r d", d=D)
    MS = PT[2][0:NB, 0, :].rearrange("b (r d) -> b r d", d=D)
    MA = PT[3][0:NB, 0, :].rearrange("b (r d) -> b r d", d=D)
    OG = sb("OG", [128, NG, SEQ])
    RC = sb("RC", [128, TT, GH])
    ON = sb("ON", [128, TT, D])
    OT = sb("OT1", [128, SEQ])
    TMP = WM[1][:, 0:TT * D].rearrange("p (t d) -> p t d", d=D)
    TMP2 = sb("TMP2", [128, TT, D])
    FLIP = TMP2[:, 0, :]
    names = ("ex", "ex1", "score", "sc", "mask0", "mask1", "repl", "sel", "w", "comb", "r1", "r2")
    flat = PT[3][:].rearrange("p t n -> p (t n)")
    R = {n: flat[:, TT * E * i:TT * E * (i + 1)].rearrange("p (t e) -> p t e", e=E) for i, n in enumerate(names)}
    names = ("hi1", "lo1", "hi2", "lo2", "t1", "m", "l", "t2", "gs", "rank", "gm")
    flat = PT[2][:].rearrange("p t n -> p (t n)")
    NGR = TT * GROUPS
    Gs = {n: flat[:, NGR * i:NGR * (i + 1)].rearrange("p (t g) -> p t g", g=GROUPS) for i, n in enumerate(names)}
    GT, GQ, GQ2, GQ3 = (flat[:, 512 + 256 * i:768 + 256 * i].rearrange("p (t g k) -> p t g k", g=GROUPS, k=GROUPS)
                        for i in range(4))
    V8 = sb("V8", [128, TT, 8])
    WS = sb("WS", [128, TT])
    WS1 = sb("WS1", [128, TT])
    WS2 = sb("WS2", [128, TT])
    WS3 = sb("WS3", [128, TT])
    CB = sb("CB", [128, TT, 3, E], BF16)
    CBT = sb("CBT", [96, SEQ], BF16)
    SG = [PT[0][:, i, :] for i in range(2)]
    HU = [PT[0][:, 2 + i, :] for i in range(2)]
    HI = [PT[1][:, i, :] for i in range(2)]
    YT = PT[1][:, 2, :]

    P = [psum[:, i, :] for i in range(8)]
    SC = [P[2], P[3], P[4], P[1]]
    TP = [P[5], P[6], P[0]]
    LT = 3
    LC = LT

    s_c = sem("inputs_small")
    s_ce = sem("silu_steps")
    s_mm = sem("mod_products")
    s_ms = sem("mod_steps")
    s_mw = sem("rows_written")
    s_gl = sem("gates_loaded")
    s_eb = sem("bias_row_steps")
    s_bl = sem("bias_loaded")
    s_bt = sem("bias_turned")
    s_bf = sem("bias_kept")
    s_x = sem("x_loaded")
    s_mid = sem("x_mid_stored")
    s_wk = sem("x_work_stored")
    NC = 27

    c = {}

    def add(prefix, items):
        more = 512 if prefix == "a1_" else 0
        for name, per in items:
            c[prefix + name] = Count(sem(prefix + name), per, per + more)

    UN = GH * TT
    for a in ("a0_", "a1_"):
        add(a, [("st", TT), ("mv", TT), ("sd", 1), ("rd", 1), ("xn", TT), ("xt", 1), ("ht", 1), ("qm", GH),
                ("v", TT), ("vp", TT), ("sc", UN), ("mx", UN), ("ex", UN), ("pt", UN), ("ptc", UN - GH), ("ptd", GH), ("pv", NG), ("og", NG),
                ("o", 2), ("rc", 2), ("on", 2), ("g", 1), ("x", 1)])
    add("a1_", [("qk", 2), ("qkc", 2), ("nt", 1), ("ntc", 1), ("wo", 1), ("bo", 1)])
    add("m_", [("st", TT), ("mv", TT), ("sd", 1), ("rd", 1), ("xn", TT), ("xt", 1), ("ht", 1), ("lg", 1), ("ex", 1),
               ("cb", 1), ("ct", 1), ("cbt", 1), ("g", EP + 1), ("u", EP + 1), ("c", EP), ("sg", EP + 1), ("hu", EP),
               ("hi", EP + 1), ("dn", EP + 1), ("y", 1), ("yt", 1), ("z", 1), ("gz", 1), ("x", 1)])
    add("f_", [("st", TT), ("mv", TT), ("sd", 1), ("rd", 1), ("xn", TT), ("gm", 1), ("h", 1)])
    NR = 35
    c["route"] = Count(sem("route_steps"), NR, 0)

    def wait(eng, name, it, n):
        eng.wait_ge(c[name].sem, c[name].at(it, n))

    def before(eng, name, it, n):
        eng.wait_ge(c[name].sem, c[name].before(it, n))

    def done(name):
        return c[name].sem

    def copied(eng, a, it, u):
        h, qt = divmod(u, TT)
        if qt == TT - 1:
            wait(eng, a + "ptd", it, h + 1)
        else:
            wait(eng, a + "ptc", it, (TT - 1) * h + (qt + 1))

    def copy_probabilities(eng, copy, a, it, u):
        h, qt = divmod(u, TT)
        wait(eng, a + "pt", it, u + 1)
        if h >= NPT and qt in (0, TT - 1):
            wait(eng, a + "pv", it, (h - NPT) // HPG + 1)
        copy(PT[h % NPT][:, 0:qt + 1, 128 * qt:128 * qt + 128],
             TP[u % 3][:, 0:128 * (qt + 1)].rearrange("p (k q) -> p k q", q=128))\
            .then_inc(done(a + ("ptd" if qt == TT - 1 else "ptc")), 1)

    def credits(eng, names):
        for n in names.split():
            eng.sem_inc(c[n].sem, c[n].credit)

    xin = x_in.rearrange("b (t p) d -> b p t d", p=128)
    xmid = x_mid.rearrange("b (t p) d -> b p t d", p=128)
    xwork = x_work.rearrange("b (t p) d -> b p t d", p=128)

    def alone(eng):
        eng.sem_inc(s_alone, 1)

    def batch(x, b):
        return x[bass.ds(b, 1)].rearrange("o p t d -> p (o t) d")

    def sync_program(sp):
        small = [(WM[0][:], dr["wmod0"]), (WM[1][:], dr["wmod1"]), (CT[:, 0, :], dr["c0T"]), (CT[:, 1, :], dr["c1T"]),
                 (EB[:, 256:512], dr["relT"]), (BIAS0[:], dr["causal"]), (HM[:], dr["hmask"]),
                 (WV[0][:], dr["place"]), (WV[1][:], dr["WVT"]),
                 (BV[0][:], dr["ones_row"].broadcast_to([128, SEQ])), (BV[1][:], dr["bV_row"].broadcast_to([128, SEQ])),
                 (SEL[:], dr["select"]), (WQ[:], dr["WQT"]), (WK[:], dr["WKT"]), (WOT[:], dr["WOT"]), (BQK[:], dr["bQK"]),
                 (BO[:], dr["bO"].broadcast_to([128, D])), (GW[:], dr["gwT"]), (GB[:], dr["gbias"].broadcast_to([128, E])),
                 (LOW[:], dr["lower"]), (WG[:], dr["wgT"]), (WU[:], dr["wuT"]), (WD[:], dr["wdT"]),
                 (FLIP, dr["flip"]),
                 (SELC[:].rearrange("p a b -> p (a b)").bitcast(F32), dr["selc"])]
        assert len(small) + 2 == NC
        sp.sem_inc(s_wk, 16)
        sp.sem_inc(s_mid, 16)
        sp.dma_start(XNEXT[:], batch(xin, 0)).then_inc(s_x, 16)
        for dst, src in small:
            sp.dma_start(dst, src).then_inc(s_c, 16)
        sp.wait_ge(s_ms, 8)
        sp.dma_start(dr["rows"].rearrange("r b d -> b r d"), MR).then_inc(s_mw, 16)
        sp.wait_ge(s_eb, 3)
        sp.dma_start(dr["ebrow"], EB[:]).then_inc(s_mw, 16)
        sp.wait_ge(s_mw, 32)
        e = dr["ebrow"]
        for i in range(NG):
            src = bass.AP(e.tensor, e.offset + HPG * i * 640, [[1, 128], [640, HPG], [1, SEQ]])
            sp.dma_start(PT[i][:], src).then_inc(s_bl, 16)
        sp.dma_start(GATE[:].rearrange("p r b d -> p (r b d)"),
                     dr["rows"].rearrange("(o r) b d -> o (r b d)", o=1).broadcast_to([128, ROWS * NB * D])).then_inc(s_gl, 16)
        with sp.Fori(0, nbatch) as b:
            wait(sp, "a0_x", b, 1)
            alone(sp)
            sp.dma_start(XNEXT[:], batch(xin, (b + 1) % nbatch)).then_inc(s_x, 16)
            wait(sp, "a1_x", b, 1)
            alone(sp)
            sp.dma_start(batch(xmid, b), X[:]).then_inc(s_mid, 16)
            wait(sp, "f_h", b, 1)
            alone(sp)
            sp.dma_start(batch(xwork, b), TMP2[:]).then_inc(s_wk, 16)
        sp.wait_ge(s_wk, (nbatch + 1) * 16)
        sp.wait_ge(s_mid, (nbatch + 1) * 16)
        sp.wait_ge(s_x, (nbatch + 1) * 16)

    def tensor_program(pe):
        credits(pe, " ".join(f"{a}{n}" for a in ("a0_", "a1_") for n in ("xt", "v", "sc", "pt", "pv", "o")))
        credits(pe, "a1_qk a1_nt a1_wo m_xt m_lg m_ct m_g m_u m_c m_dn m_z")
        pe.wait_ge(s_c, 16 * (NC - 2))
        pe.wait_ge(s_ce, 4)
        for i in range(2):
            for k in range(6):
                pe.matmul(P[0][:, (6 * i + k) * NB:(6 * i + k + 1) * NB], WM[i][:, 128 * k:128 * k + 128], SIL[:, i, :],
                          start=True, stop=True)
            for k in range(2):
                last = pe.matmul(P[1 + 2 * i + k][0:NB, 0:384], SIL[:, i, :], WM[i][:, 384 * k:384 * k + 384],
                                 start=True, stop=True)
        last.then_inc(s_mm, 1)
        pe.wait_ge(s_ms, 3)
        pe.wait_ge(s_bl, 16 * NG)
        for h in range(GH):
            if h >= 2:
                pe.wait_ge(s_bf, h - 1)
            pe.matmul(P[6 + h % 2], FLIP, PT[h // HPG][:, h % HPG, :], start=True, stop=True).then_inc(s_bt, 1)

        def turn(it, a, xn):
            wait(pe, a + "xn", it, TT)
            for t in range(TT):
                last = pe.transpose(P[0][:, 128 * t:128 * t + 128], xn[:, t, :], ident)
            last.then_inc(done(a + "xt"), 1)

        def head(it, a, which):
            turn(it, a, XN if which else XN0)
            wait(pe, a + "ht", it, 1)
            if which:
                for k, w in enumerate((WQ, WK)):
                    pe.matmul(P[2 + k], w[:], HT[:], start=True, stop=True).then_inc(done(a + "qk"), 1)
            for t in range(TT):
                if t >= 2:
                    wait(pe, a + "vp", it, t - 1)
                pe.matmul(P[t % 2], HT[:, 128 * t:128 * t + 128], WV[which][:], start=True, stop=True)\
                    .then_inc(done(a + "v"), 1)
        def attention(it, a, which):
            key = KF if which else HT


            def score(u):
                h, qt = divmod(u, TT)
                n = 128 * (qt + 1)
                if qt == 0:
                    wait(pe, a + "qm", it, h + 1)
                    if h == 0 and which:
                        wait(pe, a + "qkc", it, 2)
                if u >= NS:
                    wait(pe, a + "mx", it, u + 1 - NS)
                elif u == 1 and which == 0:
                    before(pe, "a1_bo", it, 1)
                elif u == 3:
                    wait(pe, a + "vp", it, TT)
                pe.matmul(SC[u % NS][:, 0:n], QM[h % 2][:, 128 * qt:128 * qt + 128], key[:, 0:n],
                          start=True, stop=True).then_inc(done(a + "sc"), 1)

            def transposes(u):
                h, qt = divmod(u, TT)
                wait(pe, a + "ex", it, u + 1)
                if u >= 3:
                    copied(pe, a, it, u - 3)
                for kt in range(qt + 1):
                    last = pe.transpose(TP[u % 3][:, 128 * kt:128 * kt + 128], PR[u % NS][:, 128 * kt:128 * kt + 128], ident)
                last.then_inc(done(a + "pt"), 1)

            def values(g, kt):
                if kt == 0:
                    copied(pe, a, it, (g + 1) * HPG * TT - 2)
                    copied(pe, a, it, (g + 1) * HPG * TT - 1)
                    wait(pe, a + "vp", it, TT)
                    if g:
                        wait(pe, a + "og", it, g)
                for j in range(HPG):
                    h = HPG * g + j
                    last = pe.matmul(P[7][32 * j:32 * j + 32, 128 * kt:SEQ], VP[:, kt, PADD * h:PADD * h + PADD],
                                     PT[h % NPT][:, kt, 128 * kt:SEQ], start=(kt == 0), stop=(kt == TT - 1))
                if kt == TT - 1:
                    last.then_inc(done(a + "pv"), 1)

            for u in range(UN + LT):
                if u < UN:
                    score(u)
                if u >= LT:
                    transposes(u - LT)
                    g, at = divmod(u - LT, HPG * TT)
                    if g and 1 <= at <= TT:
                        values(g - 1, at - 1)
            for kt in range(TT):
                values(NG - 1, kt)
            for t in range(TT):
                if t == 0:
                    wait(pe, a + "og", it, NG)
                for g in range(NG):
                    last = pe.matmul(P[t // 2][:, SELW * (t % 2):SELW * (t % 2) + SELW], OG[:, g, 128 * t:128 * t + 128],
                                     SEL[:, g, :], start=(g == 0), stop=(g == NG - 1))
                if t % 2:
                    last.then_inc(done(a + "o"), 1)
            if which:
                wait(pe, a + "on", it, 2)
                for t in range(TT):
                    last = pe.transpose(P[2][:, 128 * t:128 * t + 128], ON[:, t, :], ident)
                last.then_inc(done(a + "nt"), 1)
                wait(pe, a + "ntc", it, 1)
                for t in range(TT):
                    last = pe.matmul(P[3][:, 128 * t:128 * t + 128], OT[:, 128 * t:128 * t + 128], WOT[:], start=True, stop=True)
                last.then_inc(done(a + "wo"), 1)

        def experts(it):
            turn(it, "m_", XN)
            wait(pe, "m_ht", it, 1)
            for t in range(TT):
                last = pe.matmul(P[1][:, E * t:E * t + E], HT[:, 128 * t:128 * t + 128], GW[:], start=True, stop=True)
            last.then_inc(done("m_lg"), 1)

            def up(e):
                if e >= 2:
                    wait(pe, "m_sg", it, e - 1)
                pe.matmul(P[2 + e % 2], WG[:, e, :], HT[:], start=True, stop=True).then_inc(done("m_g"), 1)
                if e >= 2:
                    wait(pe, "m_hu", it, e - 1)
                pe.matmul(P[4 + e % 2], WU[:, e, :], HT[:], start=True, stop=True).then_inc(done("m_u"), 1)

            def weight(e):
                if e:
                    wait(pe, "m_hi", it, e)
                else:
                    wait(pe, "m_cbt", it, 1)
                pe.matmul(P[6], SELC[:, e, :], CBT[:], start=True, stop=True).then_inc(done("m_c"), 1)

            def down(e):
                wait(pe, "m_hi", it, e + 1)
                pe.matmul(P[7], WD[:, e, :], HI[e % 2], start=(e == 0), stop=(e == EP)).then_inc(done("m_dn"), 1)

            up(0)
            up(1)
            wait(pe, "m_cb", it, 1)
            for t in range(TT):
                last = pe.transpose(P[1].bitcast(BF16)[0:96, 128 * t:128 * t + 128],
                                    CB[:, t].rearrange("p a e -> p (a e)"), identb)
            last.then_inc(done("m_ct"), 1)
            for e in range(EP + 1):
                if e < EP:
                    weight(e)
                if 2 <= e + 1 <= EP:
                    up(e + 1)
                if e >= 1:
                    down(e - 1)
            down(EP)
            wait(pe, "m_yt", it, 1)
            for t in range(TT):
                last = pe.transpose(P[0][:, 128 * t:128 * t + 128], YT[:, 128 * t:128 * t + 128], ident)
            last.then_inc(done("m_z"), 1)

        head(0, "a0_", 0)
        with pe.Fori(0, nbatch) as it:
            attention(it, "a0_", 0)
            experts(it)
            head(it, "a1_", 1)
            attention(it, "a1_", 1)
            head(it + 1, "a0_", 0)

    def scalar_program(act):
        credits(act, " ".join(f"{a}{n}" for a in ("a0_", "a1_") for n in ("ht", "ex", "ptd", "og")))
        credits(act, "a0_sd a1_sd m_sd f_sd a1_qkc a1_ntc m_ht m_ex m_cbt m_sg m_yt")
        act.wait_ge(s_c, 16 * (NC - 2))
        act.wait_ge(s_eb, 1)
        act.activation(CE[:], CT[:], ACT.Exp, scale=-1.0).then_inc(s_ce, 1)
        act.wait_ge(s_ms, 3)

        def deviation(it, a, sd=SD, mv=MV):
            wait(act, a + "mv", it, TT)
            act.activation(sd[:], mv[:, :, 1], ACT.Sqrt, bias=EPSC[:]).then_inc(done(a + "sd"), 1)

        def modulated(it, a, layer, k, b=None):
            wait(act, a + "xt", it, 1)
            b = it if b is None else b
            alone(act)
            act.activation(HT[:], P[0], ACT.Identity, bias=MODT[:, layer, k, bass.ds(b, 1)],
                           scale=MODT[:, layer, k + 1, bass.ds(b, 1)]).then_inc(done(a + "ht"), 1)

        def attention(it, a, which):
            if which:
                deviation(it, a)
                deviation(it + 1, "a0_", SD0, MV0)
                modulated(it, a, which, 0)
                for k, dst in enumerate((QF, KF)):
                    wait(act, a + "qk", it, k + 1)
                    act.activation(dst[:], P[2 + k], ACT.Identity, bias=BQK[:, k:k + 1]).then_inc(done(a + "qkc"), 1)
            def exps(u):
                h, qt = divmod(u, TT)
                n = 128 * (qt + 1)
                wait(act, a + "mx", it, u + 1)
                if u >= NS:
                    wait(act, a + "pt", it, u + 1 - NS)
                act.activation(PR[u % NS][:, 0:n], SP_[u % NS][:, 0:n], ACT.Exp, bias=NBI[u % NS][:], scale=-1.0)\
                    .then_inc(done(a + "ex"), 1)

            for u in range(UN + LC):
                if u >= LC and u % TT == (LC - 1) % TT:
                    copy_probabilities(act, lambda out, x: act.activation(out, x, ACT.Copy), a, it, u - LC)
                if u < UN:
                    exps(u)
                g, at = divmod(u, HPG * TT)
                if u < UN and g and at == LT + TT + 2:
                    out_copy(act, it, a, g - 1)
            out_copy(act, it, a, NG - 1)
            if which:
                wait(act, a + "nt", it, 1)
                act.activation(OT[:], P[2], ACT.Copy).then_inc(done(a + "ntc"), 1)

        def out_copy(act, it, a, g):
            wait(act, a + "pv", it, g + 1)
            act.activation(OG[:, g, :], P[7], ACT.Copy).then_inc(done(a + "og"), 1)

        def experts(it):
            deviation(it, "m_")
            modulated(it, "m_", 0, 3)
            wait(act, "m_lg", it, 1)
            act.activation(R["ex"].rearrange("p t e -> p (t e)"), P[1][:, 0:TT * E], ACT.Exp, scale=-1.0)\
                .then_inc(done("m_ex"), 1)
            for e in range(EP + 1):
                wait(act, "m_g", it, e + 1)
                if e >= 2:
                    wait(act, "m_hu", it, e - 1)
                act.activation(SG[e % 2], P[2 + e % 2], ACT.Silu).then_inc(done("m_sg"), 1)
                if e == 0:
                    wait(act, "m_ct", it, 1)
                    act.activation(CBT[:], P[1].bitcast(BF16)[0:96, 0:SEQ], ACT.Copy).then_inc(done("m_cbt"), 1)
            wait(act, "m_dn", it, EP + 1)
            act.activation(YT, P[7], ACT.Copy).then_inc(done("m_yt"), 1)

        deviation(0, "a0_", SD0, MV0)
        modulated(0, "a0_", 0, 0)
        with act.Fori(0, nbatch) as it:
            attention(it, "a0_", 0)
            experts(it)
            attention(it, "a1_", 1)
            modulated(it + 1, "a0_", 0, 0, (it + 1) % nbatch)
            deviation(it, "f_")

    def vector_program(ve):
        credits(ve, " ".join(f"{a}{n}" for a in ("a0_", "a1_", "m_", "f_") for n in ("st", "mv", "rd", "xn")))
        credits(ve, " ".join(f"{a}{n}" for a in ("a0_", "a1_") for n in ("vp", "mx", "ptc", "rc", "on", "g", "x")))
        credits(ve, "a1_bo m_cb m_hu m_hi m_gz m_x")
        ve.memset(EPSC[:], EPS).then_inc(s_eb, 1)
        ve.wait_ge(s_c, 16 * (NC - 2))
        ve.tensor_copy(EB[:, 0:256], EB[:, 256:257].broadcast_to([GH, 256])).then_inc(s_eb, 1)
        ve.memset(EB[:, 512:640], -1e30).then_inc(s_eb, 1)
        ve.wait_ge(s_ce, 1)
        ve.tensor_scalar(CE[:], CE[:], 1.0, None, ALU.add).then_inc(s_ce, 1)
        ve.wait_ge(s_ce, 2)
        ve.reciprocal(CE[:], CE[:]).then_inc(s_ce, 1)
        ve.wait_ge(s_ce, 3)
        ve.tensor_tensor(SIL[:], CE[:], CT[:], ALU.mult).then_inc(s_ce, 1)
        ve.wait_ge(s_mm, 1)
        ve.tensor_copy(MODT[:].rearrange("p l k b -> p (l k b)"), P[0][:, 0:12 * NB]).then_inc(s_ms, 1)
        ve.wait_ge(s_ms, 1)
        for k in (1, 4):
            ve.tensor_scalar(MODT[:, :, k, :], MODT[:, :, k, :], 1.0, None, ALU.add).then_inc(s_ms, 1)
        for i in range(2):
            for k in range(2):
                last = ve.tensor_copy(MROW[:, i, 384 * k:384 * k + 384], P[1 + 2 * i + k][0:NB, 0:384])
        last.then_inc(s_ms, 1)
        ve.wait_ge(s_ms, 4)
        g = MROW.rearrange("b l (k d) -> b l k d", d=D)[:, :, 2:6:3, :]
        ms, ma, mr = (t.rearrange("b (l k) d -> b l k d", l=2) for t in (MS, MA, MR[:, 0:4, :]))
        ve.tensor_scalar(ms, g, 0.0, 2.0, ALU.is_ge, ALU.mult).then_inc(s_ms, 1)
        ve.scalar_tensor_tensor(ma, g, -1.0, g, ALU.mult, ALU.max).then_inc(s_ms, 1)
        ve.wait_ge(s_ms, 6)
        ve.tensor_scalar(ma, ma, 0.25, None, ALU.max).then_inc(s_ms, 1)
        ve.tensor_scalar(MR[:, 4, :], MROW[:, 1, 4 * D:5 * D], 1.0, None, ALU.add)
        ve.tensor_copy(MR[:, 5, :], MROW[:, 1, 3 * D:4 * D])
        ve.wait_ge(s_ms, 7)
        ve.scalar_tensor_tensor(mr, ms, -1.0, ma, ALU.add, ALU.mult).then_inc(s_ms, 1)

        def norm(it, a, x=X, st=ST, mv=MV, sd=SD, rd=RD, xn=XN):
            for t in range(TT):
                ve.bn_stats(st[:, t, :], x[:, t, :]).then_inc(done(a + "st"), 1)
            for t in range(TT):
                wait(ve, a + "st", it, t + 1)
                alone(ve)
                ve.bn_aggr(mv[:, t, :], st[:, t, :]).then_inc(done(a + "mv"), 1)
            wait(ve, a + "sd", it, 1)
            ve.reciprocal(rd[:], sd[:]).then_inc(done(a + "rd"), 1)
            wait(ve, a + "rd", it, 1)
            for t in range(TT):
                ve.tensor_scalar(xn[:, t, :], x[:, t, :], mv[:, t, 0:1], rd[:, t:t + 1], ALU.subtract, ALU.mult)\
                    .then_inc(done(a + "xn"), 1)

        def norm_next(it):
            ve.wait_ge(s_x, (it + 1) * 16)
            norm(it, "a0_", XNEXT, ST0, MV0, SD0, RD0, XN0)

        def head(it, a, which):
            for t in range(TT):
                wait(ve, a + "v", it, t + 1)
                ve.tensor_tensor(VP[:, t, :], P[t % 2], BV[which][:], ALU.add).then_inc(done(a + "vp"), 1)

        def attention(it, a, which):
            def maxima(u):
                h, qt = divmod(u, TT)
                n = 128 * (qt + 1)
                wait(ve, a + "sc", it, u + 1)
                if u >= NS:
                    wait(ve, a + "ex", it, u + 1 - NS)
                alone(ve)
                bias = BIAS1[:, h, SEQ - n:SEQ] if which else BIAS0[:, SEQ - n:SEQ]
                ve.tensor_tensor_reduce(out=SP_[u % NS][:, 0:n], in0=SC[u % NS][:, 0:n], in1=bias, scale=-1.0,
                                        scalar=3e38, op0=ALU.add, op1=ALU.min, accum_out=NBI[u % NS][:])\
                    .then_inc(done(a + "mx"), 1)

            for u in range(UN + LC):
                if u < UN:
                    maxima(u)
                if u >= LC and u % TT != (LC - 1) % TT:
                    copy_probabilities(ve, ve.tensor_copy, a, it, u - LC)
            for k in range(2):
                wait(ve, a + "o", it, k + 1)
                o = P[k][:, 0:2 * SELW].rearrange("p (t w) -> p t w", w=SELW)
                ve.reciprocal(RC[:, 2 * k:2 * k + 2, :], o[:, :, D:SELW]).then_inc(done(a + "rc"), 1)
                wait(ve, a + "rc", it, k + 1)
                for t in range(2):
                    last = ve.tensor_tensor(ON[:, 2 * k + t, :].rearrange("p (h d) -> p h d", d=GD),
                                            o[:, t, 0:D].rearrange("p (h d) -> p h d", d=GD),
                                            RC[:, 2 * k + t, :].unsqueeze(2).broadcast_to([128, GH, GD]), ALU.mult)
                last.then_inc(done(a + "on"), 1)
            src = ON
            if which:
                wait(ve, a + "wo", it, 1)
                ve.tensor_tensor(TMP[:], P[3].rearrange("p (t d) -> p t d", d=D), BO[:].unsqueeze(1).broadcast_to([128, TT, D]),
                                 ALU.add).then_inc(done(a + "bo"), 1)
                head(it + 1, "a0_", 0)
                wait(ve, a + "bo", it, 1)
                src = TMP
            else:
                wait(ve, a + "on", it, 2)
                ve.wait_ge(s_mid, (it + 1) * 16)
                ve.wait_ge(s_wk, (it + 1) * 16)
            gated(it, a, src[:], 2 * which, x=X if which else XNEXT)

        def gate(r, it):
            return GATE[:, r, bass.ds(it, 1), :].broadcast_to([128, TT, D])

        def gated(it, a, src, r, names=("g", "x"), x=X):
            ve.tensor_tensor(TMP2[:], src, gate(r, it), ALU.mult).then_inc(done(a + names[0]), 1)
            wait(ve, a + names[0], it, 1)
            ve.tensor_tensor(X[:], x[:], TMP2[:], ALU.add).then_inc(done(a + names[1]), 1)

        def route(it):
            n = [0]

            def step(ins):
                n[0] += 1
                ins.then_inc(done("route"), 1)

            def sync():
                wait(ve, "route", it, n[0])

            tt, ts = ve.tensor_tensor, ve.tensor_scalar
            wait(ve, "m_ex", it, 1)
            step(ts(R["ex1"], R["ex"], 1.0, None, ALU.add))
            sync()
            step(ve.reciprocal(R["score"], R["ex1"]))
            sync()
            step(tt(R["sc"], R["score"], GB[:].unsqueeze(1).broadcast_to([128, TT, E]), ALU.add))
            sync()
            v = R["sc"].rearrange("p t (g k) -> p t g k", k=4)
            for dst, i, op in (("hi1", 0, ALU.max), ("lo1", 0, ALU.min), ("hi2", 2, ALU.max), ("lo2", 2, ALU.min)):
                step(tt(Gs[dst], v[:, :, :, i], v[:, :, :, i + 1], op))
            sync()
            for dst, x, y, op in (("t1", "hi1", "hi2", ALU.max), ("m", "hi1", "hi2", ALU.min), ("l", "lo1", "lo2", ALU.max)):
                step(tt(Gs[dst], Gs[x], Gs[y], op))
            sync()
            step(tt(Gs["t2"], Gs["m"], Gs["l"], ALU.max))
            sync()
            step(tt(Gs["gs"], Gs["t1"], Gs["t2"], ALU.add))
            sync()
            other = Gs["gs"].unsqueeze(2).broadcast_to([128, TT, GROUPS, GROUPS])
            own = Gs["gs"].unsqueeze(3).broadcast_to([128, TT, GROUPS, GROUPS])
            step(tt(GT, other, own, ALU.is_gt))
            step(tt(GQ, other, own, ALU.is_equal))
            sync()
            step(tt(GQ2, GQ, LOW[:].unsqueeze(1).broadcast_to([128, TT, GROUPS, GROUPS]), ALU.mult))
            sync()
            step(tt(GQ3, GT, GQ2, ALU.add))
            sync()
            step(ve.tensor_reduce(Gs["rank"], GQ3, AX.X, ALU.add))
            sync()
            step(ts(Gs["gm"], Gs["rank"], TKG - 0.5, None, ALU.is_lt))
            sync()
            step(tt(R["mask0"].rearrange("p t (g k) -> p t g k", k=4), v,
                    Gs["gm"].unsqueeze(3).broadcast_to([128, TT, GROUPS, 4]), ALU.mult))
            sync()
            step(ts(R["mask1"], R["mask0"], 0.0, None, ALU.add))
            sync()
            alone(ve)
            for t in range(TT):
                step(ve.max(V8[:, t, :], R["mask1"][:, t, :]))
            sync()
            alone(ve)
            for t in range(TT):
                step(ve.match_replace(R["repl"][:, t, :], V8[:, t, :], R["mask1"][:, t, :], -1e30))
            sync()
            step(ts(R["sel"], R["repl"], -5e29, None, ALU.is_lt))
            sync()
            step(tt(R["w"], R["sel"], R["score"], ALU.mult))
            sync()
            step(ve.tensor_reduce(WS[:], R["w"], AX.X, ALU.add))
            sync()
            step(ts(WS1[:], WS[:], 1e-20, None, ALU.add))
            sync()
            step(ve.reciprocal(WS2[:], WS1[:]))
            sync()
            step(ts(WS3[:], WS2[:], SCALE, None, ALU.mult))
            sync()
            step(tt(R["comb"], R["w"], WS3[:].unsqueeze(2).broadcast_to([128, TT, E]), ALU.mult))
            sync()
            assert n[0] == NR, n[0]
            ve.tensor_copy(CB[:, :, 0, :], R["comb"]).then_inc(s_split, 1)
            ve.wait_ge(s_split, it * 4 + 1)
            tt(R["r1"], R["comb"], CB[:, :, 0, :], ALU.subtract).then_inc(s_split, 1)
            ve.wait_ge(s_split, it * 4 + 2)
            ve.tensor_copy(CB[:, :, 1, :], R["r1"]).then_inc(s_split, 1)
            ve.wait_ge(s_split, it * 4 + 3)
            tt(R["r2"], R["r1"], CB[:, :, 1, :], ALU.subtract).then_inc(s_split, 1)
            ve.wait_ge(s_split, it * 4 + 4)
            ve.tensor_copy(CB[:, :, 2, :], R["r2"]).then_inc(done("m_cb"), 1)

        def experts(it):
            wait(ve, "a0_x", it, 1)
            norm(it, "m_")
            route(it)
            for e in range(EP + 1):
                wait(ve, "m_sg", it, e + 1)
                wait(ve, "m_u", it, e + 1)
                if e >= 2:
                    wait(ve, "m_dn", it, e - 1)
                dst = HU if e < EP else HI
                ve.tensor_tensor(dst[e % 2], P[4 + e % 2], SG[e % 2], ALU.mult)\
                    .then_inc(done("m_hu" if e < EP else "m_hi"), 1)
                if e < EP:
                    wait(ve, "m_hu", it, e + 1)
                    wait(ve, "m_c", it, e + 1)
                    ve.tensor_tensor(HI[e % 2], P[6], HU[e % 2], ALU.mult).then_inc(done("m_hi"), 1)
            wait(ve, "m_z", it, 1)
            gated(it, "m_", P[0].rearrange("p (t d) -> p t d", d=D), 1, ("gz", "x"))

        for h in range(GH):
            ve.wait_ge(s_bt, h + 1)
            ve.tensor_copy(BIAS1[:, h, :], P[6 + h % 2]).then_inc(s_bf, 1)
        ve.wait_ge(s_gl, 16)
        ve.wait_ge(s_bf, GH)
        norm_next(0)
        head(0, "a0_", 0)
        with ve.Fori(0, nbatch) as it:
            attention(it, "a0_", 0)
            experts(it)
            wait(ve, "m_x", it, 1)
            norm(it, "a1_")
            norm_next(it + 1)
            head(it, "a1_", 1)
            attention(it, "a1_", 1)
            wait(ve, "a1_x", it, 1)
            norm(it, "f_")

    def gpsimd_program(pool):
        credits(pool, "a0_qm a1_qm f_gm f_h")
        pool.wait_ge(s_c, 16 * (NC - 2))

        def masked(it, a, which, heads):
            q = QF if which else HT
            for h in heads:
                if h == 0:
                    wait(pool, a + "qkc" if which else a + "ht", it, 1)
                if h >= 2:
                    wait(pool, a + "sc", it, TT * (h - 1))
                alone(pool)
                pool.tensor_scalar(QM[h % 2][:], q[:], HM[:, h:h + 1], 0.0, ALU.mult, ALU.add).then_inc(done(a + "qm"), 1)

        def gate(r, it):
            return GATE[:, r, bass.ds(it, 1), :].broadcast_to([128, TT, D])

        masked(0, "a0_", 0, range(2))
        pool.wait_ge(s_gl, 16)
        with pool.Fori(0, nbatch) as it:
            masked(it, "a0_", 0, range(2, GH))
            masked(it, "a1_", 1, range(GH))
            masked(it + 1, "a0_", 0, range(2))
            wait(pool, "f_xn", it, TT)
            alone(pool)
            pool.tensor_tensor(TMP[:], XN[:], gate(4, it), ALU.mult).then_inc(done("f_gm"), 1)
            wait(pool, "f_gm", it, 1)
            alone(pool)
            pool.tensor_tensor(TMP2[:], TMP[:], gate(5, it), ALU.add).then_inc(done("f_h"), 1)

    s_split = sem("split_steps")
    return dict(sync=sync_program, tensor=tensor_program, scalar=scalar_program, vector=vector_program, gpsimd=gpsimd_program)


def local_layers(sb, sem, s_alone, dr, ident, identb, psum, x_out, nlayers, nbatch):
    PS = psum
    SHARED = [PS[:, i, :] for i in range(3)]
    TRP = PS[:, 3, :]
    SB = [PS[:, 4, :], PS[:, 5, :]]
    SC = [x[:, 0:2 * KEYS].rearrange("p (a c) -> p a c", a=2) for x in SB]
    OV = [PS[:, 6, :], PS[:, 7, :]]
    CX = OV[0]
    GATE = [SB[1], OV[0], SB[1]]
    LIN = [SB[0], TRP, SB[0]]
    FO = OV[1]

    WQKV = [sb(f"WQKV{i}", [128, 3 * INNER]) for i in range(2)]
    WO = [sb(f"WO{i}", [128, PAIRS, D]) for i in range(2)]
    W1 = [sb(f"W1{i}", [128, 2 * DI]) for i in range(2)]
    W2 = [sb(f"W2{i}", [128, 3, D]) for i in range(2)]
    SM = [sb(f"SM{i}", [128, 8]) for i in range(2)]
    B2 = [sb(f"B2{i}", [128, D]) for i in range(2)]
    QS = [sb(f"QS{i}", [128, 4, LD]) for i in range(2)]
    ROPE0 = sb("ROPE0", [128, TT, 4, LD])
    ROPE = sb("ROPE", [128, TT, 4, LD])
    MASKB = sb("MASKB", [128, 2, 2, KEYS], BF16)
    CEN = sb("CEN", [128, 128])
    EPSC = sb("EPSC", [128, 1])

    XA = sb("XA", [128, TT, D])
    XR = sb("XR", [128, TT, D])
    XO = sb("XO", [128, TT, D])
    XB = sb("XB", [128, TT, D])
    XS = sb("XS", [128, SEQ + 1])
    XF = sb("XF", [128, SEQ + 1])
    RAW = [sb(f"RAW{i}", [128, 512]) for i in range(3)]
    SQR = [sb(f"SQR{i}", [128, 512]) for i in range(2)]
    T1 = [sb(f"T1{i}", [128, 512]) for i in range(2)]
    T2 = [sb(f"T2{i}", [128, 512]) for i in range(2)]
    SS = sb("SS", [128, TT, 2 * LH])
    RN = sb("RN", [128, TT, 2 * LH])
    ROT = sb("ROT", [128, TT, 4, 512])
    V = sb("V", [128, TT, INNER])
    QT = [sb(f"QT{i}", [128, PAIRS, 128]) for i in range(2)]
    KD = [sb(f"KD{i}", [128, PAIRS, 2, KEYS]) for i in range(2)]
    NP = 4
    PR = [sb(f"PR{i}", [128, 2, KEYS]) for i in range(NP)]
    MX = [sb(f"MX{i}", [128, 2]) for i in range(NP)]
    NBI = [sb(f"NBI{i}", [128, 2]) for i in range(NP)]
    SU = [sb(f"SU{i}", [128, 2]) for i in range(NP)]
    RS = [sb(f"RS{i}", [128, 2]) for i in range(NP)]
    PT = [sb(f"PT{i}", [128, 2, 128]) for i in range(2)]
    PTE = [sb(f"PTE{i}", [128, 2, WIN]) for i in range(2)]
    OT = [sb(f"OT{i}", [128, PAIRS, 128]) for i in range(2)]
    SQF = sb("SQF", [128, TT, D])
    VAR = sb("VAR", [128, TT])
    STD = sb("STD", [128, TT])
    RSTD = sb("RSTD", [128, TT])
    XN0 = sb("XN0", [128, TT, D])
    WARM = sb("WARM", [128, 1])
    XN1 = sb("XN1", [128, SEQ])
    GE = [sb(f"GE{i}", [128, SEQ]) for i in range(2)]
    HID = sb("HID", [128, 3, SEQ])

    UN = TT * PAIRS

    LT, LV = 3, 4
    AHEAD = {1: [(0, 0)], 3: [(0, 1)], 5: [(0, 2)], 7: [(0, 3)], 9: [(1, 0)], 11: [(1, 1)], 14: [(1, 2)],
             16: [(1, 3)], 18: [(2, 0)], 21: [(2, 1)], 23: [(2, 2)], 24: [(0, 4)], 25: [(0, 5)], 26: [(2, 3)],
             28: [(3, 0)], 30: [(3, 1)], 32: [(1, 4)], 33: [(3, 2)], 34: [(1, 5)], UN + LV - 1: [(3, 3)]}
    FILL = [(j, k) for j in (TT - 2, TT - 1) for k in (4, 5)]
    ORDER = [a for u in range(UN + LV) for a in AHEAD.get(u, [])] + FILL
    TURN = {a: n for n, a in enumerate(ORDER)}

    TURNS = []
    for u in range(UN + LV):
        j, p = divmod(u, PAIRS)
        if 2 <= p < 6 and j + 1 < TT:
            TURNS.append(("qk", j + 1, p - 2))
        TURNS += [("project", *a) for a in AHEAD.get(u, [])]
        if (u - LV) % PAIRS == 2 and u - LV > PAIRS:
            TURNS.append(("out", (u - LV) // PAIRS - 1, 0))
    TURNS += [("out", TT - 1, 0)] + [("project", *a) for a in FILL] + [("qk", 0, k) for k in range(4)] + [("x", 0, 0)]
    assert len(TURNS) % 3 == 0

    def bank(*turn):
        return SHARED[TURNS.index(turn) % 3]
    s_tab = sem("local_tables")
    s_w = [sem(f"local_weights{i}") for i in range(2)]
    NW = 10
    s_xa = sem("xa_loaded")
    s_xr = sem("xr_loaded")
    s_st = sem("x_stored")
    s_fill = sem("local_buffers_filled")
    c = {}
    for name, per in [
        ("xt", 1), ("xs", 2), ("qkv", 6 * TT), ("raw", 6 * TT), ("sqr", 4 * TT), ("ssum", 4 * TT),
        ("t1", 4 * TT), ("t2", 4 * TT), ("rot", 4 * TT), ("norm", 1), ("nmax", 1), ("rn", 1), ("rnq", 1), ("kn", TT),
        ("qkt", 4 * TT), ("qkc", 4 * TT), ("kprev", 2 * (TT - 1)),
        ("sc", UN), ("mx", UN), ("nb", UN), ("ex", UN), ("rs", UN), ("pn", UN), ("pt", UN),
        ("ptm", UN), ("pte", UN - PAIRS), ("ov", 2 * TT), ("ovc", 2 * TT), ("wo", TT), ("res", TT),
        ("ft", 1), ("xf", 2), ("cen", 1), ("sqf", 1), ("xnt", 1), ("std", 1), ("rstd", 1), ("xn0", TT), ("xn1", 1),
        ("w1", 6), ("ge", 3), ("hid", 3), ("w2", 1), ("xb", 1), ("xo", 1),
    ]:
        c[name] = Count(sem(f"l_{name}"), per, per)
    s_rope = Count(sem("rope_scaled"), 1)

    def alone(eng):
        eng.sem_inc(s_alone, 1)

    def credits(eng, names):
        for n in names.split():
            eng.sem_inc(c[n].sem, c[n].per)

    def wait(eng, name, it, n):
        eng.wait_ge(c[name].sem, c[name].at(it, n))

    def wait_before(eng, name, it, n):
        eng.wait_ge(c[name].sem, c[name].before(it, n))

    def earlier(eng, name, it, n):
        eng.wait_ge(c[name].sem, c[name].at(it, n))

    def bank_free(eng, it, *turn):
        i = TURNS.index(turn) - 3
        what, j, k = TURNS[i]
        of = it if i >= 0 else it - 1
        if what == "qk":
            wait(eng, "qkc", of if j else of + 1, 4 * j + k + 1)
        elif what == "x":
            wait(eng, "xs", of + 2, 2)
        elif what == "project":
            wait(eng, "raw", of + 1, TURN[j, k] + 1)
        else:
            wait(eng, "res", of, j + 1)

    def seen(x, j):
        return x[:, :, (0 if j else WIN):KEYS]

    def layers(eng, next_weights, body):
        with eng.Fori(0, nlayers // 2) as lp:
            for par in range(2):
                alone(eng)
                with eng.Fori(0, nbatch - 1) as b:
                    body(lp * (2 * nbatch) + (b + par * nbatch), par, par)
                next_weights(lp, par)
                alone(eng)
                body(lp * (2 * nbatch) + (nbatch - 1 + par * nbatch), par, 1 - par)

    def weights_loaded(eng, lp, par):
        eng.wait_ge(s_w[1 - par], (lp + (1 + par)) * (16 * NW))

    def batch(x, b):
        return x[bass.ds(b, 1)].rearrange("o p t d -> p (o t) d")

    xout = x_out.rearrange("b (t p) d -> b p t d", p=128)

    def sync_program(sp):
        sp.dma_start(ROPE0[:], dr["rope"]).then_inc(s_tab, 16)
        sp.dma_start(MASKB[:].rearrange("p a b c -> p (a b c)").bitcast(F32), dr["mask"]).then_inc(s_tab, 16)
        sp.dma_start(CEN[:], dr["cen"]).then_inc(s_tab, 16)

        def weights(layer, par):
            for dst, src in [
                (WQKV[par][:], dr["Wqkv"][bass.ds(layer, 1), :, :].rearrange("o k n -> k (o n)")),
                (WO[par][:], dr["Wo"][bass.ds(layer, 1), :, :].rearrange("o (a p) n -> p (o a) n", p=128)),
                (W1[par][:], dr["W1"][bass.ds(layer, 1), :, :].rearrange("o k n -> k (o n)")),
                (W2[par][:, 0:2, :], dr["W2"][bass.ds(layer, 1), 0:256, :].rearrange("o (a p) n -> p (o a) n", p=128)),
                (W2[par][0:DI - 256, 2, :], dr["W2"][bass.ds(layer, 1), 256:DI, :].rearrange("o p n -> p (o n)")),
                (SM[par][:], dr["small"][bass.ds(layer, 1), :, :].rearrange("o k n -> k (o n)")),
                (B2[par][:], dr["b2"][bass.ds(layer, 1), :].broadcast_to([128, D])),
                (QS[par][:, 0, :], dr["qs"][bass.ds(layer, 1), 0:LD].broadcast_to([128, LD])),
                (QS[par][:, 1:3, :].rearrange("p a d -> p (a d)"), dr["qs"][bass.ds(layer, 1), LD:3 * LD].broadcast_to([128, 2 * LD])),
                (QS[par][:, 3, :], dr["qs"][bass.ds(layer, 1), 3 * LD:4 * LD].broadcast_to([128, LD])),
            ]:
                sp.dma_start(dst, src).then_inc(s_w[par], 16)

        sp.sem_inc(s_st, 16 * (nbatch - 1))
        weights(0, 0)
        sp.dma_start(XA[:], batch(xout, 0)).then_inc(s_xa, 16)
        sp.dma_start(XR[:], batch(xout, 0)).then_inc(s_xr, 16)
        for i in range(2):
            wait(sp, "xt", i, 1)
            sp.dma_start(XA[:], batch(xout, i + 1)).then_inc(s_xa, 16)

        def body(it, b):
            wait(sp, "ft", it, 1)
            wait(sp, "xb", it, 1)
            alone(sp)
            sp.dma_start(XR[:], batch(xout, (b + 1) % nbatch)).then_inc(s_xr, 16)
            wait(sp, "xt", it + 2, 1)
            sp.wait_ge(s_st, (it + 3) * 16)
            alone(sp)
            sp.dma_start(XA[:], batch(xout, (b + 3) % nbatch)).then_inc(s_xa, 16)
            wait(sp, "xo", it, 1)
            alone(sp)
            sp.dma_start(batch(xout, b), XO[:]).then_inc(s_st, 16)

        with sp.Fori(0, nlayers // 2) as lp:
            for par in range(2):
                first = lp * (2 * nbatch) + par * nbatch
                for name in ("wo", "xo"):
                    wait_before(sp, name, first, c[name].per)
                    alone(sp)
                weights((lp * 2 + (1 + par)) % nlayers if par else lp * 2 + 1, 1 - par)
                with sp.Fori(0, nbatch - 1) as b:
                    body(lp * (2 * nbatch) + (b + par * nbatch), b)
                body(lp * (2 * nbatch) + (nbatch - 1 + par * nbatch), nbatch - 1)
        sp.wait_ge(s_st, 16 * (nlayers * nbatch + nbatch - 1))
        sp.wait_ge(s_xa, 16 * (nlayers * nbatch + 3))
        sp.wait_ge(s_xr, 16 * (nlayers * nbatch + 1))
        sp.wait_ge(s_w[0], 16 * NW * (nlayers // 2 + 1))

    def tensor_program(pe):
        credits(pe, "xt qkv qkt sc pt ov wo ft cen xnt w1 w2")
        pe.wait_ge(s_fill, 5)
        pe.wait_ge(s_tab, 48)

        def transpose_x(it):
            pe.wait_ge(s_xa, (it + 1) * 16)
            for j in range(TT):
                last = pe.transpose(bank("x", 0, 0)[:, 128 * j:128 * j + 128], XA[:, j, :], ident)
            last.then_inc(c["xt"].sem, 1)

        def project(it, par, j, k):
            n = TURN[j, k]
            if n == 0:
                wait(pe, "xs", it, 2)
            pe.matmul(bank("project", j, k), XS[:, 128 * j:128 * j + 128], WQKV[par][:, 512 * k:512 * k + 512],
                      start=True, stop=True).then_inc(c["qkv"].sem, 1)

        def project_ahead(it, ahead, turns):
            for j, k in turns:
                bank_free(pe, it, "project", j, k)
                project(it + 1, ahead, j, k)

        def transpose_qk(it, j, k):
            turn = it
            if j == 0:
                it = it + 1
            if k == 0:
                wait(pe, "rot", it, 4 * j + 4)
            if k == 2:
                wait(pe, "kn", it, j + 1)
            bank_free(pe, turn, "qk", j, k)
            for i in range(4):
                last = pe.transpose(bank("qk", j, k)[:, 128 * i:128 * i + 128], ROT[:, j, k, 128 * i:128 * i + 128],
                                    ident)
            last.then_inc(c["qkt"].sem, 1)

        def scores(it, u):
            j, p = divmod(u, PAIRS)
            if p == 0:
                wait(pe, "qkc", it, 4 * (j + 1))
                if j:
                    wait(pe, "kprev", it, 2 * j)
            if u >= 2:
                wait(pe, "ex", it, u - 1)
            elif u == 0:
                wait_before(pe, "hid", it, 3)
            else:
                wait_before(pe, "ge", it, 3)
            pe.matmul(seen(SC[u % 2], j), identb, seen(MASKB[:, min(j, 1)], j), start=True, stop=False)
            pe.matmul(seen(SC[u % 2], j), QT[j % 2][:, p, :], seen(KD[j % 2][:, p], j),
                      start=False, stop=True).then_inc(c["sc"].sem, 1)

        def transpose_p(it, u):
            j, p = divmod(u, PAIRS)
            wait(pe, "pn", it, u + 1)
            earlier(pe, "ptm", it, u)
            if u > PAIRS:
                wait(pe, "pte", it, u - PAIRS)
            elif u == 0:
                wait_before(pe, "hid", it, 2)
            for hh in range(2):
                last = pe.transpose(TRP[:, 128 * hh:128 * hh + 128], PR[u % NP][:, hh, WIN:KEYS], ident)
            if j:
                for hh in range(2):
                    last = pe.transpose(TRP[0:WIN, 256 + WIN * hh:256 + WIN * hh + WIN],
                                        PR[u % NP][0:WIN, hh, 0:WIN], ident[0:WIN, 0:WIN])
            last.then_inc(c["pt"].sem, 1)

        def values(it, u):
            j, p = divmod(u, PAIRS)
            wait(pe, "ptm", it, u + 1)
            if j:
                wait(pe, "pte", it, u + 1 - PAIRS)
            if u == 0:
                wait(pe, "raw", it, 6 * TT)
            if p % 4 == 0:
                earlier(pe, "ovc", it, u // 4 - 1)
            if u == 0:
                wait_before(pe, "ge", it, 2)
            if u == 4:
                wait_before(pe, "xo", it, 1)
            for hh in range(2):
                rows = slice(64 * hh, 64 * hh + 64)
                col = 128 * (p % 4)
                h = 2 * p + hh
                last = pe.matmul(OV[u // 4 % 2][rows, col:col + 128], V[:, j, 64 * h:64 * h + 64], PT[u % 2][:, hh, :],
                                 start=True, stop=(j == 0))
                if j:
                    last = pe.matmul(OV[u // 4 % 2][rows, col:col + WIN], V[96:128, j - 1, 64 * h:64 * h + 64],
                                     PTE[u % 2][96:128, hh, :], start=False, stop=True)
            if p % 4 == 3:
                last.then_inc(c["ov"].sem, 1)

        def project_out(it, par, j):
            wait(pe, "ovc", it, 2 * (j + 1))
            bank_free(pe, it, "out", j, 0)
            for p in range(PAIRS):
                last = pe.matmul(bank("out", j, 0)[:, 0:D], OT[j % 2][:, p, :], WO[par][:, p, :],
                                 start=(p == 0), stop=(p == PAIRS - 1))
            last.then_inc(c["wo"].sem, 1)

        def feed_forward(it, par, ahead):
            wait(pe, "res", it, TT)
            wait(pe, "ptm", it, UN)
            wait(pe, "pte", it, UN - PAIRS)
            for j in range(TT):
                last = pe.transpose(TRP[:, 128 * j:128 * j + 128], XR[:, j, :], ident)
            last.then_inc(c["ft"].sem, 1)
            project_ahead(it, ahead, FILL[0:1])
            wait(pe, "xf", it, 2)
            for j in range(TT):
                last = pe.matmul(CX[:, 128 * j:128 * j + 128], XF[:, 128 * j:128 * j + 128], CEN[:],
                                 start=True, stop=True)
            last.then_inc(c["cen"].sem, 1)
            project_ahead(it, ahead, FILL[1:4])
            wait(pe, "ex", it, UN)
            for j in range(TT):
                wait(pe, "xn0", it, j + 1)
                last = pe.transpose(SB[0][:, 128 * j:128 * j + 128], XN0[:, j, :], ident)
            last.then_inc(c["xnt"].sem, 1)
            transpose_qk(it, 0, 0)
            wait(pe, "xn1", it, 1)
            for i, (at, m) in enumerate(BLK):
                if i == 2:
                    wait(pe, "ge", it, 1)
                pe.matmul(GATE[i][0:m, :], W1[par][:, DI + at:DI + at + m], XN1[:], start=True, stop=True)\
                    .then_inc(c["w1"].sem, 1)
                if i == 2:
                    wait(pe, "hid", it, 1)
                pe.matmul(LIN[i][0:m, :], W1[par][:, at:at + m], XN1[:], start=True, stop=True)\
                    .then_inc(c["w1"].sem, 1)
                if i:
                    transpose_qk(it, 0, i)
            transpose_qk(it, 0, 3)
            wait(pe, "hid", it, 3)
            for j in range(TT):
                for i, (at, m) in enumerate(BLK):
                    last = pe.matmul(FO[:, 128 * j:128 * j + 128], HID[0:m, i, 128 * j:128 * j + 128],
                                     W2[par][0:m, i, :], start=(i == 0), stop=(i == 2))
            last.then_inc(c["w2"].sem, 1)
            bank_free(pe, it, "x", 0, 0)
            transpose_x(it + 2)

        def next_weights(lp, par):
            weights_loaded(pe, lp, par)

        def body(it, par, ahead):
            for u in range(UN + LV):
                if u < UN:
                    scores(it, u)
                    if 2 <= u % PAIRS < 6 and u // PAIRS + 1 < TT:
                        transpose_qk(it, u // PAIRS + 1, u % PAIRS - 2)
                if u < UN + LV - 1:
                    project_ahead(it, ahead, AHEAD.get(u, []))
                if LT <= u < UN + LT:
                    transpose_p(it, u - LT)
                if u >= LV:
                    values(it, u - LV)
                    if (u - LV) % PAIRS == 2 and u - LV > PAIRS:
                        project_out(it, par, (u - LV) // PAIRS - 1)
            project_ahead(it, ahead, AHEAD[UN + LV - 1])
            project_out(it, par, TT - 1)
            feed_forward(it, par, ahead)

        pe.wait_ge(s_w[0], 16 * NW)
        transpose_x(0)
        for n, (j, k) in enumerate(ORDER):
            same = [i for i in range(n) if TURNS.index(("project", *ORDER[i])) % 3 == TURNS.index(("project", j, k)) % 3]
            if same:
                wait(pe, "raw", 0, same[-1] + 1)
            project(0, 0, j, k)
        for k in range(4):
            transpose_qk(-1, 0, k)
        bank_free(pe, -1, "x", 0, 0)
        transpose_x(1)
        layers(pe, next_weights, body)

    def scalar_program(act):
        credits(act, "xs raw sqr norm ex ovc qkc xf sqf std ge")
        act.wait_ge(s_fill, 5)

        def shifted(it, dst, bank, name, src_name, reader):
            wait(act, src_name, it, 1)
            wait_before(act, reader[0], it, reader[1])
            act.activation(dst[0:64, 0:SEQ], bank[0:64, :], ACT.Copy).then_inc(c[name].sem, 1)
            act.activation(dst[64:128, 1:SEQ], bank[64:128, 0:SEQ - 1], ACT.Copy).then_inc(c[name].sem, 1)

        def raw(it, turns):
            for j, k in turns:
                n = TURN[j, k]
                wait(act, "qkv", it, n + 1)
                if k < 4:
                    m = 4 * j + k
                    earlier(act, "ssum", it, m - 1)
                    act.activation(SQR[m % 2][:], bank("project", j, k), ACT.Square).then_inc(c["sqr"].sem, 1)
                    earlier(act, "t2", it, m - 2)
                    act.activation(RAW[m % 3][:], bank("project", j, k), ACT.Copy).then_inc(c["raw"].sem, 1)
                else:
                    wait_before(act, "ov", it, 2 * min(j + 2, TT))
                    act.activation(V[:, j, 512 * (k - 4):512 * (k - 4) + 512], bank("project", j, k), ACT.Copy)\
                        .then_inc(c["raw"].sem, 1)

        def load_table(function):
            act.activation(WARM[:], EPSC[:], function)

        def norms(it):
            wait(act, "ssum", it, 4 * TT)
            wait_before(act, "nmax", it, 1)
            act.activation(SS[:], SS[:], ACT.Sqrt).then_inc(c["norm"].sem, 1)

        def qk_copies(it, j, ks=range(4)):
            for k in ks:
                n = 4 * j + k
                wait(act, "qkt", it, n + 1)
                if k < 2:
                    if k == 0:
                        earlier(act, "sc", it, PAIRS * (j - 1))
                    act.activation(QT[j % 2][:, 4 * k:4 * k + 4, :].rearrange("p a n -> p (a n)"), bank("qk", j, k), ACT.Copy)\
                        .then_inc(c["qkc"].sem, 1)
                else:
                    g = slice(4 * (k - 2), 4 * (k - 2) + 4)
                    if k == 2 and j > 1:
                        wait(act, "kprev", it, 2 * j - 2)
                    src = bank("qk", j, k).rearrange("p (a n) -> p a n", a=4)
                    act.activation(KD[j % 2][0:64, g, 0, WIN:KEYS], src[0:64], ACT.Copy)
                    act.activation(KD[j % 2][64:128, g, 1, WIN:KEYS], src[64:128], ACT.Copy)\
                        .then_inc(c["qkc"].sem, 1)

        def exps(it, u):
            j, p = divmod(u, PAIRS)
            wait(act, "nb", it, u + 1)
            earlier(act, "pt", it, u + 1 - NP)
            earlier(act, "rs", it, u + 1 - NP)
            for hh in range(2):
                last = act.activation(seen(PR[u % NP], j)[:, hh, :], seen(SC[u % 2], j)[:, hh, :], ACT.Exp,
                                      bias=NBI[u % NP][:, hh:hh + 1], scale=RN[:, j, 2 * p + hh:2 * p + hh + 1],
                                      accum_out=SU[u % NP][:, hh:hh + 1])
            last.then_inc(c["ex"].sem, 1)

        def out_copy(it, g):
            j, half = divmod(g, 2)
            wait(act, "ov", it, g + 1)
            if half == 0:
                earlier(act, "wo", it, j - 1)
            act.activation(OT[j % 2][:, 4 * half:4 * half + 4, :].rearrange("p a n -> p (a n)"), OV[g % 2],
                           ACT.Copy).then_inc(c["ovc"].sem, 1)

        def next_weights(lp, par):
            weights_loaded(act, lp, par)

        def body(it, par, ahead):
            for u in range(UN + LV + 1):
                if u < UN:
                    exps(it, u)
                    if 2 <= u % PAIRS < 6 and u // PAIRS + 1 < TT:
                        qk_copies(it, u // PAIRS + 1, [u % PAIRS - 2])
                if u < UN + LV - 1:
                    raw(it + 1, AHEAD.get(u, []))
                v = u - LV - 1
                if 0 <= v < UN and v % 4 == 3:
                    out_copy(it, v // 4)
            raw(it + 1, AHEAD[UN + LV - 1])
            load_table(ACT.Sqrt)
            wait(act, "ft", it, 1)
            wait_before(act, "cen", it, 1)
            act.activation(XF[0:64, 0:SEQ], TRP[0:64, :], ACT.Copy).then_inc(c["xf"].sem, 1)
            raw(it + 1, FILL[0:1])
            wait(act, "cen", it, 1)
            wait_before(act, "std", it, 1)
            for j in range(TT):
                last = act.activation(SQF[:, j, :], CX[:, 128 * j:128 * j + 128], ACT.Square, accum_out=VAR[:, j:j + 1])
            last.then_inc(c["sqf"].sem, 1)
            wait(act, "sqf", it, 1)
            wait_before(act, "rstd", it, 1)
            act.activation(STD[:], VAR[:], ACT.Sqrt, bias=EPSC[:], scale=1.0 / D).then_inc(c["std"].sem, 1)
            raw(it + 1, FILL[1:2])
            norms(it + 1)
            raw(it + 1, FILL[2:3])
            raw(it + 1, FILL[3:4])
            load_table(ACT.Gelu)
            qk_copies(it + 1, 0, [0])
            for i, (at, m) in enumerate(BLK):
                wait(act, "w1", it, 2 * i + 1)
                earlier(act, "hid", it, i - 1)
                act.activation(GE[i % 2][0:m, :], GATE[i][0:m, :], ACT.Gelu, bias=SM[par][0:m, 3 + i:4 + i])\
                    .then_inc(c["ge"].sem, 1)
                if i:
                    qk_copies(it + 1, 0, [i])
            load_table(ACT.Exp)
            qk_copies(it + 1, 0, [3])
            shifted(it + 2, XS, bank("x", 0, 0), "xs", "xt", ("qkv", 6 * TT))

        act.wait_ge(s_w[0], 16 * NW)
        shifted(0, XS, bank("x", 0, 0), "xs", "xt", ("qkv", 6 * TT))
        raw(0, ORDER)
        norms(0)
        qk_copies(0, 0)
        shifted(1, XS, bank("x", 0, 0), "xs", "xt", ("qkv", 6 * TT))
        layers(act, next_weights, body)

    def vector_program(ve):
        credits(ve, "ssum t1 t2 nmax rn rnq mx nb rs ptm pte res rstd xn0 xn1 hid xo kprev")

        def heads(ap):
            return ap.rearrange("p (h d) -> p h d", d=LD)

        def products_start(it, m):
            j, k = divmod(m, 4)
            x = RAW[m % 3]
            wait(ve, "raw", it, TURN[j, k] + 1)
            earlier(ve, "rot", it, m - 1)
            tab = ROPE[:, j, 2 * (k // 2)].unsqueeze(1).broadcast_to([128, 8, LD])
            ve.tensor_tensor(heads(T1[m % 2][:]), heads(x[:]), tab, ALU.mult).then_inc(c["t1"].sem, 1)

        def products_end(it, m):
            j, k = divmod(m, 4)
            x = RAW[m % 3]
            xs = x[:].rearrange("p (h a d) -> p h a d", a=2, d=LD // 2)
            ts_ = T2[m % 2][:].rearrange("p (h a d) -> p h a d", a=2, d=LD // 2)
            for a in range(2):
                tab = ROPE[:, j, 2 * (k // 2) + 1, 32 * a:32 * a + 32].unsqueeze(1).broadcast_to([128, 8, 32])
                last = ve.tensor_tensor(ts_[:, :, a, :], xs[:, :, 1 - a, :], tab, ALU.mult)
            last.then_inc(c["t2"].sem, 1)
            wait(ve, "sqr", it, m + 1)
            if m == 0:
                wait_before(ve, "rnq", it, 1)
            ve.tensor_reduce(SS[:, j, 8 * k:8 * k + 8], heads(SQR[m % 2][:]), AX.X, ALU.add).then_inc(c["ssum"].sem, 1)

        def norms(it):
            wait(ve, "norm", it, 1)
            ve.tensor_scalar(SS[:], SS[:], 1e-12, None, ALU.max).then_inc(c["nmax"].sem, 1)
            wait(ve, "nmax", it, 1)
            wait_before(ve, "ex", it, UN)
            wait_before(ve, "kn", it, TT)
            ve.reciprocal(RN[:], SS[:]).then_inc(c["rn"].sem, 1)
            wait(ve, "rn", it, 1)
            ve.tensor_scalar(RN[:, :, 0:LH], RN[:, :, 0:LH], 8.0, None, ALU.mult).then_inc(c["rnq"].sem, 1)

        def maxima(it, u):
            j, p = divmod(u, PAIRS)
            wait(ve, "sc", it, u + 1)
            earlier(ve, "nb", it, u + 1 - NP)
            ve.tensor_reduce(MX[u % NP][:], seen(SC[u % 2], j), AX.X, ALU.max).then_inc(c["mx"].sem, 1)
            wait(ve, "mx", it, u + 1)
            earlier(ve, "ex", it, u + 1 - NP)
            ve.scalar_tensor_tensor(NBI[u % NP][:], MX[u % NP][:], -1.0, RN[:, j, 2 * p:2 * p + 2],
                                    ALU.mult, ALU.mult).then_inc(c["nb"].sem, 1)

        def inverse(it, u):
            wait(ve, "ex", it, u + 1)
            earlier(ve, "pn", it, u + 1 - NP)
            ve.reciprocal(RS[u % NP][:], SU[u % NP][:]).then_inc(c["rs"].sem, 1)

        def p_copy(it, u):
            wait(ve, "pt", it, u + 1)
            ve.tensor_copy(PT[u % 2][:].rearrange("p a n -> p (a n)"), TRP[:, 0:256]).then_inc(c["ptm"].sem, 1)
            if u >= PAIRS:
                ve.tensor_copy(PTE[u % 2][96:128, :, :].rearrange("p a n -> p (a n)"),
                               TRP[0:WIN, 256:256 + 2 * WIN]).then_inc(c["pte"].sem, 1)

        def key_edge(it, j):
            wait(ve, "qkc", it, 4 * (j + 1))
            earlier(ve, "sc", it, PAIRS * j)
            for hh in range(2):
                rows = slice(64 * hh, 64 * hh + 64)
                ve.tensor_copy(KD[(j + 1) % 2][rows, :, hh, 0:WIN], KD[j % 2][rows, :, hh, KEYS - WIN:KEYS])\
                    .then_inc(c["kprev"].sem, 1)

        def residual(it, j):
            wait(ve, "wo", it, j + 1)
            if j == 0:
                ve.wait_ge(s_xr, (it + 1) * 16)
            ve.tensor_tensor(XR[:, j, :], XR[:, j, :], bank("out", j, 0)[:, 0:D], ALU.add).then_inc(c["res"].sem, 1)

        def feed_forward(it, par):
            wait(ve, "std", it, 1)
            ve.reciprocal(RSTD[:], STD[:]).then_inc(c["rstd"].sem, 1)
            wait(ve, "rstd", it, 1)
            for j in range(TT):
                ve.tensor_scalar(XN0[:, j, :], CX[:, 128 * j:128 * j + 128], RSTD[:, j:j + 1], None, ALU.mult)\
                    .then_inc(c["xn0"].sem, 1)
            wait(ve, "xnt", it, 1)
            ve.tensor_scalar(XN1[:], SB[0], SM[par][:, 6:7], SM[par][:, 7:8], ALU.mult, ALU.add)\
                .then_inc(c["xn1"].sem, 1)
            norms(it + 1)
            for i, (at, m) in enumerate(BLK):
                wait(ve, "ge", it, i + 1)
                wait(ve, "w1", it, 2 * i + 2)
                ve.scalar_tensor_tensor(HID[0:m, i, :], LIN[i][0:m, :], SM[par][0:m, i:i + 1], GE[i % 2][0:m, :],
                                        ALU.add, ALU.mult).then_inc(c["hid"].sem, 1)
            wait(ve, "w2", it, 1)
            wait(ve, "xb", it, 1)
            ve.wait_ge(s_st, (it + nbatch - 1) * 16)
            ve.tensor_tensor(XO[:].rearrange("p t d -> p (t d)"), FO, XB[:].rearrange("p t d -> p (t d)"),
                             ALU.add).then_inc(c["xo"].sem, 1)

        def next_weights(lp, par):
            weights_loaded(ve, lp, par)
            ve.wait_ge(s_rope.sem, (lp * 2 + (par + 2)) * 4)

        def body(it, par, ahead):
            for u in range(UN + LV):
                if u < UN:
                    maxima(it, u)
                if u % PAIRS == 6 and u // PAIRS + 1 < TT:
                    key_edge(it, u // PAIRS)
                v = u - LT
                if 0 <= v < UN:
                    p_copy(it, v)
                v = u - 1
                if 0 <= v < UN:
                    inverse(it, v)
                for j, k in AHEAD.get(u - 1, []):
                    if k < 4:
                        products_start(it + 1, 4 * j + k)
                for j, k in AHEAD.get(u - 2, []):
                    if k < 4:
                        products_end(it + 1, 4 * j + k)
                v = u - LV
                if v > PAIRS and v % PAIRS == 3:
                    residual(it, v // PAIRS - 1)
            products_start(it + 1, 4 * TT - 1)
            residual(it, TT - 1)
            wait(ve, "ft", it, 1)
            wait_before(ve, "cen", it, 1)
            ve.tensor_copy(XF[64:128, 1:SEQ], TRP[64:128, 0:SEQ - 1]).then_inc(c["xf"].sem, 1)
            products_end(it + 1, 4 * TT - 1)
            feed_forward(it, par)

        ve.wait_ge(s_w[0], 16 * NW)
        ve.wait_ge(s_rope.sem, 4)
        for m in range(4 * TT):
            products_start(0, m)
            products_end(0, m)
        norms(0)
        layers(ve, next_weights, body)

    def gpsimd_program(pool):
        credits(pool, "rot kn pn xb")
        for n, (part, value) in enumerate([(EPSC[:], EPS), (XS[64:128, 0:1], 0.0), (XF[64:128, 0:1], 0.0),
                                           (KD[0][:], 0.0), (KD[1][:], 0.0)]):
            if n:
                pool.wait_ge(s_fill, n)
            pool.memset(part, value).then_inc(s_fill, 1)

        def scaled_tables(par):
            for i in range(4):
                pool.tensor_tensor(ROPE[:, :, i, :], ROPE0[:, :, i, :],
                                   QS[par][:, i, :].unsqueeze(1).broadcast_to([128, TT, LD]),
                                   ALU.mult).then_inc(s_rope.sem, 1)

        def rotate(it, m):
            j, k = divmod(m, 4)
            wait(pool, "t1", it, m + 1)
            wait(pool, "t2", it, m + 1)
            if k == 0:
                wait_before(pool, "qkt", it, 4 * (j + 1))
            pool.tensor_tensor(ROT[:, j, k, :], T1[m % 2][:], T2[m % 2][:], ALU.add).then_inc(c["rot"].sem, 1)

        def scale_keys(it):
            wait(pool, "rnq", it, 1)
            wait(pool, "rot", it, 4 * TT)
            for j in range(TT):
                k = ROT[:, j, 2:4, :].rearrange("p a n -> p (a n)").rearrange("p (h d) -> p h d", d=LD)
                pool.tensor_tensor(k, k, RN[:, j, LH:2 * LH].unsqueeze(2).broadcast_to([128, LH, LD]),
                                   ALU.mult).then_inc(c["kn"].sem, 1)

        def next_weights(lp, par):
            weights_loaded(pool, lp, par)
            wait(pool, "t2", lp * (2 * nbatch) + (nbatch - 1 + par * nbatch), 4 * TT)
            scaled_tables(1 - par)

        def body(it, par, ahead):
            for u in range(UN + LV + 2):
                if u < UN:
                    wait(pool, "rs", it, u + 1)
                    pr = seen(PR[u % NP], u // PAIRS)
                    pool.tensor_tensor(pr, pr, RS[u % NP][:].unsqueeze(2).broadcast_to(list(pr.shape)), ALU.mult).then_inc(c["pn"].sem, 1)
                for j, k in AHEAD.get(u - 2, []):
                    if k < 4:
                        rotate(it + 1, 4 * j + k)
            wait(pool, "res", it, TT)
            wait_before(pool, "xo", it, 1)
            pool.tensor_tensor(XB[:], XR[:], B2[par][:].unsqueeze(1).broadcast_to([128, TT, D]),
                               ALU.add).then_inc(c["xb"].sem, 1)
            scale_keys(it + 1)

        pool.wait_ge(s_w[0], 16 * NW)
        pool.wait_ge(s_tab, 48)
        scaled_tables(0)
        for m in range(4 * TT):
            rotate(0, m)
        scale_keys(0)
        layers(pool, next_weights, body)

    return dict(sync=sync_program, tensor=tensor_program, scalar=scalar_program, vector=vector_program,
                gpsimd=gpsimd_program)


def last_sum(sb, sem, dr, x_mid, x_work, out):
    G3 = sb("G3", [128, NB, D])
    XM = sb("XM", [128, NB, TT, D])
    XW = sb("XW", [128, NB, TT, D])
    s_in = sem("last_inputs_loaded")
    s_p, s_s, s_o = sem("gated"), sem("summed"), sem("out_stored")

    def batch(x, b):
        return x.rearrange("b (t p) d -> b p t d", p=128)[bass.ds(b, 1)].rearrange("o p t d -> p (o t) d")

    def sync_program(sp):
        sp.dma_start(G3[:], dr["rows"][3:4].broadcast_to([128, NB, D])).then_inc(s_in, 16)
        for b in range(NB):
            sp.dma_start(XM[:, b], batch(x_mid, b)).then_inc(s_in, 16)
            sp.dma_start(XW[:, b], batch(x_work, b)).then_inc(s_in, 16)
        for b in range(NB):
            sp.wait_ge(s_s, b + 1)
            sp.dma_start(batch(out, b), XM[:, b]).then_inc(s_o, 16)
        sp.wait_ge(s_o, 16 * NB)

    def vector_program(ve):
        ve.wait_ge(s_in, 16 * (2 * NB + 1))
        for b in range(NB):
            ve.tensor_tensor(XW[:, b], XW[:, b], G3[:, b:b + 1, :].broadcast_to([128, TT, D]), ALU.mult).then_inc(s_p, 1)
        for b in range(NB):
            ve.wait_ge(s_p, b + 1)
            ve.tensor_tensor(XM[:, b], XM[:, b], XW[:, b], ALU.add).then_inc(s_s, 1)

    return dict(sync=sync_program, vector=vector_program)


def program(nc, dr, x, out):
    for name, shape in (("rows", [ROWS, NB, D]), ("ebrow", [GH, 640])):
        dr[name] = nc.dram_tensor("scratch_" + name, shape, F32, kind="Internal").ap()
    x_mid = nc.dram_tensor("scratch_x_mid", [NB, SEQ, D], F32, kind="Internal").ap()
    x_work = nc.dram_tensor("scratch_x_work", [NB, SEQ, D], F32, kind="Internal").ap()

    with ExitStack() as whole:
        def sem(name):
            return whole.enter_context(nc.semaphore(name))

        def allocator(stack, prefix):
            def sb(name, shape, dt=F32):
                return stack.enter_context(nc.sbuf_tensor(prefix + name, shape, dt))
            return sb

        psum = whole.enter_context(nc.psum_tensor("banks", [128, 8, 512], F32))
        sb = allocator(whole, "w_")
        ident, identb = sb("ident", [128, 128]), sb("identb", [128, 128], BF16)
        s_ident = sem("identity_steps")
        s_alone = sem("nothing_waits_for_this")

        with ExitStack() as stack:
            p = blocks(allocator(stack, "b_"), sem, s_alone, dr, ident[:], identb[:], psum, x, x_mid, x_work, NB)
            block = stack.enter_context(nc.Block())

            @block.sync
            def _(sp):
                p["sync"](sp)

            @block.tensor
            def _(pe):
                pe.wait_ge(s_ident, 3)
                p["tensor"](pe)

            @block.scalar
            def _(act):
                p["scalar"](act)

            @block.vector
            def _(ve):
                p["vector"](ve)

            @block.gpsimd
            def _(pool):
                pool.memset(ident[:], 0.0).then_inc(s_ident, 1)
                pool.wait_ge(s_ident, 1)
                pool.affine_select(out=ident[:], in_=ident[:], compare_op=ALU.not_equal, fill=1.0, base=0,
                                   pattern=[[-1, 128]], channel_multiplier=1).then_inc(s_ident, 1)
                pool.wait_ge(s_ident, 2)
                pool.tensor_copy(identb[:], ident[:]).then_inc(s_ident, 1)
                p["gpsimd"](pool)

        with ExitStack() as stack:
            q = local_layers(allocator(stack, "l_"), sem, s_alone, dr, ident[:], identb[:], psum, x_work, DEPTH, NB)
            block = stack.enter_context(nc.Block())

            @block.sync
            def _(sp):
                q["sync"](sp)

            @block.tensor
            def _(pe):
                q["tensor"](pe)

            @block.scalar
            def _(act):
                q["scalar"](act)

            @block.vector
            def _(ve):
                q["vector"](ve)

            @block.gpsimd
            def _(pool):
                q["gpsimd"](pool)

        with ExitStack() as stack:
            r = last_sum(allocator(stack, "s_"), sem, dr, x_mid, x_work, out)
            block = stack.enter_context(nc.Block())

            @block.sync
            def _(sp):
                r["sync"](sp)

            @block.vector
            def _(ve):
                r["vector"](ve)


def rope_tables():
    half = np.arange(0, LD, 2, dtype=np.float32)
    freq = (1.0 / 10000.0 ** (half / LD)).astype(np.float32)
    t = np.arange(SEQ, dtype=np.float32)
    angle = t[:, None] * freq[None]
    angle = np.concatenate([angle, angle], -1)
    base = ((half + 0.4 * LD) / (1.4 * LD)).astype(np.float32)
    scale = base[None] ** ((t - SEQ // 2) / (WIN // 2))[:, None]
    scale = np.concatenate([scale, scale], -1)
    cos, sin = np.cos(angle), np.sin(angle) * np.where(np.arange(LD) < LD // 2, -1, 1)
    r = np.stack([cos * scale, sin * scale, cos / scale, sin / scale], 1).astype(np.float32)
    return r.reshape(TT, 128, 4, LD).transpose(1, 0, 2, 3)


def bf16_pairs(a):
    bits = (np.ascontiguousarray(a, dtype=np.float32).view(np.uint32) >> 16).astype(np.uint16)
    return np.ascontiguousarray(bits).view(np.float32)


def constants():
    p, col = np.arange(128), np.arange(SEQ)
    head_col = PADD * (p // GD) + p % GD
    c = {"rope": rope_tables(), "cen": np.eye(D, dtype=np.float32) - np.float32(1 / D)}
    i, k = p[:, None], np.arange(KEYS)[None]
    band = (i <= k) & (k <= i + WIN)
    out_of_band = [np.where(ok, 0.0, MASKED) for ok in (band & (k >= WIN), band)]
    c["mask"] = bf16_pairs(np.stack([np.stack([m, m], 1) for m in out_of_band], 1).reshape(128, 4 * KEYS))
    c["causal"] = np.where(col[None] - (SEQ - 128) > i, np.float32(MASKED), np.float32(0))
    c["hmask"] = np.where(p[:, None] // GD == np.arange(GH)[None], np.float32(GD ** -0.5), np.float32(0))
    c["place"] = np.where(head_col[:, None] == col[None], np.float32(1), np.float32(0))
    c["ones_row"] = np.where(col % PADD == GD, np.float32(1), np.float32(0))[None]
    select = np.zeros((128, NG, SELW), np.float32)
    for h in range(GH):
        g, j = divmod(h, HPG)
        select[PADD * j + np.arange(GD), g, GD * h + np.arange(GD)] = 1
        select[PADD * j + GD, g, D + h] = 1
    c["select"] = select
    c["flip"] = np.eye(128, dtype=np.float32)[::-1]
    c["lower"] = np.broadcast_to(np.tril(np.ones((GROUPS, GROUPS), np.float32), -1), (128, GROUPS, GROUPS))
    e = np.arange(3 * E)[:, None, None] % E
    c["selc"] = bf16_pairs((e == 2 * np.arange(EP)[None, :, None] + np.arange(128)[None, None, :] // EI)
                           .astype(np.float32).reshape(3 * E, EP * 128))
    return {n: np.ascontiguousarray(a, dtype=np.float32) for n, a in c.items()}, head_col


def layout(v):
    a, head_col = constants()
    a["wmod0"], a["wmod1"] = v["L0_wmod"], v["L1_wmod"]
    a["c0T"], a["c1T"] = v["L0_c"].T, v["L1_c"].T
    a["relT"] = v["L1_attn_rel_pos_table"][255:511][::-1].T
    a["WVT"] = np.zeros((D, SEQ), np.float32)
    a["WVT"][:, head_col] = v["L1_attn_WV"].T
    a["bV_row"] = a["ones_row"].copy()
    a["bV_row"][0, head_col] = v["L1_attn_bV"]
    a["WQT"], a["WKT"], a["WOT"] = v["L1_attn_WQ"].T, v["L1_attn_WK"].T, v["L1_attn_WO"].T
    a["bQK"] = np.stack([v["L1_attn_bQ"], v["L1_attn_bK"]], 1)
    a["bO"], a["gbias"] = v["L1_attn_bO"][None], v["L0_ffn_gate_bias"][None]
    a["gwT"] = v["L0_ffn_gate_w"].T
    for name, w, shared in (("wgT", "w_gate", "sh_gate"), ("wuT", "w_up", "sh_up")):
        w = v["L0_ffn_" + w].reshape(EP, 2 * EI, D)
        a[name] = np.concatenate([w, v["L0_ffn_" + shared][None]], 0).transpose(2, 0, 1)
    down = v["L0_ffn_w_down"].transpose(0, 2, 1).reshape(EP, 2 * EI, D)
    a["wdT"] = np.concatenate([down, v["L0_ffn_sh_down"].T[None]], 0).transpose(1, 0, 2)
    for name in ("Wqkv", "Wo", "W1", "W2", "b2"):
        a[name] = v["L1_ffn_" + name]
    b1 = v["L1_ffn_b1"]
    a["small"] = np.zeros((DEPTH, 128, 8), np.float32)
    for i, (at, m) in enumerate(BLK):
        a["small"][:, :m, i] = b1[:, at:at + m]
        a["small"][:, :m, 3 + i] = b1[:, DI + at:DI + at + m]
    a["small"][:, :, 6], a["small"][:, :, 7] = v["L1_ffn_ln_g"], v["L1_ffn_ln_b"]
    q, k = v["L1_ffn_q_scale"], v["L1_ffn_k_scale"]
    half = LD // 2
    a["qs"] = np.concatenate([q, q[:, half:], q[:, :half], k, k[:, half:], k[:, :half]], 1)
    return {n: np.ascontiguousarray(x) for n, x in a.items()}


def kernel(**inputs):
    import concourse.bacc as bacc
    from concourse.bass_utils import run_bass_kernel_spmd

    v = {name: np.asarray(a) for name, a in inputs.items()}
    arrays = layout(v)
    arrays["x"] = np.ascontiguousarray(v["L0_attn_x"])
    nc = bacc.Bacc("TRN2", target_bir_lowering=False, num_devices=1)
    dr = {n: nc.dram_tensor("in_" + n, a.shape, F32, kind="ExternalInput").ap() for n, a in arrays.items()}
    out = nc.dram_tensor("out", (NB, SEQ, D), F32, kind="ExternalOutput").ap()
    program(nc, dr, dr["x"], out)
    r = run_bass_kernel_spmd(nc, [{"in_" + n: a for n, a in arrays.items()}], core_ids=[0])
    return r.results[0]["out"]
```
